# Optimizing a Trainium2 kernel written in Bass

```python
import numpy as np
import jax
import jax.numpy as jnp

def _softmax(x, axis=-1):
    return jax.nn.softmax(x, axis=axis)

def _gelu(x):
    return jax.nn.gelu(x, approximate=True)

def _silu(x):
    return jax.nn.silu(x)

def _sigmoid(x):
    return jax.nn.sigmoid(x)

def _layernorm(x, axis=-1, eps=1e-05):
    m = jnp.mean(x, axis=axis, keepdims=True)
    v = jnp.var(x, axis=axis, keepdims=True)
    return (x - m) / jnp.sqrt(v + eps)

def _scatter_add(tgt, idx, src, axis=0):
    return tgt.at[idx].add(src)

def _segment_sum(src, seg, n):
    return jax.ops.segment_sum(src, seg, n)
kernel_name = 'mk_vit_tower_d4_tok_img256_r4_0267ca'

def setup_inputs(seed: int=0):
    np.random.seed(seed)
    _w = jnp.asarray

    def _rec_inputs():
        import jax
        import jax.numpy as jnp
        _rk = jax.random.key(seed)
        x = -7.10856e-05 + 0.999911 * jax.random.normal(jax.random.fold_in(_rk, 1), (2, 64, 128, 64), jnp.float32)
        return x
    x = _rec_inputs()

    def _L0_tok_setup():
        import jax, jax.numpy as jnp
        import numpy as np
        PATCH_LEN = 16
        STRIDE = 8
        PAD = 8
        key = jax.random.key(seed)
        k1, k2 = jax.random.split(key)
        x = jax.random.normal(k1, (32, 64, 128, 64), dtype=jnp.float32)
        in_feat = 64 * (PATCH_LEN // 2 + 1) * 2
        W = jax.random.normal(k2, (64, in_feat), dtype=jnp.float32) * 0.02
        return {'x': x, 'W': W}
    _L0_tok_all = _L0_tok_setup()
    _L0_tok_in = {k: v for k, v in _L0_tok_all.items() if k in ('W',)}
    del _L0_tok_all

    def _L0_attn_setup():
        import jax, jax.numpy as jnp
        import numpy as np
        key = jax.random.key(seed)
        k1, k2 = jax.random.split(key)
        B, N, F = (4, 1024, 64)
        nodes = jax.random.normal(k1, (B, N, F), dtype=jnp.float32)
        limit = np.sqrt(6.0 / (F + F)).astype(np.float32)
        W = jax.random.uniform(k2, (F, F), dtype=jnp.float32, minval=-limit, maxval=limit)
        return {'nodes': nodes, 'W': W}
    _L0_attn_all = _L0_attn_setup()
    _L0_attn_in = {k: v for k, v in _L0_attn_all.items() if k in ('W',)}
    del _L0_attn_all

    def _L0_ffn_setup():
        import jax, jax.numpy as jnp
        import numpy as np
        D_MODEL = 64
        N_EXPERTS = 16
        HIDDEN = 128
        SCALE = 0.02
        key = jax.random.key(seed)
        ks = jax.random.split(key, 5)
        x = jax.random.normal(ks[0], (4, 2048, D_MODEL), dtype=jnp.float32)
        gate_w = jax.random.normal(ks[1], (D_MODEL, N_EXPERTS), dtype=jnp.float32) * SCALE
        gate_b = jnp.zeros((N_EXPERTS,), dtype=jnp.float32)
        w1 = jax.random.normal(ks[2], (N_EXPERTS, D_MODEL, HIDDEN), dtype=jnp.float32) * SCALE
        w2 = jax.random.normal(ks[3], (N_EXPERTS, D_MODEL, HIDDEN), dtype=jnp.float32) * SCALE
        w3 = jax.random.normal(ks[4], (N_EXPERTS, HIDDEN, D_MODEL), dtype=jnp.float32) * SCALE
        return {'x': x, 'gate_w': gate_w, 'gate_b': gate_b, 'w1': w1, 'w2': w2, 'w3': w3}
    _L0_ffn_all = _L0_ffn_setup()
    _L0_ffn_in = {k: v for k, v in _L0_ffn_all.items() if k in ('gate_w', 'gate_b', 'w1', 'w2', 'w3')}
    del _L0_ffn_all

    def _L1_attn_setup():
        import jax, jax.numpy as jnp
        import numpy as np
        SEQ_LEN = 512
        EMBED_DIM = 64
        BATCH = 8
        LN_EPS = 1e-05

        def _layernorm(x, g, b):
            mu = jnp.mean(x, axis=-1, keepdims=True)
            var = jnp.mean(jnp.square(x - mu), axis=-1, keepdims=True)
            return (x - mu) * jax.lax.rsqrt(var + LN_EPS) * g + b
        key = jax.random.key(seed)
        ks = jax.random.split(key, 8)
        C = EMBED_DIM
        x = jax.random.normal(ks[0], (BATCH, SEQ_LEN, C), dtype=jnp.float32)
        qkv_w = jax.random.normal(ks[1], (C, 3 * C), dtype=jnp.float32) * 0.02
        qkv_b = jnp.zeros((3 * C,), dtype=jnp.float32)
        proj_w = jax.random.normal(ks[2], (C, C), dtype=jnp.float32) * 0.02
        proj_b = jnp.zeros((C,), dtype=jnp.float32)
        ln1_g = jnp.ones((C,), dtype=jnp.float32)
        ln1_b = jnp.zeros((C,), dtype=jnp.float32)
        ln2_g = jnp.ones((C,), dtype=jnp.float32)
        ln2_b = jnp.zeros((C,), dtype=jnp.float32)
        bias_table = jax.random.truncated_normal(ks[3], -2.0, 2.0, (2 * SEQ_LEN - 1,), dtype=jnp.float32) * 0.02
        scale = jnp.asarray(1.0 / np.sqrt(C), dtype=jnp.float32)
        return {'x': x, 'ln1_g': ln1_g, 'ln1_b': ln1_b, 'qkv_w': qkv_w, 'qkv_b': qkv_b, 'bias_table': bias_table, 'scale': scale, 'proj_w': proj_w, 'proj_b': proj_b, 'ln2_g': ln2_g, 'ln2_b': ln2_b}
    _L1_attn_all = _L1_attn_setup()
    _L1_attn_in = {k: v for k, v in _L1_attn_all.items() if k in ('ln1_g', 'ln1_b', 'qkv_w', 'qkv_b', 'bias_table', 'scale', 'proj_w', 'proj_b', 'ln2_g', 'ln2_b')}
    del _L1_attn_all

    def _L1_ffn_setup():
        import jax, jax.numpy as jnp
        import numpy as np
        NUM_EXPERTS = 8
        TOP_K = 2
        B, S, D = (8, 2048, 64)

        def _moe(tokens, router_w, w1, b1, w2, b2):
            N = tokens.shape[0]
            E = router_w.shape[0]
            logits = tokens.astype(jnp.float32) @ router_w.astype(jnp.float32).T
            probs = jax.nn.softmax(logits, axis=-1)
            rw, re = jax.lax.top_k(probs, TOP_K)
            if TOP_K > 1:
                rw = rw / jnp.maximum(rw.sum(-1, keepdims=True), 1e-12)
            rw = rw.astype(tokens.dtype)
            combine = jnp.zeros((N, E), tokens.dtype).at[jnp.arange(N)[:, None], re].set(rw)
            out = tokens
            for e in range(E):
                h = jax.nn.gelu(tokens @ w1[e] + b1[e], approximate=False)
                y = h @ w2[e] + b2[e]
                out = out + combine[:, e:e + 1] * y
            return out
        key = jax.random.key(seed)
        ks = jax.random.split(key, 4)
        scale = 1.0 / np.sqrt(D).astype(np.float32)
        return {'input_embeddings': jax.random.normal(ks[0], (B, S, D), jnp.float32), 'router_w': jax.random.normal(ks[1], (NUM_EXPERTS, D), jnp.float32) * scale, 'w1': jax.random.normal(ks[2], (NUM_EXPERTS, D, D), jnp.float32) * scale, 'b1': jnp.zeros((NUM_EXPERTS, D), jnp.float32), 'w2': jax.random.normal(ks[3], (NUM_EXPERTS, D, D), jnp.float32) * scale, 'b2': jnp.zeros((NUM_EXPERTS, D), jnp.float32)}
    _L1_ffn_all = _L1_ffn_setup()
    _L1_ffn_in = {k: v for k, v in _L1_ffn_all.items() if k in ('router_w', 'w1', 'b1', 'w2', 'b2')}
    del _L1_ffn_all

    def _L2_attn_setup():
        import jax, jax.numpy as jnp
        import numpy as np
        EMB, HEADS, DEPTH, SEQ, BATCH = (64, 8, 4, 2048, 4)
        DH = EMB // HEADS
        FF = 4 * EMB
        EPS = 1e-05

        def _layernorm(x, g, b):
            mu = x.mean(-1, keepdims=True)
            var = ((x - mu) ** 2).mean(-1, keepdims=True)
            return (x - mu) * jax.lax.rsqrt(var + EPS) * g + b

        def _linear_attn(x, Wq, Wk, Wv, Wo, bo):
            b, n, dm = x.shape
            split = lambda t: t.reshape(b, n, HEADS, DH).transpose(0, 2, 1, 3)
            scale = DH ** (-0.25)
            q = jax.nn.softmax(split(x @ Wq) * scale, axis=-1)
            k = jax.nn.softmax(split(x @ Wk) * scale, axis=-2)
            v = split(x @ Wv)
            context = jnp.einsum('bhnd,bhne->bhde', k, v)
            out = jnp.einsum('bhnd,bhde->bhne', q, context)
            out = out.transpose(0, 2, 1, 3).reshape(b, n, dm)
            return out @ Wo + bo

        def _forward(x, Wq, Wk, Wv, Wo, bo, ln1_g, ln1_b, W1, b1, W2, b2, ln2_g, ln2_b):
            for i in range(DEPTH):
                h = _layernorm(x, ln1_g[i], ln1_b[i])
                x = x + _linear_attn(h, Wq[i], Wk[i], Wv[i], Wo[i], bo[i])
                h = _layernorm(x, ln2_g[i], ln2_b[i])
                x = x + (jax.nn.gelu(h @ W1[i] + b1[i], approximate=False) @ W2[i] + b2[i])
            return x
        key = jax.random.key(seed)
        ks = jax.random.split(key, 8)
        w = lambda k, shape: jax.random.normal(k, shape, dtype=jnp.float32) * 0.02
        D = DEPTH
        return {'x': jax.random.normal(ks[0], (BATCH, SEQ, EMB), dtype=jnp.float32), 'Wq': w(ks[1], (D, EMB, EMB)), 'Wk': w(ks[2], (D, EMB, EMB)), 'Wv': w(ks[3], (D, EMB, EMB)), 'Wo': w(ks[4], (D, EMB, EMB)), 'bo': jnp.zeros((D, EMB), jnp.float32), 'ln1_g': jnp.ones((D, EMB), jnp.float32), 'ln1_b': jnp.zeros((D, EMB), jnp.float32), 'W1': w(ks[5], (D, EMB, FF)), 'b1': jnp.zeros((D, FF), jnp.float32), 'W2': w(ks[6], (D, FF, EMB)), 'b2': jnp.zeros((D, EMB), jnp.float32), 'ln2_g': jnp.ones((D, EMB), jnp.float32), 'ln2_b': jnp.zeros((D, EMB), jnp.float32)}
    _L2_attn_all = _L2_attn_setup()
    _L2_attn_in = {k: v for k, v in _L2_attn_all.items() if k in ('Wq', 'Wk', 'Wv', 'Wo', 'bo', 'ln1_g', 'ln1_b', 'W1', 'b1', 'W2', 'b2', 'ln2_g', 'ln2_b')}
    del _L2_attn_all

    def _L2_ffn_setup():
        import jax, jax.numpy as jnp
        import numpy as np
        E, D, H, TOP_K = (6, 64, 64, 2)
        ROUTER_H = D // 2
        key = jax.random.key(seed)
        ks = jax.random.split(key, 12)
        s = 1.0 / np.sqrt(D)
        sh = 1.0 / np.sqrt(H)
        sr = 1.0 / np.sqrt(ROUTER_H)
        return {'features': jax.random.normal(ks[0], (8, 1024, D), dtype=jnp.float32), 'router_w1': jax.random.uniform(ks[1], (D, ROUTER_H), jnp.float32, -s, s), 'router_b1': jnp.zeros((ROUTER_H,), jnp.float32), 'router_w2': jax.random.uniform(ks[2], (ROUTER_H, E), jnp.float32, -sr, sr), 'router_b2': jnp.zeros((E,), jnp.float32), 'expert_w1': jax.random.uniform(ks[3], (E, D, H), jnp.float32, -s, s), 'expert_b1': jnp.zeros((E, H), jnp.float32), 'expert_w2': jax.random.uniform(ks[4], (E, H, H), jnp.float32, -sh, sh), 'expert_b2': jnp.zeros((E, H), jnp.float32), 'expert_w3': jax.random.uniform(ks[5], (E, H, D), jnp.float32, -sh, sh), 'expert_b3': jnp.zeros((E, D), jnp.float32)}
    _L2_ffn_all = _L2_ffn_setup()
    _L2_ffn_in = {k: v for k, v in _L2_ffn_all.items() if k in ('router_w1', 'router_b1', 'router_w2', 'router_b2', 'expert_w1', 'expert_b1', 'expert_w2', 'expert_b2', 'expert_w3', 'expert_b3')}
    del _L2_ffn_all

    def _L3_attn_setup():
        import jax, jax.numpy as jnp
        import numpy as np
        IN_C = 64
        HID_C = 64
        HEADS = 8
        SCALE = 1.0 / np.sqrt(HID_C / HEADS).astype(np.float32)
        key = jax.random.key(seed)
        k_v, k_q, k_k, k_w, k_o, k_b = jax.random.split(key, 6)
        B, S = (4, 512)
        lim_in = 1.0 / np.sqrt(IN_C)
        lim_out = 1.0 / np.sqrt(IN_C * HEADS)
        v = jax.random.normal(k_v, (B, S, IN_C), dtype=jnp.float32)
        WQ = jax.random.uniform(k_q, (IN_C, IN_C * HEADS), jnp.float32, -lim_in, lim_in)
        WK = jax.random.uniform(k_k, (IN_C, IN_C * HEADS), jnp.float32, -lim_in, lim_in)
        WV = jax.random.uniform(k_w, (IN_C, IN_C * HEADS), jnp.float32, -lim_in, lim_in)
        Wout = jax.random.uniform(k_o, (IN_C * HEADS, HID_C), jnp.float32, -lim_out, lim_out)
        bout = jax.random.uniform(k_b, (HID_C,), jnp.float32, -lim_out, lim_out)
        return {'v': v, 'WQ': WQ, 'WK': WK, 'WV': WV, 'Wout': Wout, 'bout': bout}
    _L3_attn_all = _L3_attn_setup()
    _L3_attn_in = {k: v for k, v in _L3_attn_all.items() if k in ('WQ', 'WK', 'WV', 'Wout', 'bout')}
    del _L3_attn_all

    def _L3_ffn_setup():
        import jax, jax.numpy as jnp
        import numpy as np
        B, A = (1024, 8)
        IN, OUT = (64, 64)
        SH1, SH2 = (64, 128)
        EH1, EH2 = (128, 64)
        E, TOPK = (4, 2)

        def _shared_mlp(x, W1, b1, W2, b2, W3, b3):
            h = jax.nn.relu(x @ W1 + b1)
            h = jax.nn.relu(h @ W2 + b2)
            return h @ W3 + b3

        def _experts_mlp(x, eW1, eb1, eW2, eb2, eW3, eb3):
            h = jax.nn.relu(jnp.einsum('baf,efh->ebah', x, eW1) + eb1[:, None, None, :])
            h = jax.nn.relu(jnp.einsum('ebah,ehg->ebag', h, eW2) + eb2[:, None, None, :])
            o = jnp.einsum('ebag,ego->ebao', h, eW3) + eb3[:, None, None, :]
            return jnp.moveaxis(o, 0, -1)
        key = jax.random.key(seed)
        ks = jax.random.split(key, 16)
        s = 0.05
        return {'x': jax.random.normal(ks[0], (B, A, IN), jnp.float32), 'sW1': jax.random.normal(ks[1], (IN, SH1), jnp.float32) * s, 'sb1': jnp.zeros((SH1,), jnp.float32), 'sW2': jax.random.normal(ks[2], (SH1, SH2), jnp.float32) * s, 'sb2': jnp.zeros((SH2,), jnp.float32), 'sW3': jax.random.normal(ks[3], (SH2, OUT), jnp.float32) * s, 'sb3': jnp.zeros((OUT,), jnp.float32), 'eW1': jax.random.normal(ks[4], (E, IN, EH1), jnp.float32) * s, 'eb1': jnp.zeros((E, EH1), jnp.float32), 'eW2': jax.random.normal(ks[5], (E, EH1, EH2), jnp.float32) * s, 'eb2': jnp.zeros((E, EH2), jnp.float32), 'eW3': jax.random.normal(ks[6], (E, EH2, OUT), jnp.float32) * s, 'eb3': jnp.zeros((E, OUT), jnp.float32), 'gW': jax.random.normal(ks[7], (IN, E), jnp.float32) * s, 'gb': jnp.zeros((E,), jnp.float32)}
    _L3_ffn_all = _L3_ffn_setup()
    _L3_ffn_in = {k: v for k, v in _L3_ffn_all.items() if k in ('sW1', 'sb1', 'sW2', 'sb2', 'sW3', 'sb3', 'eW1', 'eb1', 'eW2', 'eb2', 'eW3', 'eb3', 'gW', 'gb')}
    del _L3_ffn_all
    return {'x': x, 'L0_tok_W': _L0_tok_in['W'], 'L0_attn_W': _L0_attn_in['W'], 'L0_ffn_gate_w': _L0_ffn_in['gate_w'], 'L0_ffn_gate_b': _L0_ffn_in['gate_b'], 'L0_ffn_w1': _L0_ffn_in['w1'], 'L0_ffn_w2': _L0_ffn_in['w2'], 'L0_ffn_w3': _L0_ffn_in['w3'], 'L1_attn_ln1_g': _L1_attn_in['ln1_g'], 'L1_attn_ln1_b': _L1_attn_in['ln1_b'], 'L1_attn_qkv_w': _L1_attn_in['qkv_w'], 'L1_attn_qkv_b': _L1_attn_in['qkv_b'], 'L1_attn_bias_table': _L1_attn_in['bias_table'], 'L1_attn_scale': _L1_attn_in['scale'], 'L1_attn_proj_w': _L1_attn_in['proj_w'], 'L1_attn_proj_b': _L1_attn_in['proj_b'], 'L1_attn_ln2_g': _L1_attn_in['ln2_g'], 'L1_attn_ln2_b': _L1_attn_in['ln2_b'], 'L1_ffn_router_w': _L1_ffn_in['router_w'], 'L1_ffn_w1': _L1_ffn_in['w1'], 'L1_ffn_b1': _L1_ffn_in['b1'], 'L1_ffn_w2': _L1_ffn_in['w2'], 'L1_ffn_b2': _L1_ffn_in['b2'], 'L2_attn_Wq': _L2_attn_in['Wq'], 'L2_attn_Wk': _L2_attn_in['Wk'], 'L2_attn_Wv': _L2_attn_in['Wv'], 'L2_attn_Wo': _L2_attn_in['Wo'], 'L2_attn_bo': _L2_attn_in['bo'], 'L2_attn_ln1_g': _L2_attn_in['ln1_g'], 'L2_attn_ln1_b': _L2_attn_in['ln1_b'], 'L2_attn_W1': _L2_attn_in['W1'], 'L2_attn_b1': _L2_attn_in['b1'], 'L2_attn_W2': _L2_attn_in['W2'], 'L2_attn_b2': _L2_attn_in['b2'], 'L2_attn_ln2_g': _L2_attn_in['ln2_g'], 'L2_attn_ln2_b': _L2_attn_in['ln2_b'], 'L2_ffn_router_w1': _L2_ffn_in['router_w1'], 'L2_ffn_router_b1': _L2_ffn_in['router_b1'], 'L2_ffn_router_w2': _L2_ffn_in['router_w2'], 'L2_ffn_router_b2': _L2_ffn_in['router_b2'], 'L2_ffn_expert_w1': _L2_ffn_in['expert_w1'], 'L2_ffn_expert_b1': _L2_ffn_in['expert_b1'], 'L2_ffn_expert_w2': _L2_ffn_in['expert_w2'], 'L2_ffn_expert_b2': _L2_ffn_in['expert_b2'], 'L2_ffn_expert_w3': _L2_ffn_in['expert_w3'], 'L2_ffn_expert_b3': _L2_ffn_in['expert_b3'], 'L3_attn_WQ': _L3_attn_in['WQ'], 'L3_attn_WK': _L3_attn_in['WK'], 'L3_attn_WV': _L3_attn_in['WV'], 'L3_attn_Wout': _L3_attn_in['Wout'], 'L3_attn_bout': _L3_attn_in['bout'], 'L3_ffn_sW1': _L3_ffn_in['sW1'], 'L3_ffn_sb1': _L3_ffn_in['sb1'], 'L3_ffn_sW2': _L3_ffn_in['sW2'], 'L3_ffn_sb2': _L3_ffn_in['sb2'], 'L3_ffn_sW3': _L3_ffn_in['sW3'], 'L3_ffn_sb3': _L3_ffn_in['sb3'], 'L3_ffn_eW1': _L3_ffn_in['eW1'], 'L3_ffn_eb1': _L3_ffn_in['eb1'], 'L3_ffn_eW2': _L3_ffn_in['eW2'], 'L3_ffn_eb2': _L3_ffn_in['eb2'], 'L3_ffn_eW3': _L3_ffn_in['eW3'], 'L3_ffn_eb3': _L3_ffn_in['eb3'], 'L3_ffn_gW': _L3_ffn_in['gW'], 'L3_ffn_gb': _L3_ffn_in['gb']}

def reference(x, L0_tok_W, L0_attn_W, L0_ffn_gate_w, L0_ffn_gate_b, L0_ffn_w1, L0_ffn_w2, L0_ffn_w3, L1_attn_ln1_g, L1_attn_ln1_b, L1_attn_qkv_w, L1_attn_qkv_b, L1_attn_bias_table, L1_attn_scale, L1_attn_proj_w, L1_attn_proj_b, L1_attn_ln2_g, L1_attn_ln2_b, L1_ffn_router_w, L1_ffn_w1, L1_ffn_b1, L1_ffn_w2, L1_ffn_b2, L2_attn_Wq, L2_attn_Wk, L2_attn_Wv, L2_attn_Wo, L2_attn_bo, L2_attn_ln1_g, L2_attn_ln1_b, L2_attn_W1, L2_attn_b1, L2_attn_W2, L2_attn_b2, L2_attn_ln2_g, L2_attn_ln2_b, L2_ffn_router_w1, L2_ffn_router_b1, L2_ffn_router_w2, L2_ffn_router_b2, L2_ffn_expert_w1, L2_ffn_expert_b1, L2_ffn_expert_w2, L2_ffn_expert_b2, L2_ffn_expert_w3, L2_ffn_expert_b3, L3_attn_WQ, L3_attn_WK, L3_attn_WV, L3_attn_Wout, L3_attn_bout, L3_ffn_sW1, L3_ffn_sb1, L3_ffn_sW2, L3_ffn_sb2, L3_ffn_sW3, L3_ffn_sb3, L3_ffn_eW1, L3_ffn_eb1, L3_ffn_eW2, L3_ffn_eb2, L3_ffn_eW3, L3_ffn_eb3, L3_ffn_gW, L3_ffn_gb):
    import jax
    import jax.numpy as jnp

    def _L0_tok_ref(x, W):
        import jax, jax.numpy as jnp
        import numpy as np
        PATCH_LEN = 16
        STRIDE = 8
        PAD = 8
        B, C, T, V = x.shape
        xp = jnp.pad(x, ((0, 0), (0, 0), (0, PAD), (0, 0)), mode='edge')
        Tp = T + PAD
        N = (Tp - PATCH_LEN) // STRIDE + 1
        idx = jnp.arange(N)[:, None] * STRIDE + jnp.arange(PATCH_LEN)[None, :]
        patches = xp[:, :, idx, :]
        patches = jnp.transpose(patches, (0, 4, 2, 3, 1))
        xf = jnp.fft.rfft(patches, axis=-2, norm='ortho')
        F = xf.shape[-2]
        x_real = xf.real.reshape(B, V, N, F * C)
        x_imag = xf.imag.reshape(B, V, N, F * C)
        x_emb = jnp.concatenate([x_real, x_imag], axis=-1)
        x_emb = x_emb @ W.T
        return x_emb.reshape(B, V * N, -1)

    def _L0_attn_ref(nodes, W):
        import jax, jax.numpy as jnp
        import numpy as np
        F = nodes.shape[-1]
        norm_const = 1.0 / jnp.sqrt(jnp.asarray(F, dtype=nodes.dtype))
        x = jnp.einsum('bnf,fg->bng', nodes, W)
        prods = jnp.einsum('bnf,bmf->bnm', x, nodes)
        att_scores = jax.nn.softmax(prods * norm_const, axis=-1)
        messgs = jnp.einsum('bnm,bmf->bnf', att_scores, nodes)
        return messgs

    def _L0_ffn_ref(x, gate_w, gate_b, w1, w2, w3):
        import jax, jax.numpy as jnp
        import numpy as np
        D_MODEL = 64
        N_EXPERTS = 16
        HIDDEN = 128
        SCALE = 0.02
        n_experts = w1.shape[0]
        logits = jnp.einsum('bsd,de->bse', x, gate_w) + gate_b
        probs = jax.nn.softmax(logits, axis=-1)
        top_probs, top_idx = jax.lax.top_k(probs, 2)
        top_probs = top_probs / jnp.sum(top_probs, axis=-1, keepdims=True)
        dispatch = jnp.sum(jax.nn.one_hot(top_idx, n_experts, dtype=x.dtype) * top_probs[..., None], axis=-2)
        h1 = jnp.einsum('bsd,edh->bseh', x, w1)
        h2 = jnp.einsum('bsd,edh->bseh', x, w2)
        hidden = jax.nn.silu(h1) * h2
        expert_out = jnp.einsum('bseh,eho->bseo', hidden, w3)
        return jnp.einsum('bseo,bse->bso', expert_out, dispatch)

    def _L1_attn_ref(x, ln1_g, ln1_b, qkv_w, qkv_b, bias_table, scale, proj_w, proj_b, ln2_g, ln2_b):
        import jax, jax.numpy as jnp
        import numpy as np
        SEQ_LEN = 512
        EMBED_DIM = 64
        BATCH = 8
        LN_EPS = 1e-05

        def _layernorm(x, g, b):
            mu = jnp.mean(x, axis=-1, keepdims=True)
            var = jnp.mean(jnp.square(x - mu), axis=-1, keepdims=True)
            return (x - mu) * jax.lax.rsqrt(var + LN_EPS) * g + b
        B, N, C = x.shape
        h = _layernorm(x, ln1_g, ln1_b)
        qkv = h @ qkv_w + qkv_b
        q, k, v = jnp.split(qkv, 3, axis=-1)
        coords = jnp.arange(N)
        rel_idx = coords[None, :] - coords[:, None] + (N - 1)
        rel_bias = bias_table[rel_idx]
        attn = jnp.einsum('bnc,bmc->bnm', q, k) + rel_bias
        attn = jax.nn.softmax(attn, axis=-1) * scale
        out = jnp.einsum('bnm,bmc->bnc', attn, v)
        out = out @ proj_w + proj_b
        out = _layernorm(out, ln2_g, ln2_b)
        return out

    def _L1_ffn_ref(input_embeddings, router_w, w1, b1, w2, b2):
        import jax, jax.numpy as jnp
        import numpy as np
        NUM_EXPERTS = 8
        TOP_K = 2
        B, S, D = (8, 2048, 64)

        def _moe(tokens, router_w, w1, b1, w2, b2):
            N = tokens.shape[0]
            E = router_w.shape[0]
            logits = tokens.astype(jnp.float32) @ router_w.astype(jnp.float32).T
            probs = jax.nn.softmax(logits, axis=-1)
            rw, re = jax.lax.top_k(probs, TOP_K)
            if TOP_K > 1:
                rw = rw / jnp.maximum(rw.sum(-1, keepdims=True), 1e-12)
            rw = rw.astype(tokens.dtype)
            combine = jnp.zeros((N, E), tokens.dtype).at[jnp.arange(N)[:, None], re].set(rw)
            out = tokens
            for e in range(E):
                h = jax.nn.gelu(tokens @ w1[e] + b1[e], approximate=False)
                y = h @ w2[e] + b2[e]
                out = out + combine[:, e:e + 1] * y
            return out
        b, s, d = input_embeddings.shape
        tokens = input_embeddings.reshape(b * s, d)
        return _moe(tokens, router_w, w1, b1, w2, b2).reshape(b, s, d)

    def _L2_attn_ref(x, Wq, Wk, Wv, Wo, bo, ln1_g, ln1_b, W1, b1, W2, b2, ln2_g, ln2_b):
        import jax, jax.numpy as jnp
        import numpy as np
        EMB, HEADS, DEPTH, SEQ, BATCH = (64, 8, 4, 2048, 4)
        DH = EMB // HEADS
        FF = 4 * EMB
        EPS = 1e-05

        def _layernorm(x, g, b):
            mu = x.mean(-1, keepdims=True)
            var = ((x - mu) ** 2).mean(-1, keepdims=True)
            return (x - mu) * jax.lax.rsqrt(var + EPS) * g + b

        def _linear_attn(x, Wq, Wk, Wv, Wo, bo):
            b, n, dm = x.shape
            split = lambda t: t.reshape(b, n, HEADS, DH).transpose(0, 2, 1, 3)
            scale = DH ** (-0.25)
            q = jax.nn.softmax(split(x @ Wq) * scale, axis=-1)
            k = jax.nn.softmax(split(x @ Wk) * scale, axis=-2)
            v = split(x @ Wv)
            context = jnp.einsum('bhnd,bhne->bhde', k, v)
            out = jnp.einsum('bhnd,bhde->bhne', q, context)
            out = out.transpose(0, 2, 1, 3).reshape(b, n, dm)
            return out @ Wo + bo

        def _forward(x, Wq, Wk, Wv, Wo, bo, ln1_g, ln1_b, W1, b1, W2, b2, ln2_g, ln2_b):
            for i in range(DEPTH):
                h = _layernorm(x, ln1_g[i], ln1_b[i])
                x = x + _linear_attn(h, Wq[i], Wk[i], Wv[i], Wo[i], bo[i])
                h = _layernorm(x, ln2_g[i], ln2_b[i])
                x = x + (jax.nn.gelu(h @ W1[i] + b1[i], approximate=False) @ W2[i] + b2[i])
            return x
        return _forward(x, Wq, Wk, Wv, Wo, bo, ln1_g, ln1_b, W1, b1, W2, b2, ln2_g, ln2_b)

    def _L2_ffn_ref(features, router_w1, router_b1, router_w2, router_b2, expert_w1, expert_b1, expert_w2, expert_b2, expert_w3, expert_b3):
        import jax, jax.numpy as jnp
        import numpy as np
        E, D, H, TOP_K = (6, 64, 64, 2)
        ROUTER_H = D // 2
        rh = jax.nn.relu(features @ router_w1 + router_b1)
        expert_logits = jax.nn.softmax(rh @ router_w2 + router_b2, axis=-1)
        top_w, top_i = jax.lax.top_k(expert_logits, TOP_K)
        routing_weights = jax.nn.softmax(top_w, axis=-1)
        h1 = jax.nn.relu(jnp.einsum('bsd,edh->bseh', features, expert_w1) + expert_b1)
        h2 = jax.nn.relu(jnp.einsum('bseh,ehf->bsef', h1, expert_w2) + expert_b2)
        expert_out = jnp.einsum('bsef,efo->bseo', h2, expert_w3) + expert_b3
        sel = jnp.take_along_axis(expert_out, top_i[:, :, :, None], axis=2)
        combined = jnp.sum(sel * routing_weights[..., None], axis=2)
        return combined

    def _L3_attn_ref(v, WQ, WK, WV, Wout, bout):
        import jax, jax.numpy as jnp
        import numpy as np
        IN_C = 64
        HID_C = 64
        HEADS = 8
        SCALE = 1.0 / np.sqrt(HID_C / HEADS).astype(np.float32)
        B, S, C = v.shape
        H = HEADS
        q = (v @ WQ).reshape(B, S, H, C)
        k = (v @ WK).reshape(B, S, H, C)
        val = (v @ WV).reshape(B, S, H, C)
        scores = jnp.einsum('bshc,bthc->bsth', q, k) * SCALE
        A = jax.nn.softmax(scores, axis=2)
        u = jnp.einsum('bsth,bthc->bshc', A, val).reshape(B, S, H * C)
        return u @ Wout + bout

    def _L3_ffn_ref(x, sW1, sb1, sW2, sb2, sW3, sb3, eW1, eb1, eW2, eb2, eW3, eb3, gW, gb):
        import jax, jax.numpy as jnp
        import numpy as np
        B, A = (1024, 8)
        IN, OUT = (64, 64)
        SH1, SH2 = (64, 128)
        EH1, EH2 = (128, 64)
        E, TOPK = (4, 2)

        def _shared_mlp(x, W1, b1, W2, b2, W3, b3):
            h = jax.nn.relu(x @ W1 + b1)
            h = jax.nn.relu(h @ W2 + b2)
            return h @ W3 + b3

        def _experts_mlp(x, eW1, eb1, eW2, eb2, eW3, eb3):
            h = jax.nn.relu(jnp.einsum('baf,efh->ebah', x, eW1) + eb1[:, None, None, :])
            h = jax.nn.relu(jnp.einsum('ebah,ehg->ebag', h, eW2) + eb2[:, None, None, :])
            o = jnp.einsum('ebag,ego->ebao', h, eW3) + eb3[:, None, None, :]
            return jnp.moveaxis(o, 0, -1)
        all_out = _experts_mlp(x, eW1, eb1, eW2, eb2, eW3, eb3)
        shared = _shared_mlp(x, sW1, sb1, sW2, sb2, sW3, sb3)
        gates = jax.nn.softmax(x @ gW + gb, axis=-1)
        topv, topi = jax.lax.top_k(gates, TOPK)
        topw = jax.nn.softmax(topv, axis=-1)
        sel = jnp.take_along_axis(all_out, topi[:, :, None, :], axis=-1)
        gated = jnp.sum(sel * topw[:, :, None, :], axis=-1)
        return shared + gated
    h = _L0_tok_ref(x, L0_tok_W)
    h = h + _L0_attn_ref(_layernorm(h, axis=-1), L0_attn_W)
    h = h + _L0_ffn_ref(_layernorm(h, axis=-1), L0_ffn_gate_w, L0_ffn_gate_b, L0_ffn_w1, L0_ffn_w2, L0_ffn_w3)
    h = h + _L1_attn_ref(_layernorm(h, axis=-1), L1_attn_ln1_g, L1_attn_ln1_b, L1_attn_qkv_w, L1_attn_qkv_b, L1_attn_bias_table, L1_attn_scale, L1_attn_proj_w, L1_attn_proj_b, L1_attn_ln2_g, L1_attn_ln2_b)
    h = h + _L1_ffn_ref(_layernorm(h, axis=-1), L1_ffn_router_w, L1_ffn_w1, L1_ffn_b1, L1_ffn_w2, L1_ffn_b2)
    h = h + _L2_attn_ref(_layernorm(h, axis=-1), L2_attn_Wq, L2_attn_Wk, L2_attn_Wv, L2_attn_Wo, L2_attn_bo, L2_attn_ln1_g, L2_attn_ln1_b, L2_attn_W1, L2_attn_b1, L2_attn_W2, L2_attn_b2, L2_attn_ln2_g, L2_attn_ln2_b)
    h = h + _L2_ffn_ref(_layernorm(h, axis=-1), L2_ffn_router_w1, L2_ffn_router_b1, L2_ffn_router_w2, L2_ffn_router_b2, L2_ffn_expert_w1, L2_ffn_expert_b1, L2_ffn_expert_w2, L2_ffn_expert_b2, L2_ffn_expert_w3, L2_ffn_expert_b3)
    h = h + _L3_attn_ref(_layernorm(h, axis=-1), L3_attn_WQ, L3_attn_WK, L3_attn_WV, L3_attn_Wout, L3_attn_bout)
    h = h + _L3_ffn_ref(_layernorm(h, axis=-1), L3_ffn_sW1, L3_ffn_sb1, L3_ffn_sW2, L3_ffn_sb2, L3_ffn_sW3, L3_ffn_sb3, L3_ffn_eW1, L3_ffn_eb1, L3_ffn_eW2, L3_ffn_eb2, L3_ffn_eW3, L3_ffn_eb3, L3_ffn_gW, L3_ffn_gb)
    return h

_drawn_inputs = setup_inputs


def setup_inputs(seed=0):
    import zlib

    import numpy as np

    out = dict(_drawn_inputs(seed))
    spreads = {'L0_ffn_gate_b': (0.0, 0.8),
     'L1_attn_ln1_g': (1.0, 0.6),
     'L1_attn_ln1_b': (0.0, 0.8),
     'L1_attn_qkv_b': (0.0, 0.309),
     'L1_attn_proj_b': (0.0, 0.1),
     'L1_attn_ln2_g': (1.0, 0.2),
     'L1_attn_ln2_b': (0.0, 0.1),
     'L1_ffn_b1': (0.0, 0.39),
     'L1_ffn_b2': (0.0, 0.1),
     'L2_attn_bo': (0.0, 0.1),
     'L2_attn_ln1_g': (1.0, 0.6),
     'L2_attn_ln1_b': (0.0, 0.8),
     'L2_attn_b1': (0.0, 0.8),
     'L2_attn_b2': (0.0, 0.1),
     'L2_attn_ln2_g': (1.0, 0.6),
     'L2_attn_ln2_b': (0.0, 0.8),
     'L2_ffn_router_b1': (0.0, 0.8),
     'L2_ffn_router_b2': (0.0, 0.8),
     'L2_ffn_expert_b1': (0.0, 0.8),
     'L2_ffn_expert_b2': (0.0, 0.8),
     'L2_ffn_expert_b3': (0.0, 0.366),
     'L3_ffn_sb1': (0.0, 0.8),
     'L3_ffn_sb2': (0.0, 0.697),
     'L3_ffn_sb3': (0.0, 0.771),
     'L3_ffn_eb1': (0.0, 0.8),
     'L3_ffn_eb2': (0.0, 0.8),
     'L3_ffn_eb3': (0.0, 1.034),
     'L3_ffn_gb': (0.0, 0.8)}
    factors = {'L0_ffn_gate_w': 8.0,
     'L0_ffn_w1': 8.0,
     'L0_ffn_w2': 8.0,
     'L0_ffn_w3': 7.916,
     'L1_attn_qkv_w': 8.0,
     'L1_attn_bias_table': 8.0,
     'L2_attn_Wq': 8.0,
     'L2_attn_Wk': 8.0,
     'L2_attn_Wv': 3.163,
     'L2_attn_Wo': 3.542,
     'L2_attn_W1': 3.264,
     'L2_attn_W2': 2.816,
     'L2_ffn_expert_w1': 3.997,
     'L2_ffn_expert_w2': 3.796,
     'L3_attn_WQ': 8.0,
     'L3_attn_WK': 8.0,
     'L3_attn_bout': 6.413,
     'L3_ffn_sW1': 6.492,
     'L3_ffn_sW2': 4.561,
     'L3_ffn_sW3': 3.231,
     'L3_ffn_eW1': 8.0,
     'L3_ffn_eW2': 6.49,
     'L3_ffn_eW3': 5.727,
     'L3_ffn_gW': 3.06}
    for name, (base, spread) in spreads.items():
        noise = np.random.default_rng([zlib.crc32(name.encode()), seed]).standard_normal(out[name].shape)
        drawn = base * np.exp(spread * noise) if base else spread * noise
        out[name] = jnp.asarray(drawn.astype(out[name].dtype))
    for name, factor in factors.items():
        out[name] = (out[name] * factor).astype(out[name].dtype)
    return out
```

```python
from contextlib import ExitStack

import numpy as np
import concourse.bass as bass
from concourse import mybir

F32 = mybir.dt.float32
F32R = mybir.dt.float32r
U32 = mybir.dt.uint32
ACT = mybir.ActivationFunctionType
ALU = mybir.AluOpType
AX = mybir.AxisListType

P = 128
B, C, TIME, V = 2, 64, 128, 64
D = 64
PATCH, STRIDE = 16, 8
NPATCH = TIME // STRIDE
N = V * NPATCH
T = B * N
NT = T // P
NTB = NT // B
BANK = 512
G = T // BANK
TPG = BANK // P
FREQ = 2 * (PATCH // 2 + 1)
EPS = 1e-5
E0, H0 = 16, 128
E1 = 8
LAYERS, FF, HEADS2 = 4, 256, 8
E2, R2 = 6, 32
HEADS = 8
E3 = 4
W2P = 2 * E2


class Layout:

    def __init__(self):
        self.at, self.n = {}, 0

    def add(self, name, cols):
        self.at[name] = (self.n, self.n + cols)
        self.n += cols

    def __getitem__(self, name):
        return slice(*self.at[name])


def split_layout_early():
    w = Layout()
    w.add("l0_attn", 128)
    w.add("l0_gate", E0)
    w.add("l0_w1", E0 * H0)
    w.add("l0_w2", E0 * H0)
    return w


def split_layout_mid():
    w = Layout()
    w.add("l1_q", 128)
    w.add("l1_k", 128)
    w.add("l1_v", 64)
    w.add("l1_gate", E1)
    w.add("l1_w1", E1 * D)
    for i in range(LAYERS):
        w.add(f"l2_k{i}", 128)
        w.add(f"l2_qv{i}", 128)
        w.add(f"l2_w1{i}", FF)
    w.add("l2_router", 128)
    w.add("l2_e1", E2 * D)
    return w


def split_layout_late():
    w = Layout()
    w.add("l3_v", HEADS * D)
    w.add("l3_gate", E3)
    w.add("l3_s1", 128)
    w.add("l3_e1", E3 * 128)
    return w


def full_layout():
    w = Layout()
    w.add("ident", 128)
    w.add("fold", D)
    w.add("expert_rows", E0)
    w.add("iota", 16)
    w.add("head_mask", 128)
    w.add("l0_w3", E0 * D)
    w.add("l1_qb", 1)
    w.add("l1_kb", 1)
    w.add("l1_post", 128)
    w.add("l1_w2", E1 // 2 * D)
    w.add("l1_b1", E1 // 2)
    w.add("l1_b2", D)
    for i in range(LAYERS):
        w.add(f"l2_wo{i}", D)
        w.add(f"l2_w2{i}", 2 * D)
        w.add(f"l2_b1{i}", 2)
    w.add("l2_rb1", 1)
    w.add("l2_rw2", E2)
    w.add("l2_e2", E2 // 2 * 128)
    w.add("l2_e3", E2 // 2 * D)
    w.add("l2_eb1", E2 // 2)
    w.add("l2_eb2", E2 // 2)
    w.add("l2_eb3", D)
    w.add("l3_post", HEADS // 2 * 128)
    w.add("l3_s2", 128)
    w.add("l3_s3", D)
    w.add("l3_sb1", 1)
    w.add("l3_sb2", 1)
    w.add("l3_e2", E3 * D)
    w.add("l3_e3", E3 // 2 * D)
    w.add("l3_eb1", E3)
    w.add("l3_eb2", E3 // 2)
    w.add("l3_eb3", D)
    return w


def row_layout():
    w = Layout()
    w.add("l0_gate_b", E0)
    for x in ("ln1_g", "ln1_b", "vb", "proj_b", "ln2_g", "ln2_b"):
        w.add("l1_" + x, D)
    w.add("l1_scale", 1)
    for i in range(LAYERS):
        for x in ("ln1_g", "ln1_b", "bo", "ln2_g", "ln2_b", "b2"):
            w.add(f"l2_{x}{i}", D)
    w.add("l2_rb2", E2)
    w.add("l3_bout", D)
    w.add("l3_sb3", D)
    w.add("l3_gate_b", E3)
    return w


class Signal:

    def __init__(self, nc, name):
        self.sem, self.base = nc.alloc_semaphore(name), 0

    def __call__(self, n):
        return self.base + n

    def passed(self, n):
        self.base += n


def wide(ap, n):
    return ap.unsqueeze(2).to_broadcast([ap.shape[0], ap.shape[1], n])


def rows_over(ap, n):
    return ap.unsqueeze(1).to_broadcast([ap.shape[0], n, ap.shape[1]])


class Tower:

    def __init__(self, nc, ctx):
        self.nc, self.ctx, self.counters, self.named = nc, ctx, {}, {}
        self.full, self.row = full_layout(), row_layout()
        self.early, self.mid, self.late = split_layout_early(), split_layout_mid(), split_layout_late()

    def sb(self, name, shape, dt=F32, ctx=None):
        self.named[name] = self.named.get(name, 0) + 1
        if self.named[name] > 1:
            name = f"{name}_{self.named[name]}"
        return (ctx or self.ctx).enter_context(self.nc.sbuf_tensor(name, shape, dt))

    def counter(self, name):
        if name not in self.counters:
            self.counters[name] = Signal(self.nc, name)
        return self.counters[name]

    def w(self, name):
        return self.w_full[:, self.full[name]]

    def r(self, name):
        return self.w_row[:, self.row[name]]




def embed_stage(tw, x, dft, wk, early, full, row):
    nc, h = tw.nc, tw.h
    NB = NPATCH + 1
    wk_landed = nc.alloc_semaphore("wk_landed")
    x_landed = [nc.alloc_semaphore(f"x_landed{b}") for b in range(B)]
    zeroed = nc.alloc_semaphore("dft_rows_zeroed")
    taps_ready = nc.alloc_semaphore("taps_ready")
    taps_copied = nc.alloc_semaphore("taps_copied")
    taps_turned = nc.alloc_semaphore("taps_turned")
    conv_ready = nc.alloc_semaphore("conv_ready")
    conv_copied = nc.alloc_semaphore("conv_copied")
    turned = nc.alloc_semaphore("embed_turned")
    hi_made = nc.alloc_semaphore("early_hi_made")
    with ExitStack() as ctx:
        xs = tw.sb("series", [P, B, NB, 4, V], ctx=ctx)
        wks = tw.sb("wk_rows", [P, C * D], ctx=ctx)
        dfts = tw.sb("dft_rows", [P, PATCH], ctx=ctx)
        taps_row = tw.sb("taps_row", [PATCH, C * D], ctx=ctx)
        taps = tw.sb("taps", [P, 2, 4, D], ctx=ctx)
        ht = tw.sb("embed_t", [P, B, V, NPATCH // 2], ctx=ctx)
        raw = tw.sb("early_raw", [P, tw.early.n], ctx=ctx)
        block = ctx.enter_context(nc.Block())

        @block.sync
        def _(sp):
            sp.wait_ge(zeroed, 2)
            sp.dma_start(wks[0:FREQ, :], wk).then_inc(wk_landed, 16)
            sp.dma_start(dfts[0:FREQ, :], dft).then_inc(wk_landed, 16)
            for b in range(B):
                blocks = x[b].rearrange("c (m u s) v -> u c m (s v)", u=2, s=4)
                for u in range(2):
                    rows = xs[64 * u:64 * u + 64, b]
                    sp.dma_start(rows[:, 0:NPATCH].rearrange("c m s v -> c m (s v)"),
                                 blocks[u]).then_inc(x_landed[b], 16)
                    for s in range(4):
                        sp.dma_start(rows[:, NPATCH, s], x[b, :, TIME - 1, :]).then_inc(x_landed[b], 16)
            sp.wait_ge(taps_copied, 8)
            for hh in range(2):
                for u in range(2):
                    for s in range(4):
                        t = 8 * hh + 4 * u + s
                        sp.dma_start(taps[64 * u:64 * u + 64, hh, s, :],
                                     taps_row[t:t + 1, :].rearrange("o (c j) -> o c j", c=C)).then_inc(taps_turned, 16)

        @block.gpsimd
        def _(pool):
            pool.memset(wks[:, :], 0.0).then_inc(zeroed, 1)
            pool.memset(dfts[:, :], 0.0).then_inc(zeroed, 1)
            for k in range(8):
                c = slice(k * tw.early.n // 8, (k + 1) * tw.early.n // 8)
                pool.wait_ge(hi_made, k + 1)
                pool.tensor_tensor(tw.early_lo[:, c], raw[:, c], tw.early_hi[:, c].bitcast(F32), ALU.subtract)

        @block.scalar
        def _(act):
            for half in range(2):
                act.dma_start(raw[64 * half:64 * half + 64, :], early).then_inc(tw.early_landed, 16)
            act.dma_start(tw.w_full[:, :], full).then_inc(tw.full_landed, 16)
            act.dma_start(tw.w_row[:, :], row.partition_broadcast(P)).then_inc(tw.row_landed, 16)
            act.wait_ge(tw.early_landed, 32)
            for k in range(8):
                c = slice(k * tw.early.n // 8, (k + 1) * tw.early.n // 8)
                nc.scalar.copy(tw.early_hi[:, c], raw[:, c]).then_inc(hi_made, 1)
            for b in range(B):
                act.wait_ge(conv_ready, b + 1)
                nc.scalar.copy(ht[:, b].rearrange("p v n -> p n v"),
                               tw.ps[:, b, :].rearrange("p (n v) -> p n v", v=V)).then_inc(conv_copied, 1)

        @block.tensor
        def _(pe):
            pe.wait_ge(wk_landed, 32)
            for k in range(8):
                nc.tensor.matmul(tw.ps[0:PATCH, k, :], dfts[:, :], wks[:, k * BANK:(k + 1) * BANK],
                                 start=True, stop=True).then_inc(taps_ready, 1)
            pe.wait_ge(taps_turned, 16 * 16)
            pe.wait_ge(taps_copied, 8)
            for b in range(B):
                pe.wait_ge(x_landed[b], 16 * 10)
                for k in range(8):
                    hh, s = k // 4, k % 4
                    for par in range(2):
                        first = hh + par
                        mm = nc.tensor.matmul(tw.ps[64 * par:64 * par + 64, b, :],
                                              taps[:, hh, s, :], xs[:, b, first:first + 15:2, s, :],
                                              start=(k == 0), stop=(k == 7))
                mm.then_inc(conv_ready, 1)
            pe.wait_ge(tw.full_landed, 16)
            for b in range(B):
                pe.wait_ge(conv_copied, b + 1)
                for vhi in range(4):
                    mm = nc.tensor.transpose(tw.ps[:, 2 + b, vhi * P:(vhi + 1) * P],
                                             ht[:, b, 16 * vhi:16 * vhi + 16, :].rearrange("p v n -> p (v n)"),
                                             tw.w("ident"))
                mm.then_inc(turned, 1)

        @block.vector
        def _(dve):
            nc.vector.memset(tw.minus_half[:, :], -0.5)
            dve.wait_ge(tw.row_landed, 16)
            for k in range(8):
                dve.wait_ge(taps_ready, k + 1)
                nc.vector.tensor_copy(taps_row[:, k * BANK:(k + 1) * BANK], tw.ps[0:PATCH, k, :])\
                    .then_inc(taps_copied, 1)
            for b in range(B):
                dve.wait_ge(turned, b + 1)
                nc.vector.tensor_copy(h[:, 8 * b:8 * b + 8, :].rearrange("p t j -> p (t j)"), tw.ps[:, 2 + b, :])




def norm_stage(tw, src, gamma=None, beta=None, keep=None, turn=True):
    nc = tw.nc
    sums, centred, squared, spread = (tw.counter(x) for x in ("ln_sums", "ln_centred", "ln_squared", "ln_spread"))
    eps_added, rooted, normed = (tw.counter(x) for x in ("ln_eps_added", "ln_rooted", "ln_normed"))
    hi_made, lo_made, turned, xt_act, xt_dve = (
        tw.counter(x) for x in ("ln_hi_made", "ln_lo_made", "ln_turned", "xt_act", "xt_dve"))
    affine = gamma is not None
    x = keep if keep is not None else tw.xn
    steps = 3 if affine else 1
    dst = (lambda g: x[:, TPG * g:TPG * g + TPG, :])
    with ExitStack() as ctx:
        total, var, rstd = (tw.sb("ln_" + n, [P, NT], ctx=ctx) for n in ("total", "var", "rstd"))
        xc = tw.sb("ln_xc", [P, NT, D], ctx=ctx)
        sq = tw.sb("ln_sq", [P, NT, D], ctx=ctx)
        pair = tw.sb("ln_pair", [P, NT, 2 * D], ctx=ctx)
        block = ctx.enter_context(nc.Block())

        @block.vector
        def _(dve):
            for g in range(G):
                t = slice(TPG * g, TPG * g + TPG)
                nc.vector.reduce_sum(total[:, t], src[:, t, :], AX.X).then_inc(sums.sem, 1)
                dve.wait_ge(sums.sem, sums(g + 1))
                nc.vector.scalar_tensor_tensor(out=xc[:, t, :], in0=wide(total[:, t], D), scalar=-1.0 / D,
                                               in1=src[:, t, :], op0=ALU.mult, op1=ALU.add)\
                    .then_inc(centred.sem, 1)
            for g in range(G):
                t = slice(TPG * g, TPG * g + TPG)
                dve.wait_ge(squared.sem, squared(g + 1))
                nc.vector.reduce_sum(var[:, t], sq[:, t, :], AX.X).then_inc(spread.sem, 1)
            for g in range(G):
                t = slice(TPG * g, TPG * g + TPG)
                dve.wait_ge(rooted.sem, rooted(g + 1))
                nc.vector.tensor_tensor(dst(g), xc[:, t, :], wide(rstd[:, t], D), ALU.mult)\
                    .then_inc(normed.sem, 1)
                if affine:
                    dve.wait_ge(normed.sem, normed(steps * g + 1))
                    nc.vector.tensor_tensor(dst(g), dst(g), rows_over(gamma, TPG), ALU.mult).then_inc(normed.sem, 1)
                    dve.wait_ge(normed.sem, normed(steps * g + 2))
                    nc.vector.tensor_tensor(dst(g), dst(g), rows_over(beta, TPG), ALU.add).then_inc(normed.sem, 1)
            if turn:
                for g in range(0, G, 2):
                    dve.wait_ge(turned.sem, turned(g + 1))
                    nc.vector.tensor_copy(tw.xt[:, BANK * g:BANK * g + BANK], tw.ps[:, g, :]).then_inc(xt_dve.sem, 1)

        @block.scalar
        def _(act):
            for g in range(G):
                t = slice(TPG * g, TPG * g + TPG)
                act.wait_ge(centred.sem, centred(g + 1))
                nc.scalar.activation(sq[:, t, :], xc[:, t, :], ACT.Square).then_inc(squared.sem, 1)
            if turn:
                for g in range(G):
                    t = slice(TPG * g, TPG * g + TPG)
                    act.wait_ge(normed.sem, normed(steps * (g + 1)))
                    nc.scalar.copy(pair[:, t, 0:D].bitcast(F32R), dst(g)).then_inc(hi_made.sem, 1)
                for g in range(1, G, 2):
                    act.wait_ge(turned.sem, turned(g + 1))
                    nc.scalar.copy(tw.xt[:, BANK * g:BANK * g + BANK], tw.ps[:, g, :]).then_inc(xt_act.sem, 1)

        @block.gpsimd
        def _(pool):
            for g in range(G):
                t = slice(TPG * g, TPG * g + TPG)
                pool.wait_ge(spread.sem, spread(g + 1))
                pool.tensor_scalar(var[:, t], var[:, t], 1.0 / D, EPS, ALU.mult, ALU.add)\
                    .then_inc(eps_added.sem, 1)
                pool.wait_ge(eps_added.sem, eps_added(g + 1))
                pool.tensor_tensor(rstd[:, t], var[:, t], tw.minus_half[:, t], ALU.pow)\
                    .then_inc(rooted.sem, 1)
            if turn:
                for g in range(G):
                    t = slice(TPG * g, TPG * g + TPG)
                    pool.wait_ge(hi_made.sem, hi_made(g + 1))
                    pool.tensor_tensor(pair[:, t, D:2 * D], dst(g), pair[:, t, 0:D], ALU.subtract)\
                        .then_inc(lo_made.sem, 1)

        if turn:
            @block.tensor
            def _(pe):
                for g in range(G):
                    pe.wait_ge(lo_made.sem, lo_made(g + 1))
                    for k in range(TPG):
                        mm = nc.tensor.transpose(tw.ps[:, g, k * P:(k + 1) * P], pair[:, TPG * g + k, :],
                                                 tw.w("ident"))
                    mm.then_inc(turned.sem, 1)
    for s in (sums, centred, squared, spread, eps_added, rooted):
        s.passed(G)
    normed.passed(steps * G)
    if turn:
        for s in (hi_made, lo_made, turned):
            s.passed(G)
        xt_dve.passed(G // 2)
        xt_act.passed(G // 2)




def attention_stage(tw, name, groups, scale, q_hi, q_lo, keys, value, post, bias_strips, finish, out):
    nc, ps = tw.nc, tw.ps
    U = 8 * len(groups)
    NG = len(groups)
    s_ready, biased, maxed, p_ready = (tw.counter(x) for x in ("s_ready", "s_biased", "s_maxed", "p_ready"))
    p_turned, pt_dve, pt_act = (tw.counter(x) for x in ("p_turned", "pt_dve", "pt_act"))
    o_ready, o_copied, y_ready, y_scaled, inv_ready, y_added = (
        tw.counter(x) for x in ("o_ready", "o_copied", "y_ready", "y_scaled", "inv_ready", "y_added"))
    unscaled = tw.counter("s_unscaled")
    S_BANK, T_BANK, O_BANK = 0, 4, 6
    HALF = N // 2
    n_add = 2 if finish != "store" else 0
    with ExitStack() as ctx:
        prob = tw.sb(name + "_prob", [P, 2, N], ctx=ctx)
        prob_t = tw.sb(name + "_prob_t", [P, 2, 2, NTB, HALF], ctx=ctx)
        nmax = tw.sb(name + "_nmax", [P, U], ctx=ctx)
        raw_max = tw.sb(name + "_raw_max", [P, U], ctx=ctx)
        total = tw.sb(name + "_total", [P, NG, 4, 2], ctx=ctx)
        inv = tw.sb(name + "_inv", [P, NG, 4, 2], ctx=ctx)
        o_sb = tw.sb(name + "_o", [P, 2, BANK], ctx=ctx)
        y_sb = tw.sb(name + "_y", [P, 2, 4, 2, D], ctx=ctx)
        if bias_strips is not None:
            logits = tw.sb(name + "_logits", [P, 2, N], ctx=ctx)
        block = ctx.enter_context(nc.Block())

        def parts(u):
            return u // 8, u % 8 // 4, u % 4

        @block.tensor
        def _(pe):
            for i in range(U + 20):
                if i < U:
                    g, j, nt = parts(i)
                    members, q0, k0, _ = groups[g]
                    if i >= 2:
                        if bias_strips is None:
                            pe.wait_ge(p_ready.sem, p_ready(i - 1))
                        else:
                            pe.wait_ge(biased.sem, biased(i - 1))
                    for mh in range(2):
                        for k, q in enumerate((q_hi, q_lo)):
                            mm = nc.tensor.matmul(ps[:, S_BANK + 2 * (i % 2) + mh, :],
                                                  q(members[j])[:, q0[j] + nt * P:q0[j] + nt * P + P],
                                                  keys[:, k0[j] + mh * BANK:k0[j] + mh * BANK + BANK],
                                                  start=(k == 0), stop=(k == 1))
                    mm.then_inc(s_ready.sem, 1)
                if 1 <= i <= U:
                    u = i - 1
                    pe.wait_ge(p_ready.sem, p_ready(u + 1))
                    for half in range(2):
                        if u >= 1:
                            copied = pt_act if half else pt_dve
                            pe.wait_ge(copied.sem, copied(u))
                        for k in range(4):
                            mm = nc.tensor.transpose(ps[:, T_BANK + half, k * P:(k + 1) * P],
                                                     prob[:, u % 2, (4 * half + k) * P:(4 * half + k + 1) * P],
                                                     tw.w("ident"))
                        mm.then_inc(p_turned.sem, 1)
                g, w = (i - 9) // 8, (i - 9) % 8
                if 0 <= g < NG:
                    members = groups[g][0]
                    if w == 0:
                        pe.wait_ge(pt_dve.sem, pt_dve(8 * (g + 1)))
                        pe.wait_ge(pt_act.sem, pt_act(8 * (g + 1)))
                        if g >= 2:
                            pe.wait_ge(y_scaled.sem, y_scaled(g - 1))
                    for j in range(2):
                        mm = nc.tensor.matmul(ps[64 * j:64 * j + 64, O_BANK + g % 2, :], value(members[j], w),
                                              prob_t[:, g % 2, j, w, :], start=(w == 0), stop=(w == 7))
                    if w == 7:
                        mm.then_inc(o_ready.sem, 1)
                g = (i - 18) // 8
                if (i - 18) % 8 == 0 and 0 <= g < NG:
                    pe.wait_ge(o_copied.sem, o_copied(g + 1))
                    for nt in range(4):
                        mm = nc.tensor.matmul(ps[:, O_BANK + g % 2, nt * P:(nt + 1) * P],
                                              o_sb[:, g % 2, nt * P:(nt + 1) * P], post(g), start=True, stop=True)
                    mm.then_inc(y_ready.sem, 1)

        @block.scalar
        def _(act):
            for i in range(U + 20):
                if i < U:
                    g, j, nt = parts(i)
                    act.wait_ge(maxed.sem, maxed(i + 1))
                    if i >= 2:
                        act.wait_ge(p_turned.sem, p_turned(2 * (i - 1)))
                    source = ps[:, S_BANK + 2 * (i % 2):S_BANK + 2 * (i % 2) + 2, :].rearrange("p a b -> p (a b)")
                    if bias_strips is not None:
                        source = logits[:, i % 2, :]
                    nc.scalar.activation(prob[:, i % 2, :], source, ACT.Exp, bias=nmax[:, i:i + 1], scale=scale,
                                         accum_out=total[:, g, nt, j:j + 1]).then_inc(p_ready.sem, 1)
                if 1 <= i <= U:
                    u = i - 1
                    g, j, nt = parts(u)
                    act.wait_ge(p_turned.sem, p_turned(2 * u + 2))
                    if g >= 2 and u % 8 == 0:
                        act.wait_ge(o_ready.sem, o_ready(g - 1))
                    nc.scalar.copy(prob_t[:, g % 2, j, 4:8, nt * P:(nt + 1) * P],
                                   ps[:, T_BANK + 1, :].rearrange("p (a b) -> p a b", a=4)).then_inc(pt_act.sem, 1)
                g = (i - 17) // 8
                if (i - 17) % 8 == 0 and 0 <= g < NG:
                    act.wait_ge(o_ready.sem, o_ready(g + 1))
                    if g >= 2:
                        act.wait_ge(y_ready.sem, y_ready(g - 1))
                    nc.scalar.copy(o_sb[:, g % 2, :], ps[:, O_BANK + g % 2, :]).then_inc(o_copied.sem, 1)

        @block.vector
        def _(dve):
            for i in range(U + 20):
                if i < U:
                    g, j, nt = parts(i)
                    dve.wait_ge(s_ready.sem, s_ready(i + 1))
                    source = ps[:, S_BANK + 2 * (i % 2):S_BANK + 2 * (i % 2) + 2, :].rearrange("p a b -> p (a b)")
                    if bias_strips is not None:
                        qt = groups[g][3] + nt
                        vhi, par = qt // 2, qt % 2
                        if i >= 2:
                            dve.wait_ge(p_ready.sem, p_ready(i - 1))
                        for kpar in range(2):
                            strip = bias_strips[:, kpar - par + 1, (3 - vhi) * P:(7 - vhi) * P]
                            view = logits[:, i % 2, :].rearrange("p (a k b) -> p a k b", a=4, k=2)[:, :, kpar, :]
                            scores = source.rearrange("p (a k b) -> p a k b", a=4, k=2)[:, :, kpar, :]
                            ins = nc.vector.tensor_tensor(view, scores, strip.rearrange("p (a b) -> p a b", a=4),
                                                          ALU.add)
                        ins.then_inc(biased.sem, 1)
                        dve.wait_ge(biased.sem, biased(i + 1))
                        source = logits[:, i % 2, :]
                    if scale == 1.0:
                        nc.vector.tensor_reduce(nmax[:, i:i + 1], source, AX.X, ALU.max, negate=True)\
                            .then_inc(maxed.sem, 1)
                    else:
                        nc.vector.tensor_reduce(raw_max[:, i:i + 1], source, AX.X, ALU.max, negate=True)\
                            .then_inc(unscaled.sem, 1)
                        dve.wait_ge(unscaled.sem, unscaled(i + 1))
                        nc.vector.tensor_scalar(nmax[:, i:i + 1], raw_max[:, i:i + 1], scale, None, ALU.mult)\
                            .then_inc(maxed.sem, 1)
                if 1 <= i <= U:
                    u = i - 1
                    g, j, nt = parts(u)
                    dve.wait_ge(p_turned.sem, p_turned(2 * u + 1))
                    if g >= 2 and u % 8 == 0:
                        dve.wait_ge(o_ready.sem, o_ready(g - 1))
                    nc.vector.tensor_copy(prob_t[:, g % 2, j, 0:4, nt * P:(nt + 1) * P],
                                          ps[:, T_BANK, :].rearrange("p (a b) -> p a b", a=4)).then_inc(pt_dve.sem, 1)
                g = (i - 8) // 8
                if (i - 8) % 8 == 0 and 0 <= g < NG:
                    dve.wait_ge(p_ready.sem, p_ready(8 * (g + 1)))
                    nc.vector.reciprocal(inv[:, g], total[:, g]).then_inc(inv_ready.sem, 1)
                g = (i - 19) // 8
                if (i - 19) % 8 == 0 and 0 <= g < NG:
                    dve.wait_ge(y_ready.sem, y_ready(g + 1))
                    dve.wait_ge(inv_ready.sem, inv_ready(g + 1))
                    if g >= 2 and n_add:
                        dve.wait_ge(y_added.sem, y_added(n_add * (g - 1)))
                    rows = ps[:, O_BANK + g % 2, :].rearrange("p (n e) -> p n e", n=8)
                    if finish == "store":
                        for j in range(2):
                            ins = nc.vector.tensor_tensor(
                                out(g, j), ps[:, O_BANK + g % 2, :].rearrange("p (n j e) -> p n j e", n=4, j=2)[:, :, j],
                                wide(inv[:, g, :, j], D), ALU.mult)
                        ins.then_inc(y_scaled.sem, 1)
                    else:
                        nc.vector.tensor_tensor(y_sb[:, g % 2].rearrange("p n j e -> p (n j) e"), rows,
                                                wide(inv[:, g].rearrange("p n j -> p (n j)"), D), ALU.mult)\
                            .then_inc(y_scaled.sem, 1)

        if n_add:
            @block.gpsimd
            def _(pool):
                for g in range(NG):
                    pool.wait_ge(y_scaled.sem, y_scaled(g + 1))
                    for j in range(2):
                        if g or j:
                            pool.wait_ge(y_added.sem, y_added(2 * g + j))
                        pool.tensor_tensor(out(g, j), out(g, j), y_sb[:, g % 2, :, j, :], ALU.add)\
                            .then_inc(y_added.sem, 1)
    for s in (s_ready, maxed, p_ready, pt_dve, pt_act):
        s.passed(U)
    if scale != 1.0:
        unscaled.passed(U)
    if bias_strips is not None:
        biased.passed(U)
    p_turned.passed(2 * U)
    for s in (o_ready, o_copied, y_ready, y_scaled, inv_ready):
        s.passed(NG)
    y_added.passed(n_add * NG)


def project_stage(tw, jobs):
    nc, ps = tw.nc, tw.ps
    made, hi_made, lo_made, kept = (tw.counter(x) for x in ("pj_made", "pj_hi", "pj_lo", "pj_kept"))
    nk = 0
    with ExitStack() as ctx:
        high = tw.sb("key_high", [P, 2, BANK], ctx=ctx)
        block = ctx.enter_context(nc.Block())

        @block.tensor
        def _(pe):
            for n, (wh, wl, col, bias, kind, dst) in enumerate(jobs):
                if n >= 8:
                    pe.wait_ge(lo_made.sem, lo_made(n - 7))
                    pe.wait_ge(hi_made.sem, hi_made(n - 7))
                nc.tensor.matmul(ps[:, n % 8, :], wh, tw.xt[:, col:col + BANK], start=True, stop=False)
                nc.tensor.matmul(ps[:, n % 8, :], wl, tw.xt[:, col:col + BANK], start=False, stop=True)\
                    .then_inc(made.sem, 1)

        @block.scalar
        def _(act):
            k = 0
            for n, (wh, wl, col, bias, kind, dst) in enumerate(jobs):
                act.wait_ge(made.sem, made(n + 1))
                b = bias if bias is not None else 0.0
                if kind == "queries":
                    nc.scalar.activation(dst[0], ps[:, n % 8, :], ACT.Identity, bias=b).then_inc(hi_made.sem, 1)
                else:
                    lower = b[D:P, :] if bias is not None else 0.0
                    upper = b[0:D, :] if bias is not None else 0.0
                    if k >= 2:
                        act.wait_ge(lo_made.sem, lo_made(n - 1))
                    nc.scalar.activation(dst[0][0:D, :], ps[0:D, n % 8, :], ACT.Identity, bias=upper)
                    nc.scalar.activation(high[D:P, k % 2, :].bitcast(F32R), ps[D:P, n % 8, :], ACT.Identity,
                                         bias=lower).then_inc(hi_made.sem, 1)
                    k += 1

        @block.vector
        def _(dve):
            k = 0
            for n, (wh, wl, col, bias, kind, dst) in enumerate(jobs):
                dve.wait_ge(hi_made.sem, hi_made(n + 1))
                b = bias if bias is not None else 0.0
                if kind == "queries":
                    nc.vector.scalar_tensor_tensor(out=dst[1], in0=ps[:, n % 8, :], scalar=b,
                                                   in1=dst[0].bitcast(F32), op0=ALU.add, op1=ALU.subtract)\
                        .then_inc(lo_made.sem, 1)
                else:
                    lower = b[D:P, :] if bias is not None else 0.0
                    nc.vector.scalar_tensor_tensor(out=dst[0][D:P, :], in0=ps[D:P, n % 8, :], scalar=lower,
                                                   in1=high[D:P, k % 2, :], op0=ALU.add, op1=ALU.subtract)\
                        .then_inc(lo_made.sem, 1)
                    k += 1
    for s in (made, hi_made, lo_made):
        s.passed(len(jobs))


def value_stage(tw, wh, wl, cols, tiles, dst, bias=None):
    nc, ps = tw.nc, tw.ps
    made, copied = tw.counter("vl_made"), tw.counter("vl_copied")
    with ExitStack() as ctx:
        block = ctx.enter_context(nc.Block())

        @block.tensor
        def _(pe):
            for n, t in enumerate(tiles):
                if n >= 8:
                    pe.wait_ge(copied.sem, copied(n - 7))
                nc.tensor.matmul(ps[:, n % 8, 0:cols], tw.xt[:, t * P:(t + 1) * P], wh, start=True, stop=False)
                nc.tensor.matmul(ps[:, n % 8, 0:cols], tw.xt[:, t * P:(t + 1) * P], wl, start=False, stop=True)\
                    .then_inc(made.sem, 1)

        @block.vector
        def _(dve):
            for n, t in enumerate(tiles):
                dve.wait_ge(made.sem, made(n + 1))
                if bias is None:
                    nc.vector.tensor_copy(dst(t), ps[:, n % 8, 0:cols]).then_inc(copied.sem, 1)
                else:
                    nc.vector.tensor_tensor(dst(t), ps[:, n % 8, 0:cols], bias, ALU.add).then_inc(copied.sem, 1)
    made.passed(len(tiles))
    copied.passed(len(tiles))




def route_stage(tw, experts, lhs, parts, bias, second_softmax):
    nc, ps, E = tw.nc, tw.ps, experts
    made, step, ex, turned, ct_dve = (tw.counter(x) for x in ("rt_made", "rt_step", "rt_exp", "rt_turned", "rt_ct"))
    ex_count = 2 if second_softmax else 1
    EP = max(E, 8)
    count = [0]
    last_step = 23 if second_softmax else 22
    with ExitStack() as ctx:
        lg = tw.sb("rt_logits", [P, NT, E], ctx=ctx)
        mx = tw.sb("rt_max", [P, NT], ctx=ctx)
        pr = tw.sb("rt_probs", [P, NT, EP], ctx=ctx)
        top = tw.sb("rt_top", [P, NT, 8], ctx=ctx)
        idx = tw.sb("rt_index", [P, NT, 8], U32, ctx=ctx)
        idf = tw.sb("rt_index_f", [P, NT, 2], ctx=ctx)
        wt = tw.sb("rt_weight", [P, NT, 2], ctx=ctx)
        sm = tw.sb("rt_sum", [P, NT], ctx=ctx)
        cw = tw.sb("rt_combine", [P, NT, E], ctx=ctx)
        c2 = tw.sb("rt_combine2", [P, NT, E], ctx=ctx)
        cp = tw.sb("rt_pair", [P, NT, P], ctx=ctx)
        block = ctx.enter_context(nc.Block())
        logits = ps[:, 0, 0:NT * E].rearrange("p (t e) -> p t e", e=E)

        @block.tensor
        def _(pe):
            for t in range(NT):
                for k, part in enumerate(parts):
                    mm = nc.tensor.matmul(logits[:, t, :], lhs(t), part, start=(k == 0), stop=(k == len(parts) - 1))
            mm.then_inc(made.sem, 1)
            pe.wait_ge(step.sem, step(last_step))
            for g in range(G):
                for k in range(TPG):
                    mm = nc.tensor.transpose(ps[:, 1 + g, k * P:(k + 1) * P], cp[:, TPG * g + k, :], tw.w("ident"))
                mm.then_inc(turned.sem, 1)

        @block.scalar
        def _(act):
            act.wait_ge(step.sem, step(5))
            nc.scalar.activation(pr[:, :, 0:E], lg[:, :, :], ACT.Exp).then_inc(ex.sem, 1)
            if second_softmax:
                act.wait_ge(step.sem, step(12))
                nc.scalar.activation(wt[:, :, 1], wt[:, :, 1], ACT.Exp).then_inc(ex.sem, 1)

        @block.vector
        def _(dve):
            def then(ins):
                count[0] += 1
                ins.then_inc(step.sem, 1)
                dve.wait_ge(step.sem, step(count[0]))

            then(nc.vector.memset(cp[:, :, :], 0.0))
            then(nc.vector.memset(pr[:, :, :], -1.0))
            dve.wait_ge(made.sem, made(1))
            if bias is not None:
                then(nc.vector.tensor_tensor(lg[:, :, :], logits, rows_over(bias, NT), ALU.add))
            else:
                then(nc.vector.tensor_copy(lg[:, :, :], logits))
            then(nc.vector.reduce_max(mx[:, :], lg[:, :, :], AX.X))
            then(nc.vector.tensor_tensor(lg[:, :, :], lg[:, :, :], wide(mx[:, :], E), ALU.subtract))
            dve.wait_ge(ex.sem, ex(1))
            then(nc.vector.reduce_sum(sm[:, :], pr[:, :, 0:E], AX.X))
            then(nc.vector.reciprocal(sm[:, :], sm[:, :]))
            then(nc.vector.tensor_tensor(pr[:, :, 0:E], pr[:, :, 0:E], wide(sm[:, :], E), ALU.mult))
            for t in range(NT):
                ins = nc.vector.max(top[:, t, :], pr[:, t, :])
            then(ins)
            for t in range(NT):
                ins = nc.vector.max_index(idx[:, t, :], top[:, t, :], pr[:, t, :])
            then(ins)
            then(nc.vector.tensor_copy(idf[:, :, :], idx[:, :, 0:2]))
            if second_softmax:
                then(nc.vector.tensor_tensor(wt[:, :, 1], top[:, :, 1], top[:, :, 0], ALU.subtract))
                dve.wait_ge(ex.sem, ex(2))
                then(nc.vector.tensor_scalar(sm[:, :], wt[:, :, 1], 1.0, None, ALU.add))
                then(nc.vector.reciprocal(sm[:, :], sm[:, :]))
                then(nc.vector.tensor_copy(wt[:, :, 0], sm[:, :]))
                then(nc.vector.tensor_tensor(wt[:, :, 1], wt[:, :, 1], sm[:, :], ALU.mult))
            else:
                then(nc.vector.tensor_tensor(sm[:, :], top[:, :, 0], top[:, :, 1], ALU.add))
                then(nc.vector.tensor_scalar(sm[:, :], sm[:, :], 1e-12, None, ALU.max))
                then(nc.vector.reciprocal(sm[:, :], sm[:, :]))
                then(nc.vector.tensor_tensor(wt[:, :, :], top[:, :, 0:2], wide(sm[:, :], 2), ALU.mult))
            for k, c in enumerate((cw, c2)):
                then(nc.vector.tensor_tensor(c[:, :, :], rows_over(tw.w("iota")[:, 0:E], NT), wide(idf[:, :, k], E),
                                             ALU.is_equal))
                then(nc.vector.tensor_tensor(c[:, :, :], c[:, :, :], wide(wt[:, :, k], E), ALU.mult))
            then(nc.vector.tensor_tensor(cw[:, :, :], cw[:, :, :], c2[:, :, :], ALU.add))
            then(nc.vector.tensor_copy(cp[:, :, 0:E].bitcast(F32R), cw[:, :, :]))
            then(nc.vector.tensor_tensor(cp[:, :, D:D + E], cw[:, :, :], cp[:, :, 0:E], ALU.subtract))
            assert count[0] == last_step
            for g in range(G):
                dve.wait_ge(turned.sem, turned(g + 1))
                nc.vector.tensor_copy(tw.ct[:, BANK * g:BANK * g + BANK], ps[:, 1 + g, :])
    made.passed(1)
    step.passed(count[0])
    ex.passed(ex_count)
    turned.passed(G)




def swiglu_experts_stage(tw, h, later):
    nc, ps = tw.nc, tw.ps
    U = G * E0
    up, silu, gated, hid_ready, down = (tw.counter(x) for x in ("x0_up", "x0_silu", "x0_gated", "x0_hidden", "x0_down"))
    y_copied, y_ready, y_added = (tw.counter(x) for x in ("x_ycopied", "x_yready", "x_yadded"))
    Y = 6
    w1, w2 = tw.early["l0_w1"], tw.early["l0_w2"]
    with ExitStack() as ctx:
        sg = tw.sb("x0_sg", [P, 2, BANK], ctx=ctx)
        gt = tw.sb("x0_gt", [P, 2, BANK], ctx=ctx)
        hid = tw.sb("x0_hid", [P, 2, BANK], ctx=ctx)
        yt = tw.sb("x0_yt", [P, 2, BANK], ctx=ctx)
        raws = [tw.sb(f"later_raw{n}", [P, src.shape[1]], ctx=ctx) for n, (src, _, _) in enumerate(later)]
        block = ctx.enter_context(nc.Block())

        @block.sync
        def _(sp):
            for raw, (src, _, _) in zip(raws, later):
                for half in range(2):
                    sp.dma_start(raw[64 * half:64 * half + 64, :], src).then_inc(tw.later_landed, 16)

        @block.gpsimd
        def _(pool):
            pool.wait_ge(tw.later_landed, 32 * len(later))
            for n, (raw, (_, hi, lo)) in enumerate(zip(raws, later)):
                pool.tensor_scalar(hi[:, :], raw[:, :], 1.0, 1.0, ALU.mult, ALU.mult).then_inc(tw.later_hi, 1)
                pool.wait_ge(tw.later_hi, n + 1)
                pool.tensor_tensor(lo[:, :], raw[:, :], hi[:, :].bitcast(F32), ALU.subtract)

        @block.tensor
        def _(pe):
            for i in range(U + 4):
                if i < U:
                    t, e = i // E0, i % E0
                    if i >= 2:
                        pe.wait_ge(hid_ready.sem, hid_ready(i - 1))
                    cols = slice(t * BANK, (t + 1) * BANK)
                    for k, w in ((0, w1), (2, w2)):
                        for n, part in enumerate((tw.early_hi, tw.early_lo)):
                            nc.tensor.matmul(ps[:, k + i % 2, :], part[:, w.start + e * H0:w.start + e * H0 + H0],
                                             tw.xt[:, cols], start=(n == 0), stop=(n == 1))
                    nc.tensor.matmul(ps[:, 4 + i % 2, :], tw.sel128[:, e, :], tw.ct[:, cols],
                                     start=True, stop=True).then_inc(up.sem, 1)
                u = i - 2
                if 0 <= u < U:
                    t, e = u // E0, u % E0
                    pe.wait_ge(hid_ready.sem, hid_ready(u + 1))
                    if e == 0 and t >= 2:
                        pe.wait_ge(y_added.sem, y_added(t - 1))
                    half = 64 * (e % 2)
                    nc.tensor.matmul(ps[half:half + 64, Y + t % 2, :], tw.w("l0_w3")[:, e * D:(e + 1) * D],
                                     hid[:, u % 2, :], start=(e < 2), stop=(e >= E0 - 2)).then_inc(down.sem, 1)
                t = (i - 3) // E0 - 1
                if (i - 3) % E0 == 0 and 0 <= t < G:
                    pe.wait_ge(y_copied.sem, y_copied(t + 1))
                    for k in range(TPG):
                        mm = nc.tensor.matmul(ps[:, Y + t % 2, k * D:(k + 1) * D], yt[:, t % 2, k * P:(k + 1) * P],
                                              tw.w("fold"), start=True, stop=True)
                    mm.then_inc(y_ready.sem, 1)

        @block.scalar
        def _(act):
            for i in range(U + 4):
                if i < U:
                    act.wait_ge(up.sem, up(i + 1))
                    if i >= 2:
                        act.wait_ge(gated.sem, gated(i - 1))
                    nc.scalar.activation(sg[:, i % 2, :], ps[:, i % 2, :], ACT.Silu).then_inc(silu.sem, 1)
                t = (i - 2) // E0 - 1
                if (i - 2) % E0 == 0 and 0 <= t < G:
                    act.wait_ge(down.sem, down(E0 * (t + 1)))
                    nc.scalar.copy(yt[:, t % 2, :], ps[:, Y + t % 2, :]).then_inc(y_copied.sem, 1)

        @block.vector
        def _(dve):
            for i in range(U + 4):
                if i < U:
                    dve.wait_ge(silu.sem, silu(i + 1))
                    nc.vector.tensor_tensor(gt[:, i % 2, :], sg[:, i % 2, :], ps[:, 2 + i % 2, :], ALU.mult)\
                        .then_inc(gated.sem, 1)
                    dve.wait_ge(gated.sem, gated(i + 1))
                    if i >= 2:
                        dve.wait_ge(down.sem, down(i - 1))
                    nc.vector.tensor_tensor(hid[:, i % 2, :], gt[:, i % 2, :], ps[:, 4 + i % 2, :], ALU.mult)\
                        .then_inc(hid_ready.sem, 1)
                t = (i - 3) // E0 - 1
                if (i - 3) % E0 == 0 and 0 <= t < G:
                    dve.wait_ge(y_ready.sem, y_ready(t + 1))
                    rows = h[:, TPG * t:TPG * t + TPG, :]
                    nc.vector.tensor_tensor(rows, rows, ps[:, Y + t % 2, 0:TPG * D].rearrange("p (k d) -> p k d", d=D),
                                            ALU.add).then_inc(y_added.sem, 1)
    for s in (up, silu, gated, hid_ready, down):
        s.passed(U)
    for s in (y_copied, y_ready, y_added):
        s.passed(G)


def pair_experts_stage(tw, h, pairs, w1, b1, func, mid, w3, b3, extra, shared=None):
    nc, ps = tw.nc, tw.ps
    NS = pairs + (1 if shared else 0)
    U = G * NS
    up, act1, mid_ready, act2, hid_ready, down = (
        tw.counter(x) for x in ("xp_up", "xp_act1", "xp_mid", "xp_act2", "xp_hidden", "xp_down"))
    y_copied, y_ready, y_added, y_kept = (tw.counter(x) for x in ("x_ycopied", "x_yready", "x_yadded", "xp_kept"))
    Y = 6
    with ExitStack() as ctx:
        a1 = tw.sb("xp_a1", [P, 2, 2, BANK], ctx=ctx)
        a2 = tw.sb("xp_a2", [P, 2, BANK], ctx=ctx)
        hid = tw.sb("xp_hid", [P, 2, BANK], ctx=ctx)
        yt = tw.sb("xp_yt", [P, 2, BANK], ctx=ctx)
        block = ctx.enter_context(nc.Block())

        def is_shared(u):
            return u % NS == pairs

        def ups(u):
            if is_shared(u):
                return [shared["w1"]]
            w = w1(u % NS)
            return w if isinstance(w, list) else [w]

        @block.tensor
        def _(pe):
            for i in range(U + 4):
                if i < U:
                    t = i // NS
                    cols = slice(t * BANK, (t + 1) * BANK)
                    if i >= 2:
                        pe.wait_ge(hid_ready.sem, hid_ready(i - 1))
                    for k, (hi, lo) in enumerate(ups(i)):
                        mm = nc.tensor.matmul(ps[:, 2 * (i % 2) + k, :], hi, tw.xt[:, cols], start=True, stop=False)
                        mm = nc.tensor.matmul(ps[:, 2 * (i % 2) + k, :], lo, tw.xt[:, cols], start=False, stop=True)
                    mm.then_inc(up.sem, 1)
                u = i - 1
                if mid is not None and 0 <= u < U:
                    pe.wait_ge(act1.sem, act1(u + 1))
                    bank = 2 * (u % 2)
                    if is_shared(u):
                        mm = nc.tensor.matmul(ps[:, bank, :], shared["w2"], a1[:, u % 2, 0, :], start=True, stop=True)
                    else:
                        ms = mid[0](u % NS)
                        if isinstance(ms, list):
                            for k, m in enumerate(ms):
                                mm = nc.tensor.matmul(ps[64 * k:64 * k + 64, bank, :], m, a1[:, u % 2, k, :],
                                                      start=True, stop=True)
                        else:
                            mm = nc.tensor.matmul(ps[:, bank, :], ms, a1[:, u % 2, 0, :], start=True, stop=True)
                    mm.then_inc(mid_ready.sem, 1)
                if 0 <= u < U and not is_shared(u):
                    t, q = u // NS, u % NS
                    cols = slice(t * BANK, (t + 1) * BANK)
                    if u >= 2:
                        pe.wait_ge(hid_ready.sem, hid_ready(u - 1))
                    nc.tensor.matmul(ps[:, 4 + u % 2, :], tw.sel64[:, 2 * q:2 * q + 2, :].rearrange("p a b -> p (a b)"),
                                     tw.ct[:, cols], start=True, stop=True).then_inc(tw.spread_ready.sem, 1)
                u = i - 2
                if 0 <= u < U:
                    t, q = u // NS, u % NS
                    pe.wait_ge(hid_ready.sem, hid_ready(u + 1))
                    if q == 0 and t >= 2:
                        pe.wait_ge(y_added.sem, y_added(t - 1))
                    half = 64 * (q % 2)
                    w = shared["w3"] if is_shared(u) else w3(q)
                    nc.tensor.matmul(ps[half:half + 64, Y + t % 2, :], w, hid[:, u % 2, :],
                                     start=(q < 2), stop=(q >= NS - 2)).then_inc(down.sem, 1)
                t = (i - 3) // NS - 1
                if (i - 3) % NS == 0 and 0 <= t < G:
                    pe.wait_ge(y_copied.sem, y_copied(t + 1))
                    for k in range(TPG):
                        dst = ps[:, Y + t % 2, k * D:(k + 1) * D]
                        nc.tensor.matmul(dst, yt[:, t % 2, k * P:(k + 1) * P], tw.w("fold"), start=True, stop=False)
                        c = t * BANK + k * P
                        mm = nc.tensor.matmul(dst, tw.ct[:, c:c + P].bitcast(F32), b3, start=False, stop=True)
                    mm.then_inc(y_ready.sem, 1)

        routed_to = [sum(not is_shared(v) for v in range(u + 1)) for u in range(U)]

        @block.scalar
        def _(act):
            for i in range(U + 4):
                if i < U:
                    act.wait_ge(up.sem, up(i + 1))
                    if i >= 2:
                        if mid is None:
                            act.wait_ge(hid_ready.sem, hid_ready(i - 1))
                        else:
                            act.wait_ge(mid_ready.sem, mid_ready(i - 1))
                    bs = [shared["b1"]] if is_shared(i) else b1(i % NS)
                    for k, b in enumerate(bs):
                        ins = nc.scalar.activation(a1[:, i % 2, k, :], ps[:, 2 * (i % 2) + k, :], func, bias=b)
                    ins.then_inc(act1.sem, 1)
                u = i - 1
                if mid is not None and 0 <= u < U and not is_shared(u):
                    act.wait_ge(mid_ready.sem, mid_ready(u + 1))
                    if u >= 2:
                        act.wait_ge(hid_ready.sem, hid_ready(u - 1))
                    nc.scalar.activation(a2[:, u % 2, :], ps[:, 2 * (u % 2), :], ACT.Relu, bias=mid[1](u % NS))\
                        .then_inc(act2.sem, 1)
                t = (i - 2) // NS - 1
                if (i - 2) % NS == 0 and 0 <= t < G:
                    act.wait_ge(down.sem, down(NS * (t + 1)))
                    nc.scalar.copy(yt[:, t % 2, :], ps[:, Y + t % 2, :]).then_inc(y_copied.sem, 1)

        @block.vector
        def _(dve):
            for i in range(U + 5):
                u = i - 1
                if 0 <= u < U:
                    if u >= 2:
                        dve.wait_ge(down.sem, down(u - 1))
                    if is_shared(u):
                        dve.wait_ge(mid_ready.sem, mid_ready(u + 1))
                        nc.vector.tensor_scalar(hid[:, u % 2, :], ps[:, 2 * (u % 2), :], shared["b2"], 0.0, ALU.add,
                                                ALU.max).then_inc(hid_ready.sem, 1)
                    else:
                        if mid is None:
                            dve.wait_ge(act1.sem, act1(u + 1))
                        else:
                            dve.wait_ge(act2.sem, act2(routed_to[u]))
                        dve.wait_ge(tw.spread_ready.sem, tw.spread_ready(routed_to[u]))
                        source = a1[:, u % 2, 0, :] if mid is None else a2[:, u % 2, :]
                        nc.vector.tensor_tensor(hid[:, u % 2, :], source, ps[:, 4 + u % 2, :], ALU.mult)\
                            .then_inc(hid_ready.sem, 1)
                t = (i - 4) // NS - 1
                if (i - 4) % NS == 0 and 0 <= t < G:
                    rows = h[:, TPG * t:TPG * t + TPG, :]
                    if extra is not None:
                        nc.vector.tensor_tensor(rows, rows, extra(t), ALU.add).then_inc(y_kept.sem, 1)
                        dve.wait_ge(y_kept.sem, y_kept(t + 1))
                    dve.wait_ge(y_ready.sem, y_ready(t + 1))
                    nc.vector.tensor_tensor(rows, rows, ps[:, Y + t % 2, 0:TPG * D].rearrange("p (k d) -> p k d", d=D),
                                            ALU.add).then_inc(y_added.sem, 1)
    for s in (up, act1, hid_ready, down):
        s.passed(U)
    if mid is not None:
        mid_ready.passed(U)
        act2.passed(G * pairs)
    tw.spread_ready.passed(G * pairs)
    for s in (y_copied, y_ready, y_added):
        s.passed(G)
    if extra is not None:
        y_kept.passed(G)




def linear_attention_stage(tw, x, layer):
    nc, ps = tw.nc, tw.ps
    DH = D // HEADS2
    scale = float(DH) ** -0.25
    kp, qp, kmax, kneg, ek, ekt, ekc = (tw.counter(x) for x in (
        "la_keys", "la_qv", "la_kmax", "la_kneg", "la_ek", "la_ekt", "la_ekc"))
    vc, qm, qd, qe, qs, qi, qn = (tw.counter(x) for x in (
        "la_vc", "la_qmax", "la_qdiff", "la_qexp", "la_qsum", "la_qinv", "la_qn"))
    ctx_ready, ctx_masked, cw_ready, cw_scaled, kinv, qt, qtc, y, yb = (tw.counter(x) for x in (
        "la_ctx", "la_masked", "la_cw", "la_cws", "la_kinv", "la_qt", "la_qtc", "la_y", "la_yb"))
    k_hi, k_lo = tw.mid_hi[:, tw.mid[f"l2_k{layer}"]], tw.mid_lo[:, tw.mid[f"l2_k{layer}"]]
    qv = [p[:, tw.mid[f"l2_qv{layer}"]] for p in (tw.mid_hi, tw.mid_lo)]
    HT = NTB // 2
    with ExitStack() as ctx:
        sb = lambda name, shape: tw.sb("la_" + name, shape, ctx=ctx)
        eks = sb("ek", [P, N])
        ekts = sb("ekt", [P, NTB, P])
        vs = sb("v", [P, NTB, B, D])
        qc = sb("qc", [P, NT, D])
        qexp = sb("qexp", [P, NT, D])
        qns = sb("qn", [P, NTB, B, D])
        qts = sb("qt", [P, N])
        qmx = sb("qmx", [P, NT * HEADS2])
        qsm = sb("qsm", [P, NT * HEADS2])
        qiv = sb("qiv", [P, NT * HEADS2])
        km = sb("km", [P, 2])
        ks = sb("ks", [P, 2])
        cms = sb("cm", [P, P])
        block = ctx.enter_context(nc.Block())

        @block.tensor
        def _(pe):
            for g in range(G):
                nc.tensor.matmul(ps[:, g, :], k_hi, tw.xt[:, g * BANK:(g + 1) * BANK], start=True, stop=False)
                nc.tensor.matmul(ps[:, g, :], k_lo, tw.xt[:, g * BANK:(g + 1) * BANK], start=False, stop=True)\
                    .then_inc(kp.sem, 1)
            for g in range(G):
                for k in range(TPG):
                    t = TPG * g + k
                    for n, part in enumerate(qv):
                        mm = nc.tensor.matmul(ps[:, 4 + g, k * P:(k + 1) * P], tw.xt[:, t * P:(t + 1) * P], part,
                                              start=(n == 0), stop=(n == 1))
                mm.then_inc(qp.sem, 1)
            pe.wait_ge(ek.sem, ek(2))
            for c in range(2):
                for k in range(HT):
                    i = HT * c + k
                    mm = nc.tensor.transpose(ps[:, c, k * P:(k + 1) * P], eks[:, i * P:(i + 1) * P], tw.w("ident"))
                mm.then_inc(ekt.sem, 1)
            pe.wait_ge(ekc.sem, ekc(2))
            pe.wait_ge(vc.sem, vc(G))
            for i in range(NTB):
                mm = nc.tensor.matmul(ps[:, 2, 0:P], vs[:, i, :, :].rearrange("p b d -> p (b d)"), ekts[:, i, :],
                                      start=(i == 0), stop=(i == NTB - 1))
            mm.then_inc(ctx_ready.sem, 1)
            pe.wait_ge(qn.sem, qn(G))
            for c in range(2):
                for k in range(HT):
                    i = HT * c + k
                    mm = nc.tensor.transpose(ps[:, 4 + c, k * P:(k + 1) * P],
                                             qns[:, i, :, :].rearrange("p b d -> p (b d)"), tw.w("ident"))
                mm.then_inc(qt.sem, 1)
            pe.wait_ge(ctx_masked.sem, ctx_masked(1))
            nc.tensor.matmul(ps[:, 3, 0:D], cms[:, :], tw.w(f"l2_wo{layer}"), start=True, stop=True)\
                .then_inc(cw_ready.sem, 1)
            pe.wait_ge(cw_scaled.sem, cw_scaled(2))
            for c in range(2):
                pe.wait_ge(qtc.sem, qtc(c + 1))
                for k in range(HT):
                    i = HT * c + k
                    mm = nc.tensor.matmul(ps[:, 6 + c, k * P:(k + 1) * P], qts[:, i * P:(i + 1) * P], tw.cw_block[:, :],
                                          start=True, stop=True)
                mm.then_inc(y.sem, 1)

        @block.vector
        def _(dve):
            for b in range(B):
                r = slice(64 * b, 64 * b + 64)
                dve.wait_ge(kp.sem, kp(2 * b + 2))
                nc.vector.tensor_reduce(km[r, 0:1], ps[r, 2 * b:2 * b + 2, :], AX.XY, ALU.max, negate=True)\
                    .then_inc(kmax.sem, 1)
            dve.wait_ge(kmax.sem, kmax(2))
            nc.vector.tensor_scalar(km[:, 1:2], km[:, 0:1], scale, None, ALU.mult).then_inc(kneg.sem, 1)
            for g in range(G):
                dve.wait_ge(qp.sem, qp(g + 1))
                heads = slice(TPG * HEADS2 * g, TPG * HEADS2 * (g + 1))
                q = ps[:, 4 + g, :].rearrange("p (k c d) -> p k c d", k=TPG, c=2)[:, :, 0, :]
                q4 = q.rearrange("p k (h d) -> p k h d", d=DH)
                nc.vector.reduce_max(qmx[:, heads].rearrange("p (k h) -> p k h", k=TPG), q4, AX.X).then_inc(qm.sem, 1)
                dve.wait_ge(qm.sem, qm(g + 1))
                mx = qmx[:, heads].rearrange("p (k h) -> p k h", k=TPG).unsqueeze(3).to_broadcast([P, TPG, HEADS2, DH])
                nc.vector.tensor_tensor(qc[:, TPG * g:TPG * g + TPG, :].rearrange("p k (h d) -> p k h d", d=DH), q4, mx,
                                        ALU.subtract).then_inc(qd.sem, 1)
            for c in range(2):
                dve.wait_ge(ekt.sem, ekt(c + 1))
                nc.vector.tensor_copy(ekts[:, HT * c:HT * c + HT, :].rearrange("p k c -> p (k c)"), ps[:, c, :])\
                    .then_inc(ekc.sem, 1)
            for g in range(G):
                heads = slice(TPG * HEADS2 * g, TPG * HEADS2 * (g + 1))
                dve.wait_ge(qe.sem, qe(g + 1))
                e = qexp[:, TPG * g:TPG * g + TPG, :].rearrange("p k (h d) -> p (k h) d", d=DH)
                nc.vector.reduce_sum(qsm[:, heads], e, AX.X).then_inc(qs.sem, 1)
                dve.wait_ge(qs.sem, qs(g + 1))
                nc.vector.reciprocal(qiv[:, heads], qsm[:, heads]).then_inc(qi.sem, 1)
                dve.wait_ge(qi.sem, qi(g + 1))
                b, i0 = TPG * g // NTB, TPG * g % NTB
                dst = qns[:, i0:i0 + TPG, b, :].rearrange("p k (h d) -> p k h d", d=DH)
                iv = qiv[:, heads].rearrange("p (k h) -> p k h", k=TPG).unsqueeze(3).to_broadcast([P, TPG, HEADS2, DH])
                nc.vector.tensor_tensor(dst, qexp[:, TPG * g:TPG * g + TPG, :].rearrange("p k (h d) -> p k h d", d=DH),
                                        iv, ALU.mult).then_inc(qn.sem, 1)
            dve.wait_ge(ek.sem, ek(2))
            nc.vector.reciprocal(ks[:, 1:2], ks[:, 0:1]).then_inc(kinv.sem, 1)
            dve.wait_ge(ctx_ready.sem, ctx_ready(1))
            nc.vector.tensor_tensor(cms[:, :], ps[:, 2, 0:P], tw.w("head_mask"), ALU.mult).then_inc(ctx_masked.sem, 1)
            dve.wait_ge(kinv.sem, kinv(1))
            dve.wait_ge(cw_ready.sem, cw_ready(1))
            for b in range(B):
                r = slice(64 * b, 64 * b + 64)
                nc.vector.tensor_scalar(tw.cw_block[r, 64 * b:64 * b + 64], ps[r, 3, 0:D], ks[r, 1:2], None, ALU.mult)\
                    .then_inc(cw_scaled.sem, 1)
            for c in range(2):
                dve.wait_ge(y.sem, y(c + 1))
                dve.wait_ge(yb.sem, yb(1))
                for b in range(B):
                    rows = x[:, NTB * b + HT * c:NTB * b + HT * c + HT, :]
                    src = ps[:, 6 + c, :].rearrange("p (k b d) -> p k b d", k=HT, b=B)[:, :, b, :]
                    nc.vector.tensor_tensor(rows, rows, src, ALU.add)

        @block.scalar
        def _(act):
            act.wait_ge(kneg.sem, kneg(1))
            for b in range(B):
                r = slice(64 * b, 64 * b + 64)
                nc.scalar.activation(eks[r, :], ps[r, 2 * b:2 * b + 2, :].rearrange("p a b -> p (a b)"), ACT.Exp,
                                     bias=km[r, 1:2], scale=scale, accum_out=ks[r, 0:1]).then_inc(ek.sem, 1)
            for g in range(G):
                act.wait_ge(qd.sem, qd(g + 1))
                b, i0 = TPG * g // NTB, TPG * g % NTB
                v = ps[:, 4 + g, :].rearrange("p (k c d) -> p k c d", k=TPG, c=2)[:, :, 1, :]
                nc.scalar.copy(vs[:, i0:i0 + TPG, b, :], v).then_inc(vc.sem, 1)
                nc.scalar.activation(qexp[:, TPG * g:TPG * g + TPG, :], qc[:, TPG * g:TPG * g + TPG, :], ACT.Exp,
                                     scale=scale).then_inc(qe.sem, 1)
            for c in range(2):
                act.wait_ge(qt.sem, qt(c + 1))
                nc.scalar.copy(qts[:, c * BANK:(c + 1) * BANK], ps[:, 4 + c, :]).then_inc(qtc.sem, 1)

        @block.gpsimd
        def _(pool):
            pool.tensor_tensor(x[:, :, :], x[:, :, :], rows_over(tw.r(f"l2_bo{layer}"), NT), ALU.add)\
                .then_inc(yb.sem, 1)
    for s, n in ((kp, G), (qp, G), (kmax, 2), (kneg, 1), (ek, 2), (ekt, 2), (ekc, 2), (vc, G), (qm, G), (qd, G), (qe, G),
                 (qs, G), (qi, G), (qn, G), (ctx_ready, 1), (ctx_masked, 1), (cw_ready, 1), (cw_scaled, 2), (kinv, 1),
                 (qt, 2), (qtc, 2), (y, 2), (yb, 1)):
        s.passed(n)


def gelu_mlp_stage(tw, x, layer):
    nc, ps = tw.nc, tw.ps
    U = 2 * G
    up, gelu, y, yb, added = (tw.counter(s) for s in ("ml_up", "ml_gelu", "ml_y", "ml_yb", "ml_added"))
    w1 = tw.mid[f"l2_w1{layer}"]
    b1, w2 = tw.w(f"l2_b1{layer}"), tw.w(f"l2_w2{layer}")
    with ExitStack() as ctx:
        hid = tw.sb("ml_hid", [P, U, BANK], ctx=ctx)
        block = ctx.enter_context(nc.Block())

        @block.tensor
        def _(pe):
            for i in range(U + 3):
                if i < U:
                    t, c = i // 2, i % 2
                    if i >= 4:
                        pe.wait_ge(gelu.sem, gelu(i - 3))
                    for n, part in enumerate((tw.mid_hi, tw.mid_lo)):
                        mm = nc.tensor.matmul(ps[:, i % 4, :], part[:, w1.start + c * P:w1.start + (c + 1) * P],
                                              tw.xt[:, t * BANK:(t + 1) * BANK], start=(n == 0), stop=(n == 1))
                    mm.then_inc(up.sem, 1)
                t = (i - 4) // 2
                if i >= 4 and i % 2 == 0:
                    pe.wait_ge(gelu.sem, gelu(2 * t + 2))
                    for k in range(TPG):
                        for c in range(2):
                            mm = nc.tensor.matmul(ps[:, 4 + t, k * D:(k + 1) * D], hid[:, 2 * t + c, k * P:(k + 1) * P],
                                                  w2[:, c * D:(c + 1) * D], start=(c == 0), stop=(c == 1))
                    mm.then_inc(y.sem, 1)

        @block.scalar
        def _(act):
            for i in range(U):
                act.wait_ge(up.sem, up(i + 1))
                nc.scalar.activation(hid[:, i, :], ps[:, i % 4, :], ACT.Gelu, bias=b1[:, i % 2:i % 2 + 1])\
                    .then_inc(gelu.sem, 1)

        @block.gpsimd
        def _(pool):
            pool.tensor_tensor(x[:, :, :], x[:, :, :], rows_over(tw.r(f"l2_b2{layer}"), NT), ALU.add)\
                .then_inc(yb.sem, 1)

        @block.vector
        def _(dve):
            dve.wait_ge(yb.sem, yb(1))
            for t in range(G):
                dve.wait_ge(y.sem, y(t + 1))
                rows = x[:, TPG * t:TPG * t + TPG, :]
                nc.vector.tensor_tensor(rows, rows, ps[:, 4 + t, 0:TPG * D].rearrange("p (k d) -> p k d", d=D), ALU.add)
    for s, n in ((up, U), (gelu, U), (y, G), (yb, 1)):
        s.passed(n)




def relu_stage(tw, hi, lo, bias, dst):
    nc, ps = tw.nc, tw.ps
    made = tw.counter("re_made")
    with ExitStack() as ctx:
        block = ctx.enter_context(nc.Block())

        @block.tensor
        def _(pe):
            for g in range(G):
                cols = slice(g * BANK, (g + 1) * BANK)
                nc.tensor.matmul(ps[:, g, :], hi, tw.xt[:, cols], start=True, stop=False)
                nc.tensor.matmul(ps[:, g, :], lo, tw.xt[:, cols], start=False, stop=True).then_inc(made.sem, 1)

        @block.scalar
        def _(act):
            for g in range(G):
                act.wait_ge(made.sem, made(g + 1))
                nc.scalar.activation(dst[:, g * BANK:(g + 1) * BANK], ps[:, g, :], ACT.Relu, bias=bias)
    made.passed(G)


def scale_shift_stage(tw, x, scale, shift):
    nc = tw.nc
    with nc.Block() as block:
        @block.vector
        def _(dve):
            nc.vector.scalar_tensor_tensor(out=x[:, :, :], in0=x[:, :, :], scalar=scale, in1=rows_over(shift, NT),
                                           op0=ALU.mult, op1=ALU.add)


def add_stage(tw, x, y):
    nc = tw.nc
    with nc.Block() as block:
        @block.vector
        def _(dve):
            nc.vector.tensor_tensor(x[:, :, :], x[:, :, :], y, ALU.add)


def score_matrices_stage(tw, qk, a_hi, a_lo):
    nc, ps = tw.nc, tw.ps
    landed, made, hi_made = (tw.counter(x) for x in ("sm_landed", "sm_made", "sm_hi"))
    with ExitStack() as ctx:
        w = tw.sb("sm_qk", [P, 2, HEADS // 2, P], ctx=ctx)
        block = ctx.enter_context(nc.Block())

        @block.sync
        def _(sp):
            sp.dma_start(w[:, :, :, :].rearrange("p a b c -> p (a b c)"), qk).then_inc(landed.sem, 16)

        @block.tensor
        def _(pe):
            pe.wait_ge(landed.sem, landed(16))
            for hd in range(HEADS):
                r = slice(64 * (hd % 2), 64 * (hd % 2) + 64)
                mm = nc.tensor.matmul(ps[:, hd, 0:P], w[r, 0, hd // 2, :], w[r, 1, hd // 2, :], start=True, stop=True)
                mm.then_inc(made.sem, 1)

        @block.scalar
        def _(act):
            act.wait_ge(made.sem, made(HEADS))
            nc.scalar.copy(a_hi[:, :, :], ps[:, :, 0:P]).then_inc(hi_made.sem, 1)

        @block.vector
        def _(dve):
            dve.wait_ge(hi_made.sem, hi_made(1))
            nc.vector.tensor_tensor(a_lo[:, :, :], ps[:, :, 0:P], a_hi[:, :, :].bitcast(F32), ALU.subtract)
    landed.passed(16)
    made.passed(HEADS)
    hi_made.passed(1)


def constants_stage(tw, selectors, width):
    nc = tw.nc
    with nc.Block() as block:
        @block.vector
        def _(dve):
            dve.wait_ge(tw.full_landed, 16)
            nc.vector.tensor_copy(selectors[:, :, :], wide(tw.w("expert_rows")[:, 0:selectors.shape[1]], width))


def vit_tower_kernel(nc, x, dft, wk, early, mid, late, full, row, toeplitz, qk, out, upto=99):
    with ExitStack() as ctx:
        tw = Tower(nc, ctx)
        tw.ps = ctx.enter_context(nc.psum_tensor("ps", [P, 8, BANK], F32))
        h = tw.h = tw.sb("h", [P, NT, D])
        tw.xt = tw.sb("xt", [P, T], F32R)
        tw.w_full = tw.sb("w_full", [P, tw.full.n])
        tw.w_row = tw.sb("w_row", [P, tw.row.n])
        tw.minus_half = tw.sb("minus_half", [P, NT])
        tw.late_hi = tw.sb("late_hi", [P, tw.late.n], F32R)
        tw.late_lo = tw.sb("late_lo", [P, tw.late.n], F32R)
        tw.early_landed, tw.full_landed, tw.row_landed, tw.later_landed, tw.later_hi, tw.strips_landed, tw.out_landed = (
            nc.alloc_semaphore(name) for name in ("early_landed", "full_landed", "row_landed", "later_landed",
                                                  "later_hi", "strips_landed", "out_landed"))
        tw.spread_ready = tw.counter("xp_spread")

        def xt_tile(t):
            return tw.xt[:, t * P:(t + 1) * P]

        def parts(pack, lay, name):
            hi, lo = pack
            return hi[:, lay[name]], lo[:, lay[name]]

        mids = ctx.enter_context(ExitStack())
        tw.xn = tw.sb("xn", [P, NT, D], ctx=mids)
        tw.mid_hi = tw.sb("mid_hi", [P, tw.mid.n], F32R, ctx=mids)
        tw.mid_lo = tw.sb("mid_lo", [P, tw.mid.n], F32R, ctx=mids)
        MID, LATE = (tw.mid_hi, tw.mid_lo), (tw.late_hi, tw.late_lo)

        with ExitStack() as l0:
            tw.early_hi = tw.sb("early_hi", [P, tw.early.n], F32R, ctx=l0)
            tw.early_lo = tw.sb("early_lo", [P, tw.early.n], F32R, ctx=l0)
            EARLY = (tw.early_hi, tw.early_lo)
            embed_stage(tw, x, dft, wk, early, full, row)
            if upto >= 1:
                norm_stage(tw, h, keep=tw.xn)
                with ExitStack() as at:
                    qh = tw.sb("a0_qh", [P, T], F32R, ctx=at)
                    ql = tw.sb("a0_ql", [P, T], F32R, ctx=at)
                    wh, wl = parts(EARLY, tw.early, "l0_attn")
                    project_stage(tw, [(wh, wl, g * BANK, None, "queries",
                                        (qh[:, g * BANK:(g + 1) * BANK], ql[:, g * BANK:(g + 1) * BANK]))
                                       for g in range(G)])
                    groups = [((0, 1), [b * N + nh * BANK for b in range(B)], [b * N for b in range(B)], 4 * nh)
                              for nh in range(2)]
                    attention_stage(tw, "a0", groups, 1.0 / 8.0, lambda m: qh, lambda m: ql, tw.xt,
                                    lambda m, w: tw.xn[:, NTB * m + w, :], lambda g: tw.w("ident"), None, "add",
                                    lambda g, j: h[:, NTB * j + 4 * g:NTB * j + 4 * g + 4, :])
            if upto >= 2:
                norm_stage(tw, h)
                tw.ct = tw.sb("ct0", [P, T], F32R, ctx=l0)
                tw.sel128 = tw.sb("sel128", [P, E0, H0], F32R, ctx=l0)
                constants_stage(tw, tw.sel128, H0)
                route_stage(tw, E0, xt_tile, parts(EARLY, tw.early, "l0_gate"), tw.r("l0_gate_b"), False)
                swiglu_experts_stage(tw, h, [(mid, tw.mid_hi, tw.mid_lo), (late, tw.late_hi, tw.late_lo)])

        if upto >= 3:
            with ExitStack() as l1:
                strips = tw.sb("bias_strips", [P, 3, 7 * P], ctx=l1)
                load_strips_stage(tw, toeplitz, strips)
                norm_stage(tw, h, keep=tw.xn, turn=False)
                norm_stage(tw, tw.xn, tw.r("l1_ln1_g"), tw.r("l1_ln1_b"), keep=tw.xn)
                qh = tw.sb("a1_qh", [P, T], F32R, ctx=l1)
                ql = tw.sb("a1_ql", [P, T], F32R, ctx=l1)
                kk = tw.sb("a1_k", [P, T], F32R, ctx=l1)
                vt = tw.sb("a1_v", [P, NT, D], ctx=l1)
                ob = tw.sb("a1_out", [P, NT, D], ctx=l1)
                jobs = []
                for g in range(G):
                    cols = slice(g * BANK, (g + 1) * BANK)
                    jobs.append((*parts(MID, tw.mid, "l1_q"), g * BANK, tw.w("l1_qb"), "queries",
                                 (qh[:, cols], ql[:, cols])))
                    jobs.append((*parts(MID, tw.mid, "l1_k"), g * BANK, tw.w("l1_kb"), "keys", (kk[:, cols],)))
                project_stage(tw, jobs)
                value_stage(tw, *parts(MID, tw.mid, "l1_v"), D, range(NT), lambda t: vt[:, t, :], tw.r("l1_vb"))
                groups = [((0, 1), [b * N + nh * BANK for b in range(B)], [b * N for b in range(B)], 4 * nh)
                          for nh in range(2)]
                attention_stage(tw, "a1", groups, 1.0, lambda m: qh, lambda m: ql, kk,
                                lambda m, w: vt[:, NTB * m + w, :], lambda g: tw.w("l1_post"), strips, "store",
                                lambda g, j: ob[:, NTB * j + 4 * g:NTB * j + 4 * g + 4, :])
                scale_shift_stage(tw, ob, tw.r("l1_scale"), tw.r("l1_proj_b"))
                norm_stage(tw, ob, tw.r("l1_ln2_g"), tw.r("l1_ln2_b"), keep=ob, turn=False)
                add_stage(tw, h, ob[:, :, :])
        if upto >= 4:
            with ExitStack() as f1:
                tw.ct = tw.sb("ct1", [P, T], F32R, ctx=f1)
                tw.sel64 = tw.sb("sel64_1", [P, E1, D], F32R, ctx=f1)
                constants_stage(tw, tw.sel64, D)
                norm_stage(tw, h, keep=tw.xn)
                route_stage(tw, E1, xt_tile, parts(MID, tw.mid, "l1_gate"), None, False)
                w1 = tw.mid["l1_w1"].start
                pair_experts_stage(
                    tw, h, E1 // 2,
                    lambda q: tuple(p[:, w1 + q * P:w1 + (q + 1) * P] for p in MID),
                    lambda q: [tw.w("l1_b1")[:, q:q + 1]], ACT.Gelu, None,
                    lambda q: tw.w("l1_w2")[:, q * D:(q + 1) * D], tw.w("l1_b2"),
                    lambda t: tw.xn[:, TPG * t:TPG * t + TPG, :])

        if upto >= 5:
            with ExitStack() as l2:
                x2 = tw.sb("x2", [P, NT, D], ctx=l2)
                tw.cw_block = tw.sb("cw_block", [P, P], ctx=l2)
                clear_stage(tw, tw.cw_block)
                norm_stage(tw, h, keep=x2, turn=False)
                for layer in range(LAYERS):
                    norm_stage(tw, x2, tw.r(f"l2_ln1_g{layer}"), tw.r(f"l2_ln1_b{layer}"), keep=tw.xn)
                    linear_attention_stage(tw, x2, layer)
                    norm_stage(tw, x2, tw.r(f"l2_ln2_g{layer}"), tw.r(f"l2_ln2_b{layer}"), keep=tw.xn)
                    gelu_mlp_stage(tw, x2, layer)
                add_stage(tw, h, x2[:, :, :])
        if upto >= 6:
            with ExitStack() as f2:
                tw.ct = tw.sb("ct2", [P, T], F32R, ctx=f2)
                tw.sel64 = tw.sb("sel64_2", [P, E2, D], F32R, ctx=f2)
                rh = tw.sb("router_hidden", [P, T], ctx=f2)
                constants_stage(tw, tw.sel64, D)
                norm_stage(tw, h)
                relu_stage(tw, *parts(MID, tw.mid, "l2_router"), tw.w("l2_rb1"), rh)
                route_stage(tw, E2, lambda t: rh[:, t * P:(t + 1) * P], [tw.w("l2_rw2")], tw.r("l2_rb2"), True)
                w1 = tw.mid["l2_e1"].start
                pair_experts_stage(
                    tw, h, E2 // 2,
                    lambda q: tuple(p[:, w1 + q * P:w1 + (q + 1) * P] for p in MID),
                    lambda q: [tw.w("l2_eb1")[:, q:q + 1]], ACT.Relu,
                    (lambda q: tw.w("l2_e2")[:, q * P:(q + 1) * P], lambda q: tw.w("l2_eb2")[:, q:q + 1]),
                    lambda q: tw.w("l2_e3")[:, q * D:(q + 1) * D], tw.w("l2_eb3"), None)
        mids.close()

        tw.xn = tw.sb("xn3", [P, NT, D]) if upto >= 7 else None
        if upto >= 7:
            norm_stage(tw, h)
            with ExitStack() as l3:
                a_hi = tw.sb("a3_hi", [P, HEADS, P], F32R, ctx=l3)
                a_lo = tw.sb("a3_lo", [P, HEADS, P], F32R, ctx=l3)
                score_matrices_stage(tw, qk, a_hi, a_lo)
                qh = tw.sb("a3_qh", [P, HEADS, BANK], F32R, ctx=l3)
                ql = tw.sb("a3_ql", [P, HEADS, BANK], F32R, ctx=l3)
                vt = tw.sb("a3_v", [P, NTB, HEADS * D], ctx=l3)
                for b in range(B):
                    value_stage(tw, *parts(LATE, tw.late, "l3_v"), HEADS * D, range(NTB * b, NTB * (b + 1)),
                                lambda t: vt[:, t % NTB, :])
                    for nh in range(2):
                        project_stage(tw, [(a_hi[:, m, :], a_lo[:, m, :], b * N + nh * BANK, None, "queries",
                                            (qh[:, m, :], ql[:, m, :])) for m in range(HEADS)])
                        groups = [((2 * k, 2 * k + 1), [0, 0], [b * N, b * N], 4 * nh) for k in range(HEADS // 2)]
                        attention_stage(tw, "a3", groups, float(1.0 / np.sqrt(D / HEADS).astype(np.float32)),
                                        lambda m: qh[:, m, :], lambda m: ql[:, m, :], tw.xt,
                                        lambda m, w: vt[:, w, m * D:(m + 1) * D],
                                        lambda g: tw.w("l3_post")[:, g * P:(g + 1) * P], None, "add",
                                        lambda g, j: h[:, NTB * b + 4 * nh:NTB * b + 4 * nh + 4, :])
            add_stage(tw, h, rows_over(tw.r("l3_bout"), NT))
        if upto >= 8:
            with ExitStack() as f3:
                tw.ct = tw.sb("ct3", [P, T], F32R, ctx=f3)
                tw.sel64 = tw.sb("sel64_3", [P, E3, D], F32R, ctx=f3)
                constants_stage(tw, tw.sel64, D)
                norm_stage(tw, h)
                route_stage(tw, E3, xt_tile, parts(LATE, tw.late, "l3_gate"), tw.r("l3_gate_b"), True)
                w1 = tw.late["l3_e1"].start
                pair_experts_stage(
                    tw, h, E3 // 2,
                    lambda q: [tuple(p[:, w1 + e * P:w1 + (e + 1) * P] for p in LATE) for e in (2 * q, 2 * q + 1)],
                    lambda q: [tw.w("l3_eb1")[:, e:e + 1] for e in (2 * q, 2 * q + 1)], ACT.Relu,
                    (lambda q: [tw.w("l3_e2")[:, e * D:(e + 1) * D] for e in (2 * q, 2 * q + 1)],
                     lambda q: tw.w("l3_eb2")[:, q:q + 1]),
                    lambda q: tw.w("l3_e3")[:, q * D:(q + 1) * D], tw.w("l3_eb3"),
                    lambda t: rows_over(tw.r("l3_sb3"), TPG),
                    shared=dict(w1=parts(LATE, tw.late, "l3_s1"), b1=tw.w("l3_sb1"), w2=tw.w("l3_s2"),
                                b2=tw.w("l3_sb2"), w3=tw.w("l3_s3")))
        store_stage(tw, h, out)


def load_strips_stage(tw, toeplitz, strips):
    nc = tw.nc
    with nc.Block() as block:
        @block.sync
        def _(sp):
            sp.dma_start(strips[:, :, :], toeplitz).then_inc(tw.strips_landed, 16)
            sp.wait_ge(tw.strips_landed, 16)


def clear_stage(tw, tile):
    with tw.nc.Block() as block:
        @block.vector
        def _(dve):
            tw.nc.vector.memset(tile[:, :], 0.0)


def store_stage(tw, h, out):
    with tw.nc.Block() as block:
        @block.sync
        def _(sp):
            for b in range(B):
                sp.dma_start(out[b].rearrange("(v p k) j -> p v (k j)", v=4, k=2),
                             h[:, NTB * b:NTB * (b + 1), :].rearrange("p (v k) j -> p v (k j)", k=2))\
                    .then_inc(tw.out_landed, 16)
            sp.wait_ge(tw.out_landed, 16 * B)




def twice(a):
    return np.concatenate([a, a], axis=-1)


def pad_to(a, rows, cols):
    out = np.zeros((rows, cols), a.dtype)
    out[:a.shape[0], :a.shape[1]] = a
    return out


def blocks_of(a, b):
    out = np.zeros((a.shape[0] + b.shape[0], a.shape[1] + b.shape[1]), a.dtype)
    out[:a.shape[0], :a.shape[1]] = a
    out[a.shape[0]:, a.shape[1]:] = b
    return out


def side_by_side(a):
    return np.concatenate(list(a), axis=1)


def stacked_pairs(a):
    return np.concatenate([np.concatenate([a[i], a[i + 1]], 0) for i in range(0, len(a), 2)], 1)


def pair_columns(a):
    return np.ascontiguousarray(a.reshape(len(a) // 2, 2 * D).T)


def by_expert(a):
    out = np.zeros((P, a.shape[1]), a.dtype)
    out[:len(a)] = a
    out[D:D + len(a)] = a
    return out


def pack(layout, parts, rows):
    f = np.zeros((rows, layout.n), np.float32)
    for name, a in parts.items():
        c = layout[name]
        assert a.shape == (rows, c.stop - c.start), (name, a.shape)
        f[:, c] = a
    assert set(parts) == set(layout.at)
    return f


def lay_out(i):
    k, t = np.arange(FREQ)[:, None], np.arange(PATCH)[None, :]
    nf = FREQ // 2
    dft = np.where(k < nf, np.cos(2 * np.pi * k * t / PATCH), -np.sin(2 * np.pi * (k - nf) * t / PATCH))
    arrays = {"x": i["x"], "dft": (dft / np.sqrt(PATCH)).astype(np.float32)}
    arrays["wk"] = i["L0_tok_W"].reshape(D, FREQ, C).transpose(1, 2, 0).reshape(FREQ, C * D)
    arrays["early"] = pack(split_layout_early(), {
        "l0_attn": twice(i["L0_attn_W"]), "l0_gate": i["L0_ffn_gate_w"],
        "l0_w1": side_by_side(i["L0_ffn_w1"]), "l0_w2": side_by_side(i["L0_ffn_w2"])}, D)
    qkv, qkvb = i["L1_attn_qkv_w"], i["L1_attn_qkv_b"]
    mid = {"l1_q": twice(qkv[:, 0:D]), "l1_k": twice(qkv[:, D:2 * D]), "l1_v": qkv[:, 2 * D:3 * D],
           "l1_gate": i["L1_ffn_router_w"].T, "l1_w1": side_by_side(i["L1_ffn_w1"]),
           "l2_router": pad_to(i["L2_ffn_router_w1"], D, P), "l2_e1": side_by_side(i["L2_ffn_expert_w1"])}
    for n in range(LAYERS):
        mid[f"l2_k{n}"] = twice(i["L2_attn_Wk"][n])
        mid[f"l2_qv{n}"] = np.concatenate([i["L2_attn_Wq"][n], i["L2_attn_Wv"][n]], 1)
        mid[f"l2_w1{n}"] = i["L2_attn_W1"][n]
    arrays["mid"] = pack(split_layout_mid(), mid, D)
    arrays["late"] = pack(split_layout_late(), {
        "l3_v": i["L3_attn_WV"], "l3_gate": i["L3_ffn_gW"], "l3_s1": pad_to(i["L3_ffn_sW1"], D, P),
        "l3_e1": side_by_side(i["L3_ffn_eW1"])}, D)
    eye = np.eye(P, dtype=np.float32)
    row, col = np.arange(P)[:, None], np.arange(P)[None, :]
    full = {"ident": eye, "fold": eye[:, :D] + eye[:, D:],
            "expert_rows": (row % D == np.arange(E0)[None, :]).astype(np.float32),
            "iota": np.broadcast_to(np.arange(16, dtype=np.float32), (P, 16)),
            "head_mask": (row // HEADS2 == col // HEADS2).astype(np.float32),
            "l0_w3": side_by_side(i["L0_ffn_w3"]),
            "l1_qb": twice(qkvb[0:D])[:, None], "l1_kb": twice(qkvb[D:2 * D])[:, None],
            "l1_post": blocks_of(i["L1_attn_proj_w"], i["L1_attn_proj_w"]),
            "l1_w2": stacked_pairs(i["L1_ffn_w2"]), "l1_b1": pair_columns(i["L1_ffn_b1"]),
            "l1_b2": by_expert(i["L1_ffn_b2"]),
            "l2_rb1": pad_to(i["L2_ffn_router_b1"][:, None], P, 1), "l2_rw2": pad_to(i["L2_ffn_router_w2"], P, E2),
            "l2_e2": side_by_side([blocks_of(i["L2_ffn_expert_w2"][e], i["L2_ffn_expert_w2"][e + 1])
                                   for e in range(0, E2, 2)]),
            "l2_e3": stacked_pairs(i["L2_ffn_expert_w3"]), "l2_eb1": pair_columns(i["L2_ffn_expert_b1"]),
            "l2_eb2": pair_columns(i["L2_ffn_expert_b2"]), "l2_eb3": by_expert(i["L2_ffn_expert_b3"]),
            "l3_post": side_by_side([blocks_of(i["L3_attn_Wout"][P * k:P * k + D], i["L3_attn_Wout"][P * k + D:P * k + P])
                                     for k in range(HEADS // 2)]),
            "l3_s2": pad_to(i["L3_ffn_sW2"], P, P), "l3_s3": i["L3_ffn_sW3"],
            "l3_sb1": pad_to(i["L3_ffn_sb1"][:, None], P, 1), "l3_sb2": i["L3_ffn_sb2"][:, None],
            "l3_e2": side_by_side(i["L3_ffn_eW2"]), "l3_e3": stacked_pairs(i["L3_ffn_eW3"]),
            "l3_eb1": i["L3_ffn_eb1"].T, "l3_eb2": pair_columns(i["L3_ffn_eb2"]), "l3_eb3": by_expert(i["L3_ffn_eb3"])}
    for n in range(LAYERS):
        full[f"l2_wo{n}"] = np.concatenate([i["L2_attn_Wo"][n]] * 2, 0)
        full[f"l2_w2{n}"] = np.concatenate([i["L2_attn_W2"][n][0:P], i["L2_attn_W2"][n][P:FF]], 1)
        full[f"l2_b1{n}"] = i["L2_attn_b1"][n].reshape(2, P).T
    arrays["full"] = pack(full_layout(), full, P)
    rows = {"l0_gate_b": i["L0_ffn_gate_b"], "l1_vb": qkvb[2 * D:], "l1_scale": i["L1_attn_scale"].reshape(1),
            "l1_proj_b": i["L1_attn_proj_b"], "l2_rb2": i["L2_ffn_router_b2"], "l3_bout": i["L3_attn_bout"],
            "l3_sb3": i["L3_ffn_sb3"], "l3_gate_b": i["L3_ffn_gb"]}
    for n in ("ln1_g", "ln1_b", "ln2_g", "ln2_b"):
        rows["l1_" + n] = i["L1_attn_" + n]
    for k in range(LAYERS):
        for n in ("ln1_g", "ln1_b", "bo", "ln2_g", "ln2_b", "b2"):
            rows[f"l2_{n}{k}"] = i["L2_attn_" + n][k]
    arrays["row"] = pack(row_layout(), {k: v[None, :] for k, v in rows.items()}, 1)[0]
    p, q, c = (np.arange(n) for n in (P, 3, 7 * P))
    distance = 2 * (c[None, None, :] - 3 * P - p[:, None, None]) + q[None, :, None] - 1
    arrays["toeplitz"] = i["L1_attn_bias_table"][np.minimum(distance + N - 1, len(i["L1_attn_bias_table"]) - 1)]

    def head_rows(w):
        t = w.T.reshape(HEADS // 2, P, D).transpose(1, 0, 2)
        return twice(t).reshape(P, HEADS // 2 * P)

    arrays["qk"] = np.concatenate([head_rows(i["L3_attn_WQ"]), head_rows(i["L3_attn_WK"])], 1)
    return {k: np.ascontiguousarray(v) for k, v in arrays.items()}


def kernel(**inputs):
    import concourse.bacc as _bacc
    from concourse.bass_utils import run_bass_kernel_spmd as _run

    arrays = lay_out({k: np.asarray(v) for k, v in inputs.items()})
    nc = _bacc.Bacc("TRN2", target_bir_lowering=False, num_devices=1)
    args = {k: nc.dram_tensor("in_" + k, a.shape, mybir.dt.from_np(a.dtype), kind="ExternalInput").ap()
            for k, a in arrays.items()}
    out = nc.dram_tensor("out_h", (B, N, D), F32, kind="ExternalOutput").ap()
    vit_tower_kernel(nc, out=out, **args)
    r = _run(nc, [{"in_" + k: a for k, a in arrays.items()}], core_ids=[0])
    return r.results[0]["out_h"]
```

```python
from contextlib import ExitStack

import numpy as np
import concourse.bass as bass
from concourse import mybir

F32 = mybir.dt.float32
F32R = mybir.dt.float32r
U32 = mybir.dt.uint32
ACT = mybir.ActivationFunctionType
ALU = mybir.AluOpType
AX = mybir.AxisListType

P = 128
B, C, TIME, V = 2, 64, 128, 64
D = 64
PATCH, STRIDE = 16, 8
NPATCH = TIME // STRIDE
N = V * NPATCH
T = B * N
NT = T // P
NTB = NT // B
BANK = 512
G = T // BANK
TPG = BANK // P
FREQ = 2 * (PATCH // 2 + 1)
TAP_FEATURES = P // FREQ
TAP_ROWS = TAP_FEATURES * FREQ
TAP_SETS = -(-D // TAP_FEATURES)
EPS = 1e-5
E0, H0 = 16, 128
E1 = 8
LAYERS, FF, HEADS2 = 4, 256, 8
E2, R2 = 6, 32
HEADS = 8
E3 = 4
PREPARED = 4
W2P = 2 * E2


class Layout:

    def __init__(self):
        self.at, self.n = {}, 0

    def add(self, name, cols):
        self.at[name] = (self.n, self.n + cols)
        self.n += cols

    def __getitem__(self, name):
        return slice(*self.at[name])


def split_layout_early():
    w = Layout()
    w.add("l0_attn", 128)
    w.add("l0_gate", E0)
    w.add("l0_w1", E0 * H0)
    w.add("l0_w2", E0 * H0)
    return w


def split_layout_mid():
    w = Layout()
    w.add("l1_q", 128)
    w.add("l1_k", 128)
    w.add("l1_v", 64)
    w.add("l1_gate", E1)
    w.add("l1_w1", E1 * D)
    for i in range(LAYERS):
        w.add(f"l2_k{i}", 128)
        w.add(f"l2_qv{i}", 128)
        w.add(f"l2_w1{i}", FF)
    w.add("l2_router", 128)
    w.add("l2_e1", E2 * D)
    return w


def split_layout_late():
    w = Layout()
    w.add("l3_v", HEADS * D)
    w.add("l3_gate", E3)
    w.add("l3_s1", 128)
    w.add("l3_e1", E3 * 128)
    return w


def full_layout():
    w = Layout()
    w.add("ident", 128)
    w.add("fold", D)
    w.add("expert_rows", E0)
    w.add("iota", 16)
    w.add("head_mask", 128)
    w.add("l0_w3", E0 * D)
    w.add("l1_qb", 1)
    w.add("l1_kb", 1)
    w.add("l1_post", 128)
    w.add("l1_w2", E1 // 2 * D)
    w.add("l1_b1", E1 // 2)
    w.add("l1_b2", D)
    for i in range(LAYERS):
        w.add(f"l2_wo{i}", D)
        w.add(f"l2_w2{i}", 2 * D)
        w.add(f"l2_b1{i}", 2)
    w.add("l2_rb1", 1)
    w.add("l2_rw2", E2)
    w.add("l2_e2", E2 // 2 * 128)
    w.add("l2_e3", E2 // 2 * D)
    w.add("l2_eb1", E2 // 2)
    w.add("l2_eb2", E2 // 2)
    w.add("l2_eb3", D)
    w.add("l3_post", HEADS // 2 * 128)
    w.add("l3_s2", 128)
    w.add("l3_s3", D)
    w.add("l3_sb1", 1)
    w.add("l3_sb2", 1)
    w.add("l3_e2", E3 * D)
    w.add("l3_e3", E3 // 2 * D)
    w.add("l3_eb1", E3)
    w.add("l3_eb2", E3 // 2)
    w.add("l3_eb3", D)
    return w


def row_layout():
    w = Layout()
    w.add("l0_gate_b", E0)
    for x in ("ln1_g", "ln1_b", "vb", "proj_b", "ln2_g", "ln2_b"):
        w.add("l1_" + x, D)
    w.add("l1_scale", 1)
    for i in range(LAYERS):
        for x in ("ln1_g", "ln1_b", "bo", "ln2_g", "ln2_b", "b2"):
            w.add(f"l2_{x}{i}", D)
    w.add("l2_rb2", E2)
    w.add("l3_bout", D)
    w.add("l3_sb3", D)
    w.add("l3_gate_b", E3)
    return w


class Signal:

    def __init__(self, nc, name):
        self.sem, self.base = nc.alloc_semaphore(name), 0

    def __call__(self, n):
        return self.base + n

    def passed(self, n):
        self.base += n


def wide(ap, n):
    return ap.unsqueeze(2).to_broadcast([ap.shape[0], ap.shape[1], n])


def rows_over(ap, n):
    return ap.unsqueeze(1).to_broadcast([ap.shape[0], n, ap.shape[1]])


class Tower:

    def __init__(self, nc, ctx):
        self.nc, self.ctx, self.counters, self.named = nc, ctx, {}, {}
        self.full, self.row = full_layout(), row_layout()
        self.early, self.mid, self.late = split_layout_early(), split_layout_mid(), split_layout_late()

    def sb(self, name, shape, dt=F32, ctx=None):
        self.named[name] = self.named.get(name, 0) + 1
        if self.named[name] > 1:
            name = f"{name}_{self.named[name]}"
        return (ctx or self.ctx).enter_context(self.nc.sbuf_tensor(name, shape, dt))

    def counter(self, name):
        if name not in self.counters:
            self.counters[name] = Signal(self.nc, name)
        return self.counters[name]

    def w(self, name):
        return self.w_full[:, self.full[name]]

    def r(self, name):
        return self.w_row[:, self.row[name]]




def embed_stage(tw, x, wk, early, full, row):
    nc, h = tw.nc, tw.h
    NB = NPATCH + 1
    wk_landed = nc.alloc_semaphore("wk_landed")
    x_landed = [nc.alloc_semaphore(f"x_landed{b}") for b in range(B)]
    taps_ready = nc.alloc_semaphore("taps_ready")
    taps_copied = nc.alloc_semaphore("taps_copied")
    conv_ready = nc.alloc_semaphore("conv_ready")
    conv_copied = nc.alloc_semaphore("conv_copied")
    turned = nc.alloc_semaphore("embed_turned")
    hi_made = nc.alloc_semaphore("early_hi_made")
    with ExitStack() as ctx:
        xs = tw.sb("series", [P, B, NB, 4, V], ctx=ctx)
        wks = tw.sb("wk_rows", [TAP_ROWS, TAP_SETS * C + PATCH * TAP_FEATURES], ctx=ctx)
        taps = tw.sb("taps", [P, 2, 4, D], ctx=ctx)
        ht = tw.sb("embed_t", [P, B, V, NPATCH // 2], ctx=ctx)
        raw = tw.sb("early_raw", [P, tw.early.n], ctx=ctx)

        def piece(k):
            return slice(k * tw.early.n // 8, (k + 1) * tw.early.n // 8)

        block = ctx.enter_context(nc.Block())

        @block.sync
        def _(sp):
            sp.dma_start(wks[:, :], wk).then_inc(wk_landed, 16)
            for b in range(B):
                blocks = x[b].rearrange("c (m u s) v -> u c m (s v)", u=2, s=4)
                for u in range(2):
                    rows = xs[64 * u:64 * u + 64, b]
                    sp.dma_start(rows[:, 0:NPATCH].rearrange("c m s v -> c m (s v)"),
                                 blocks[u]).then_inc(x_landed[b], 16)
                    sp.dma_start(rows[:, NPATCH], x[b, :, TIME - 1:TIME, :].to_broadcast([C, 4, V]))\
                        .then_inc(x_landed[b], 16)
            sp.dma_start(tw.w_full[:, :], full).then_inc(tw.full_landed, 16)
            for half in range(2):
                sp.dma_start(raw[64 * half:64 * half + 64, :], early).then_inc(tw.early_landed, 16)
            sp.dma_start(tw.w_row[:, :], row.partition_broadcast(P)).then_inc(tw.row_landed, 16)

        @block.gpsimd
        def _(pool):
            for k in range(5, 8):
                pool.wait_ge(hi_made, k - 4)
                pool.tensor_tensor(tw.early_lo[:, piece(k)], raw[:, piece(k)], tw.early_hi[:, piece(k)].bitcast(F32),
                                   ALU.subtract)

        @block.scalar
        def _(act):
            for b in range(B):
                act.wait_ge(conv_ready, b + 1)
                nc.scalar.copy(ht[:, b].rearrange("p v n -> p n v"),
                               tw.ps[:, b, :].rearrange("p (n v) -> p n v", v=V)).then_inc(conv_copied, 1)
                if b == 0:
                    act.wait_ge(tw.early_landed, 32)
                    for k in (5, 6, 7, 0, 1, 2, 3, 4):
                        nc.scalar.copy(tw.early_hi[:, piece(k)], raw[:, piece(k)]).then_inc(hi_made, 1)

        @block.tensor
        def _(pe):
            pe.wait_ge(wk_landed, 16)
            width = TAP_FEATURES * PATCH // 2
            for n in range(TAP_SETS):
                for u in range(2):
                    dft = wks[:, TAP_SETS * C + u * width:TAP_SETS * C + (u + 1) * width]
                    bank, c = 4 + n // 5, n % 5 * width
                    mm = nc.tensor.matmul(tw.ps[64 * u:64 * u + 64, bank, c:c + width],
                                          wks[:, n * C:(n + 1) * C], dft, start=True, stop=True)
                if n % 5 == 4:
                    mm.then_inc(taps_ready, 1)
            pe.wait_ge(taps_copied, 2)
            for b in range(B):
                pe.wait_ge(x_landed[b], 16 * 4)
                for k in range(8):
                    hh, s = k // 4, k % 4
                    for par in range(2):
                        first = hh + par
                        mm = nc.tensor.matmul(tw.ps[64 * par:64 * par + 64, b, :],
                                              taps[:, hh, s, :], xs[:, b, first:first + 15:2, s, :],
                                              start=(k == 0), stop=(k == 7))
                mm.then_inc(conv_ready, 1)
            pe.wait_ge(tw.full_landed, 16)
            for b in range(B):
                pe.wait_ge(conv_copied, b + 1)
                for vhi in range(4):
                    mm = nc.tensor.transpose(tw.ps[:, 2 + b, vhi * P:(vhi + 1) * P],
                                             ht[:, b, 16 * vhi:16 * vhi + 16, :].rearrange("p v n -> p (v n)"),
                                             tw.w("ident"))
                mm.then_inc(turned, 1)

        @block.vector
        def _(dve):
            nc.vector.memset(tw.minus_half[:, :], -0.5)
            for n in range(2):
                dve.wait_ge(taps_ready, n + 1)
                j0, nj = 5 * TAP_FEATURES * n, min(5 * TAP_FEATURES, D - 5 * TAP_FEATURES * n)
                nc.vector.tensor_copy(taps[:, :, :, j0:j0 + nj],
                                      tw.ps[:, 4 + n, 0:8 * nj].rearrange("p (j h s) -> p h s j", h=2, s=4))\
                    .then_inc(taps_copied, 1)
            for k in range(5):
                dve.wait_ge(hi_made, k + 4)
                nc.vector.tensor_tensor(tw.early_lo[:, piece(k)], raw[:, piece(k)], tw.early_hi[:, piece(k)].bitcast(F32),
                                        ALU.subtract)
            for b in range(B):
                dve.wait_ge(turned, b + 1)
                nc.vector.tensor_copy(h[:, 8 * b:8 * b + 8, :].rearrange("p t j -> p (t j)"), tw.ps[:, 2 + b, :])
            dve.wait_ge(tw.row_landed, 16)




def norm_stage(tw, src, gamma=None, beta=None, keep=None, turn=True):
    nc = tw.nc
    sums, centred, squared, spread = (tw.counter(x) for x in ("ln_sums", "ln_centred", "ln_squared", "ln_spread"))
    eps_added, rooted, normed = (tw.counter(x) for x in ("ln_eps_added", "ln_rooted", "ln_normed"))
    hi_made, lo_made, turned = (tw.counter(x) for x in ("ln_hi_made", "ln_lo_made", "ln_turned"))
    affine = gamma is not None
    x = keep if keep is not None else tw.xn
    steps = 3 if affine else 1
    dst = (lambda g: x[:, TPG * g:TPG * g + TPG, :])
    with ExitStack() as ctx:
        total, var, rstd = (tw.sb("ln_" + n, [P, NT], ctx=ctx) for n in ("total", "var", "rstd"))
        xc = tw.sb("ln_xc", [P, NT, D], ctx=ctx)
        sq = tw.sb("ln_sq", [P, NT, D], ctx=ctx)
        pair = tw.sb("ln_pair", [P, NT, 2 * D], ctx=ctx)
        block = ctx.enter_context(nc.Block())

        @block.vector
        def _(dve):
            for i in range(-1, G + 4):
                if 0 <= i < G:
                    t = slice(TPG * i, TPG * i + TPG)
                    dve.wait_ge(sums.sem, sums(i + 1))
                    nc.vector.scalar_tensor_tensor(out=xc[:, t, :], in0=wide(total[:, t], D), scalar=-1.0 / D,
                                                   in1=src[:, t, :], op0=ALU.mult, op1=ALU.add)\
                        .then_inc(centred.sem, 1)
                g = i - 1
                if 0 <= g < G:
                    t = slice(TPG * g, TPG * g + TPG)
                    dve.wait_ge(squared.sem, squared(g + 1))
                    nc.vector.reduce_sum(var[:, t], sq[:, t, :], AX.X).then_inc(spread.sem, 1)
                if i + 1 < G:
                    t = slice(TPG * (i + 1), TPG * (i + 1) + TPG)
                    nc.vector.reduce_sum(total[:, t], src[:, t, :], AX.X).then_inc(sums.sem, 1)
                g = i - 3
                if 0 <= g < G:
                    t = slice(TPG * g, TPG * g + TPG)
                    dve.wait_ge(rooted.sem, rooted(g + 1))
                    nc.vector.tensor_tensor(dst(g), xc[:, t, :], wide(rstd[:, t], D), ALU.mult)\
                        .then_inc(normed.sem, 1)
                g = i - 1
                if 0 <= g < G:
                    t = slice(TPG * g, TPG * g + TPG)
                    dve.wait_ge(spread.sem, spread(g + 1))
                    nc.vector.tensor_scalar(var[:, t], var[:, t], EPS, None, ALU.add).then_inc(eps_added.sem, 1)
                g = i - 3
                if affine and 0 <= g < G:
                    dve.wait_ge(normed.sem, normed(steps * g + 1))
                    nc.vector.tensor_tensor(dst(g), dst(g), rows_over(gamma, TPG), ALU.mult)\
                        .then_inc(normed.sem, 1)
                    dve.wait_ge(normed.sem, normed(steps * g + 2))
                    nc.vector.tensor_tensor(dst(g), dst(g), rows_over(beta, TPG), ALU.add).then_inc(normed.sem, 1)
                g = i - 4
                if turn and 0 <= g < G:
                    t = slice(TPG * g, TPG * g + TPG)
                    dve.wait_ge(hi_made.sem, hi_made(g + 1))
                    nc.vector.tensor_tensor(pair[:, t, D:2 * D], dst(g), pair[:, t, 0:D], ALU.subtract)\
                        .then_inc(lo_made.sem, 1)
            if turn:
                dve.wait_ge(turned.sem, turned(G))
                nc.vector.tensor_copy(tw.xt[:, T - BANK:T], tw.ps[:, G - 1, :])

        @block.scalar
        def _(act):
            for g in range(G):
                t = slice(TPG * g, TPG * g + TPG)
                act.wait_ge(centred.sem, centred(g + 1))
                nc.scalar.activation(sq[:, t, :], xc[:, t, :], ACT.Square, scale=float(D) ** -0.5)\
                    .then_inc(squared.sem, 1)
            if turn:
                for g in range(G):
                    t = slice(TPG * g, TPG * g + TPG)
                    act.wait_ge(normed.sem, normed(steps * (g + 1)))
                    nc.scalar.copy(pair[:, t, 0:D].bitcast(F32R), dst(g)).then_inc(hi_made.sem, 1)
                    if g >= 2:
                        act.wait_ge(turned.sem, turned(g - 1))
                        nc.scalar.copy(tw.xt[:, BANK * (g - 2):BANK * (g - 1)], tw.ps[:, g - 2, :])
                act.wait_ge(turned.sem, turned(G - 1))
                nc.scalar.copy(tw.xt[:, BANK * (G - 2):BANK * (G - 1)], tw.ps[:, G - 2, :])

        @block.gpsimd
        def _(pool):
            for g in range(G):
                t = slice(TPG * g, TPG * g + TPG)
                pool.wait_ge(eps_added.sem, eps_added(g + 1))
                pool.tensor_tensor(rstd[:, t], var[:, t], tw.minus_half[:, t], ALU.pow)\
                    .then_inc(rooted.sem, 1)

        if turn:
            @block.tensor
            def _(pe):
                for g in range(G):
                    pe.wait_ge(lo_made.sem, lo_made(g + 1))
                    for k in range(TPG):
                        mm = nc.tensor.transpose(tw.ps[:, g, k * P:(k + 1) * P], pair[:, TPG * g + k, :],
                                                 tw.w("ident"))
                    mm.then_inc(turned.sem, 1)
    for s in (sums, centred, squared, spread, eps_added, rooted):
        s.passed(G)
    normed.passed(steps * G)
    if turn:
        for s in (hi_made, lo_made, turned):
            s.passed(G)




def attention_stage(tw, name, groups, scale, q_hi, q_lo, keys, value, post, bias_strips, finish, out,
                    project=None):
    nc, ps = tw.nc, tw.ps
    U = 8 * len(groups)
    NG = len(groups)
    s_ready, biased, maxed, p_ready = (tw.counter(x) for x in ("s_ready", "s_biased", "s_maxed", "p_ready"))
    p_turned, pt_first, pt_second = (tw.counter(x) for x in ("p_turned", "pt_first", "pt_second"))
    o_ready, o_copied, y_ready, y_scaled, inv_ready, y_added = (
        tw.counter(x) for x in ("o_ready", "o_copied", "y_ready", "y_scaled", "inv_ready", "y_added"))
    unscaled = tw.counter("s_unscaled")
    S_BANK, T_BANK, O_BANK = 0, 4, 6
    nq_made, nq_hi, nq_lo = (tw.counter(x) for x in ("nq_made", "nq_hi", "nq_lo"))
    projected = 2 * (NG - PREPARED) if project else 0

    def query_job(i, lag):
        g, w = (i - lag - 21) // 8, (i - lag - 21) % 8
        return 2 * g + w // 2 if w in (0, 2) and 0 <= 2 * g + w // 2 < projected else None

    HALF = N // 2
    n_add = 2 if finish != "store" else 0
    with ExitStack() as ctx:
        prob = tw.sb(name + "_prob", [P, 2, N], ctx=ctx)
        prob_t = tw.sb(name + "_prob_t", [P, 2, 2, NTB, HALF], ctx=ctx)
        nmax = tw.sb(name + "_nmax", [P, U], ctx=ctx)
        raw_max = tw.sb(name + "_raw_max", [P, U], ctx=ctx)
        total = tw.sb(name + "_total", [P, NG, 4, 2], ctx=ctx)
        inv = tw.sb(name + "_inv", [P, NG, 4, 2], ctx=ctx)
        o_sb = tw.sb(name + "_o", [P, 2, BANK], ctx=ctx)
        y_sb = tw.sb(name + "_y", [P, 2, 4, 2, D], ctx=ctx)
        if bias_strips is not None:
            logits = tw.sb(name + "_logits", [P, 2, N], ctx=ctx)
        block = ctx.enter_context(nc.Block())

        def parts(u):
            return u // 8, u % 8 // 4, u % 4

        @block.tensor
        def _(pe):
            for i in range(U + 21):
                if i < U:
                    g, j, nt = parts(i)
                    _, q0, k0, _ = groups[g]
                    if project and g >= PREPARED and i % 8 == 0:
                        pe.wait_ge(nq_lo.sem, nq_lo(2 * (g - PREPARED) + 2))
                    if i >= 2:
                        if bias_strips is None:
                            pe.wait_ge(p_ready.sem, p_ready(i - 1))
                        else:
                            pe.wait_ge(biased.sem, biased(i - 1))
                    for mh in range(2):
                        for k, q in enumerate((q_hi, q_lo)):
                            mm = nc.tensor.matmul(ps[:, S_BANK + 2 * (i % 2) + mh, :],
                                                  q(g, j)[:, q0[j] + nt * P:q0[j] + nt * P + P],
                                                  keys[:, k0[j] + mh * BANK:k0[j] + mh * BANK + BANK],
                                                  start=(k == 0), stop=(k == 1))
                    mm.then_inc(s_ready.sem, 1)
                if 2 <= i < U + 2:
                    u = i - 2
                    pe.wait_ge(p_ready.sem, p_ready(u + 1))
                    for half in range(2):
                        if u >= 1:
                            copied = pt_second if half else pt_first
                            pe.wait_ge(copied.sem, copied(u))
                        for k in range(4):
                            mm = nc.tensor.transpose(ps[:, T_BANK + half, k * P:(k + 1) * P],
                                                     prob[:, u % 2, (4 * half + k) * P:(4 * half + k + 1) * P],
                                                     tw.w("ident"))
                        mm.then_inc(p_turned.sem, 1)
                g, w = (i - 10) // 8, (i - 10) % 8
                if 0 <= g < NG:
                    members = groups[g][0]
                    if w == 0:
                        pe.wait_ge(pt_first.sem, pt_first(8 * (g + 1)))
                        pe.wait_ge(pt_second.sem, pt_second(8 * (g + 1)))
                        if g >= 2:
                            pe.wait_ge(y_scaled.sem, y_scaled(g - 1))
                            if 2 * (g - 1) <= projected:
                                pe.wait_ge(nq_lo.sem, nq_lo(2 * (g - 1)))
                    for j in range(2):
                        mm = nc.tensor.matmul(ps[64 * j:64 * j + 64, O_BANK + g % 2, :], value(members[j], w),
                                              prob_t[:, g % 2, j, w, :], start=(w == 0), stop=(w == 7))
                    if w == 7:
                        mm.then_inc(o_ready.sem, 1)
                g = (i - 19) // 8
                if (i - 19) % 8 == 0 and 0 <= g < NG:
                    pe.wait_ge(o_copied.sem, o_copied(g + 1))
                    for nt in range(4):
                        mm = nc.tensor.matmul(ps[:, O_BANK + g % 2, nt * P:(nt + 1) * P],
                                              o_sb[:, g % 2, nt * P:(nt + 1) * P], post(g), start=True, stop=True)
                    mm.then_inc(y_ready.sem, 1)
                n = query_job(i, 0)
                if n is not None:
                    pe.wait_ge(y_scaled.sem, y_scaled(n // 2 + 1))
                    if n >= 1:
                        pe.wait_ge(nq_lo.sem, nq_lo(n))
                    (wh, wl), c = project(n // 2 + PREPARED, n % 2)
                    for k, part in enumerate((wh, wl)):
                        mm = nc.tensor.matmul(ps[:, O_BANK + n // 2 % 2, :], part, tw.xt[:, c:c + BANK],
                                              start=(k == 0), stop=(k == 1))
                    mm.then_inc(nq_made.sem, 1)

        @block.scalar
        def _(act):
            for i in range(U + 21):
                if 2 <= i < U + 2:
                    u = i - 2
                    g, j, nt = parts(u)
                    act.wait_ge(p_turned.sem, p_turned(2 * u + 2))
                    if g >= 2 and u % 8 == 0:
                        act.wait_ge(o_ready.sem, o_ready(g - 1))
                    if bias_strips is not None:
                        nc.scalar.copy(prob_t[:, g % 2, j, 0:4, nt * P:(nt + 1) * P],
                                       ps[:, T_BANK, :].rearrange("p (a b) -> p a b", a=4)).then_inc(pt_first.sem, 1)
                    nc.scalar.copy(prob_t[:, g % 2, j, 4:8, nt * P:(nt + 1) * P],
                                   ps[:, T_BANK + 1, :].rearrange("p (a b) -> p a b", a=4)).then_inc(pt_second.sem, 1)
                if i < U:
                    g, j, nt = parts(i)
                    act.wait_ge(maxed.sem, maxed(i + 1))
                    if i >= 2:
                        act.wait_ge(p_turned.sem, p_turned(2 * (i - 1)))
                    source = ps[:, S_BANK + 2 * (i % 2):S_BANK + 2 * (i % 2) + 2, :].rearrange("p a b -> p (a b)")
                    if bias_strips is not None:
                        source = logits[:, i % 2, :]
                    nc.scalar.activation(prob[:, i % 2, :], source, ACT.Exp, bias=nmax[:, i:i + 1], scale=scale,
                                         accum_out=total[:, g, nt, j:j + 1]).then_inc(p_ready.sem, 1)
                g = (i - 18) // 8
                if (i - 18) % 8 == 0 and 0 <= g < NG:
                    act.wait_ge(o_ready.sem, o_ready(g + 1))
                    if g >= 2:
                        act.wait_ge(y_ready.sem, y_ready(g - 1))
                    nc.scalar.copy(o_sb[:, g % 2, :], ps[:, O_BANK + g % 2, :]).then_inc(o_copied.sem, 1)
                n = query_job(i, 0)
                if n is not None:
                    act.wait_ge(nq_made.sem, nq_made(n + 1))
                    nc.scalar.copy(q_hi(n // 2 + PREPARED, n % 2), ps[:, O_BANK + n // 2 % 2, :]).then_inc(nq_hi.sem, 1)

        @block.vector
        def _(dve):
            for i in range(U + 21):
                if i < U:
                    g, j, nt = parts(i)
                    dve.wait_ge(s_ready.sem, s_ready(i + 1))
                    source = ps[:, S_BANK + 2 * (i % 2):S_BANK + 2 * (i % 2) + 2, :].rearrange("p a b -> p (a b)")
                    if bias_strips is not None:
                        qt = groups[g][3] + nt
                        vhi, par = qt // 2, qt % 2
                        if i >= 2:
                            dve.wait_ge(p_ready.sem, p_ready(i - 1))
                        for kpar in range(2):
                            strip = bias_strips[:, kpar - par + 1, (3 - vhi) * P:(7 - vhi) * P]
                            view = logits[:, i % 2, :].rearrange("p (a k b) -> p a k b", a=4, k=2)[:, :, kpar, :]
                            scores = source.rearrange("p (a k b) -> p a k b", a=4, k=2)[:, :, kpar, :]
                            ins = nc.vector.tensor_tensor(view, scores, strip.rearrange("p (a b) -> p a b", a=4),
                                                          ALU.add)
                        ins.then_inc(biased.sem, 1)
                        dve.wait_ge(biased.sem, biased(i + 1))
                        source = logits[:, i % 2, :]
                    if scale == 1.0:
                        nc.vector.tensor_reduce(nmax[:, i:i + 1], source, AX.X, ALU.max, negate=True)\
                            .then_inc(maxed.sem, 1)
                    else:
                        nc.vector.tensor_reduce(raw_max[:, i:i + 1], source, AX.X, ALU.max, negate=True)\
                            .then_inc(unscaled.sem, 1)
                        dve.wait_ge(unscaled.sem, unscaled(i + 1))
                        nc.vector.tensor_scalar(nmax[:, i:i + 1], raw_max[:, i:i + 1], scale, None, ALU.mult)\
                            .then_inc(maxed.sem, 1)
                if bias_strips is None and 2 <= i < U + 2:
                    u = i - 2
                    g, j, nt = parts(u)
                    dve.wait_ge(p_turned.sem, p_turned(2 * u + 1))
                    if g >= 2 and u % 8 == 0:
                        dve.wait_ge(o_ready.sem, o_ready(g - 1))
                    nc.vector.tensor_copy(prob_t[:, g % 2, j, 0:4, nt * P:(nt + 1) * P],
                                          ps[:, T_BANK, :].rearrange("p (a b) -> p a b", a=4)).then_inc(pt_first.sem, 1)
                n = query_job(i, 1)
                if n is not None:
                    dve.wait_ge(nq_hi.sem, nq_hi(n + 1))
                    nc.vector.tensor_tensor(q_lo(n // 2 + PREPARED, n % 2), ps[:, O_BANK + n // 2 % 2, :],
                                            q_hi(n // 2 + PREPARED, n % 2).bitcast(F32), ALU.subtract)\
                        .then_inc(nq_lo.sem, 1)
                g = (i - 9) // 8
                if (i - 9) % 8 == 0 and 0 <= g < NG:
                    dve.wait_ge(p_ready.sem, p_ready(8 * (g + 1)))
                    nc.vector.reciprocal(inv[:, g], total[:, g]).then_inc(inv_ready.sem, 1)
                g = (i - 20) // 8
                if (i - 20) % 8 == 0 and 0 <= g < NG:
                    dve.wait_ge(y_ready.sem, y_ready(g + 1))
                    dve.wait_ge(inv_ready.sem, inv_ready(g + 1))
                    if g >= 2 and n_add:
                        dve.wait_ge(y_added.sem, y_added(n_add * (g - 1)))
                    rows = ps[:, O_BANK + g % 2, :].rearrange("p (n e) -> p n e", n=8)
                    if finish == "store":
                        for j in range(2):
                            ins = nc.vector.tensor_tensor(
                                out(g, j), ps[:, O_BANK + g % 2, :].rearrange("p (n j e) -> p n j e", n=4, j=2)[:, :, j],
                                wide(inv[:, g, :, j], D), ALU.mult)
                        ins.then_inc(y_scaled.sem, 1)
                    else:
                        nc.vector.tensor_tensor(y_sb[:, g % 2].rearrange("p n j e -> p (n j) e"), rows,
                                                wide(inv[:, g].rearrange("p n j -> p (n j)"), D), ALU.mult)\
                            .then_inc(y_scaled.sem, 1)

        if n_add:
            @block.gpsimd
            def _(pool):
                for g in range(NG):
                    pool.wait_ge(y_scaled.sem, y_scaled(g + 1))
                    for j in range(2):
                        if g or j:
                            pool.wait_ge(y_added.sem, y_added(2 * g + j))
                        pool.tensor_tensor(out(g, j), out(g, j), y_sb[:, g % 2, :, j, :], ALU.add)\
                            .then_inc(y_added.sem, 1)
    for s in (s_ready, maxed, p_ready, pt_first, pt_second):
        s.passed(U)
    if scale != 1.0:
        unscaled.passed(U)
    if bias_strips is not None:
        biased.passed(U)
    p_turned.passed(2 * U)
    for s in (o_ready, o_copied, y_ready, y_scaled, inv_ready):
        s.passed(NG)
    y_added.passed(n_add * NG)
    for s in (nq_made, nq_hi, nq_lo):
        s.passed(projected)


def project_stage(tw, jobs):
    nc, ps = tw.nc, tw.ps
    made, hi_made, lo_made, kept = (tw.counter(x) for x in ("pj_made", "pj_hi", "pj_lo", "pj_kept"))
    nk = 0
    with ExitStack() as ctx:
        high = tw.sb("key_high", [P, 2, BANK], ctx=ctx)
        block = ctx.enter_context(nc.Block())

        @block.tensor
        def _(pe):
            for n, (wh, wl, col, bias, kind, dst) in enumerate(jobs):
                if n >= 8:
                    pe.wait_ge(lo_made.sem, lo_made(n - 7))
                    pe.wait_ge(hi_made.sem, hi_made(n - 7))
                nc.tensor.matmul(ps[:, n % 8, :], wh, tw.xt[:, col:col + BANK], start=True, stop=False)
                nc.tensor.matmul(ps[:, n % 8, :], wl, tw.xt[:, col:col + BANK], start=False, stop=True)\
                    .then_inc(made.sem, 1)

        @block.scalar
        def _(act):
            k = 0
            for n, (wh, wl, col, bias, kind, dst) in enumerate(jobs):
                act.wait_ge(made.sem, made(n + 1))
                b = bias if bias is not None else 0.0
                if kind == "queries":
                    nc.scalar.activation(dst[0], ps[:, n % 8, :], ACT.Identity, bias=b).then_inc(hi_made.sem, 1)
                else:
                    lower = b[D:P, :] if bias is not None else 0.0
                    upper = b[0:D, :] if bias is not None else 0.0
                    if k >= 2:
                        act.wait_ge(lo_made.sem, lo_made(n - 1))
                    nc.scalar.activation(dst[0][0:D, :], ps[0:D, n % 8, :], ACT.Identity, bias=upper)
                    nc.scalar.activation(high[D:P, k % 2, :].bitcast(F32R), ps[D:P, n % 8, :], ACT.Identity,
                                         bias=lower).then_inc(hi_made.sem, 1)
                    k += 1

        @block.vector
        def _(dve):
            k = 0
            for n, (wh, wl, col, bias, kind, dst) in enumerate(jobs):
                dve.wait_ge(hi_made.sem, hi_made(n + 1))
                b = bias if bias is not None else 0.0
                if kind == "queries":
                    nc.vector.scalar_tensor_tensor(out=dst[1], in0=ps[:, n % 8, :], scalar=b,
                                                   in1=dst[0].bitcast(F32), op0=ALU.add, op1=ALU.subtract)\
                        .then_inc(lo_made.sem, 1)
                else:
                    lower = b[D:P, :] if bias is not None else 0.0
                    nc.vector.scalar_tensor_tensor(out=dst[0][D:P, :], in0=ps[D:P, n % 8, :], scalar=lower,
                                                   in1=high[D:P, k % 2, :], op0=ALU.add, op1=ALU.subtract)\
                        .then_inc(lo_made.sem, 1)
                    k += 1
    for s in (made, hi_made, lo_made):
        s.passed(len(jobs))


def value_stage(tw, wh, wl, cols, tiles, dst, bias=None):
    nc, ps = tw.nc, tw.ps
    made, copied = tw.counter("vl_made"), tw.counter("vl_copied")
    with ExitStack() as ctx:
        block = ctx.enter_context(nc.Block())

        @block.tensor
        def _(pe):
            for n, t in enumerate(tiles):
                if n >= 8:
                    pe.wait_ge(copied.sem, copied(n - 7))
                nc.tensor.matmul(ps[:, n % 8, 0:cols], tw.xt[:, t * P:(t + 1) * P], wh, start=True, stop=False)
                nc.tensor.matmul(ps[:, n % 8, 0:cols], tw.xt[:, t * P:(t + 1) * P], wl, start=False, stop=True)\
                    .then_inc(made.sem, 1)

        @block.vector
        def _(dve):
            for n, t in enumerate(tiles):
                dve.wait_ge(made.sem, made(n + 1))
                if bias is None:
                    nc.vector.tensor_copy(dst(t), ps[:, n % 8, 0:cols]).then_inc(copied.sem, 1)
                else:
                    nc.vector.tensor_tensor(dst(t), ps[:, n % 8, 0:cols], bias, ALU.add).then_inc(copied.sem, 1)
    made.passed(len(tiles))
    copied.passed(len(tiles))




def route_stage(tw, experts, lhs, gate, bias, second_softmax, selectors):
    nc, ps, E = tw.nc, tw.ps, experts
    made, step, ex, turned, ct_dve = (tw.counter(x) for x in ("rt_made", "rt_step", "rt_exp", "rt_turned", "rt_ct"))
    cleared = tw.counter("rt_cleared")
    ex_count = 2 if second_softmax else 1
    EP = max(E, 8)
    count = [0]
    split = isinstance(gate, tuple)
    NP = 2 if split else 1
    last_step = 18 + (1 if split else 0) + (1 if bias is not None else 0) + (1 if second_softmax else 0)
    centred_step = 3 + (1 if split else 0) + (1 if bias is not None else 0)
    with ExitStack() as ctx:
        lg = tw.sb("rt_logits", [P, NT, E], ctx=ctx)
        mx = tw.sb("rt_max", [P, NT], ctx=ctx)
        pr = tw.sb("rt_probs", [P, NT, EP], ctx=ctx)
        top = tw.sb("rt_top", [P, NT, 8], ctx=ctx)
        idx = tw.sb("rt_index", [P, NT, 8], U32, ctx=ctx)
        idf = tw.sb("rt_index_f", [P, NT, 2], ctx=ctx)
        wt = tw.sb("rt_weight", [P, NT, 2], ctx=ctx)
        sm = tw.sb("rt_sum", [P, NT], ctx=ctx)
        cw = tw.sb("rt_combine", [P, NT, E], ctx=ctx)
        c2 = tw.sb("rt_combine2", [P, NT, 2, E], ctx=ctx)
        gates = tw.sb("rt_gates", [P, 2, E], F32R, ctx=ctx)
        cp = tw.sb("rt_pair", [P, NT, P], ctx=ctx)
        block = ctx.enter_context(nc.Block())
        logits = ps[:, 0, 0:NT * NP * E].rearrange("p (t k e) -> p t k e", k=NP, e=E)

        @block.tensor
        def _(pe):
            if split:
                pe.wait_ge(step.sem, step(1))
            moving = gates[:, :, :].rearrange("p k e -> p (k e)") if split else gate
            for t in range(NT):
                mm = nc.tensor.matmul(logits[:, t].rearrange("p k e -> p (k e)"), lhs(t), moving,
                                      start=True, stop=True)
            mm.then_inc(made.sem, 1)
            pe.wait_ge(step.sem, step(last_step))
            for g in range(G):
                for k in range(TPG):
                    mm = nc.tensor.transpose(ps[:, 1 + g, k * P:(k + 1) * P], cp[:, TPG * g + k, :], tw.w("ident"))
                mm.then_inc(turned.sem, 1)

        @block.scalar
        def _(act):
            nc.scalar.copy(selectors[:, :, :], wide(tw.w("expert_rows")[:, 0:E], selectors.shape[2]))
            act.wait_ge(step.sem, step(centred_step))
            act.wait_ge(cleared.sem, cleared(1))
            nc.scalar.activation(pr[:, :, 0:E], lg[:, :, :], ACT.Exp).then_inc(ex.sem, 1)
            if second_softmax:
                act.wait_ge(step.sem, step(centred_step + 7))
                nc.scalar.activation(wt[:, :, 1], wt[:, :, 1], ACT.Exp).then_inc(ex.sem, 1)
            for g in range(1, G, 2):
                act.wait_ge(turned.sem, turned(g + 1))
                nc.scalar.copy(tw.ct[:, BANK * g:BANK * g + BANK], ps[:, 1 + g, :])

        @block.gpsimd
        def _(pool):
            pool.memset(pr[:, :, :], -1.0).then_inc(cleared.sem, 1)
            pool.memset(cp[:, :, :], 0.0).then_inc(cleared.sem, 1)

        @block.vector
        def _(dve):
            def then(ins):
                count[0] += 1
                ins.then_inc(step.sem, 1)
                dve.wait_ge(step.sem, step(count[0]))

            if split:
                nc.vector.tensor_copy(gates[:, 0, :], gate[0])
                then(nc.vector.tensor_copy(gates[:, 1, :], gate[1]))
            dve.wait_ge(made.sem, made(1))
            then(nc.vector.reduce_sum(lg[:, :, :], logits.rearrange("p t k e -> p t e k"), AX.X))
            if bias is not None:
                then(nc.vector.tensor_tensor(lg[:, :, :], lg[:, :, :], rows_over(bias, NT), ALU.add))
            then(nc.vector.reduce_max(mx[:, :], lg[:, :, :], AX.X))
            then(nc.vector.tensor_tensor(lg[:, :, :], lg[:, :, :], wide(mx[:, :], E), ALU.subtract))
            dve.wait_ge(ex.sem, ex(1))
            then(nc.vector.reduce_sum(sm[:, :], pr[:, :, 0:E], AX.X))
            then(nc.vector.reciprocal(sm[:, :], sm[:, :]))
            then(nc.vector.tensor_tensor(pr[:, :, 0:E], pr[:, :, 0:E], wide(sm[:, :], E), ALU.mult))
            for t in range(NT):
                ins = nc.vector.max(top[:, t, :], pr[:, t, :])
            then(ins)
            for t in range(NT):
                ins = nc.vector.max_index(idx[:, t, :], top[:, t, :], pr[:, t, :])
            then(ins)
            then(nc.vector.tensor_copy(idf[:, :, :], idx[:, :, 0:2]))
            if second_softmax:
                then(nc.vector.tensor_tensor(wt[:, :, 1], top[:, :, 1], top[:, :, 0], ALU.subtract))
                dve.wait_ge(ex.sem, ex(2))
                then(nc.vector.tensor_scalar(sm[:, :], wt[:, :, 1], 1.0, None, ALU.add))
                then(nc.vector.reciprocal(sm[:, :], sm[:, :]))
                then(nc.vector.tensor_copy(wt[:, :, 0], sm[:, :]))
                then(nc.vector.tensor_tensor(wt[:, :, 1], wt[:, :, 1], sm[:, :], ALU.mult))
            else:
                then(nc.vector.tensor_tensor(sm[:, :], top[:, :, 0], top[:, :, 1], ALU.add))
                then(nc.vector.tensor_scalar(sm[:, :], sm[:, :], 1e-12, None, ALU.max))
                then(nc.vector.reciprocal(sm[:, :], sm[:, :]))
                then(nc.vector.tensor_tensor(wt[:, :, :], top[:, :, 0:2], wide(sm[:, :], 2), ALU.mult))
            chosen = c2[:, :, :, :].rearrange("p t k e -> p (t k) e")
            numbers = idf[:, :, :].rearrange("p t k -> p (t k)")
            then(nc.vector.tensor_tensor(chosen, rows_over(tw.w("iota")[:, 0:E], 2 * NT), wide(numbers, E),
                                         ALU.is_equal))
            then(nc.vector.tensor_tensor(chosen, chosen, wide(wt[:, :, :].rearrange("p t k -> p (t k)"), E), ALU.mult))
            then(nc.vector.tensor_tensor(cw[:, :, :], c2[:, :, 0], c2[:, :, 1], ALU.add))
            dve.wait_ge(cleared.sem, cleared(2))
            then(nc.vector.tensor_copy(cp[:, :, 0:E].bitcast(F32R), cw[:, :, :]))
            then(nc.vector.tensor_tensor(cp[:, :, D:D + E], cw[:, :, :], cp[:, :, 0:E], ALU.subtract))
            assert count[0] == last_step
            for g in range(0, G, 2):
                dve.wait_ge(turned.sem, turned(g + 1))
                nc.vector.tensor_copy(tw.ct[:, BANK * g:BANK * g + BANK], ps[:, 1 + g, :])
    made.passed(1)
    step.passed(count[0])
    ex.passed(ex_count)
    cleared.passed(2)
    turned.passed(G)




def swiglu_experts_stage(tw, h, later):
    nc, ps = tw.nc, tw.ps
    U = G * E0
    up, silu, gated, hid_ready, down = (tw.counter(x) for x in ("x0_up", "x0_silu", "x0_gated", "x0_hidden", "x0_down"))
    up2, spread = tw.counter("x0_up2"), tw.counter("x0_spread")
    y_copied, y_ready, y_added = (tw.counter(x) for x in ("x_ycopied", "x_yready", "x_yadded"))
    Y = 6
    w1, w2 = tw.early["l0_w1"], tw.early["l0_w2"]
    with ExitStack() as ctx:
        sg = tw.sb("x0_sg", [P, 2, BANK], ctx=ctx)
        gt = tw.sb("x0_gt", [P, 2, BANK], ctx=ctx)
        hid = tw.sb("x0_hid", [P, 2, BANK], ctx=ctx)
        yt = tw.sb("x0_yt", [P, 2, BANK], ctx=ctx)
        raws = [tw.sb(f"later_raw{n}", [P, src.shape[1]], ctx=ctx) for n, (src, _, _) in enumerate(later)]
        block = ctx.enter_context(nc.Block())

        @block.sync
        def _(sp):
            for raw, (src, _, _) in zip(raws, later):
                for half in range(2):
                    sp.dma_start(raw[64 * half:64 * half + 64, :], src).then_inc(tw.later_landed, 16)

        @block.gpsimd
        def _(pool):
            pool.wait_ge(tw.later_landed, 32 * len(later))
            for n, (raw, (_, hi, lo)) in enumerate(zip(raws, later)):
                pool.tensor_scalar(hi[:, :], raw[:, :], 1.0, 1.0, ALU.mult, ALU.mult).then_inc(tw.later_hi, 1)
                pool.wait_ge(tw.later_hi, n + 1)
                pool.tensor_tensor(lo[:, :], raw[:, :], hi[:, :].bitcast(F32), ALU.subtract)

        @block.tensor
        def _(pe):
            for i in range(U + 4):
                if i < U:
                    t, e = i // E0, i % E0
                    cols = slice(t * BANK, (t + 1) * BANK)
                    for k, w, read, ready in ((0, w1, silu, up), (2, w2, gated, up2)):
                        if i >= 2:
                            pe.wait_ge(read.sem, read(i - 1))
                        for n, part in enumerate((tw.early_hi, tw.early_lo)):
                            mm = nc.tensor.matmul(ps[:, k + i % 2, :], part[:, w.start + e * H0:w.start + e * H0 + H0],
                                                  tw.xt[:, cols], start=(n == 0), stop=(n == 1))
                        mm.then_inc(ready.sem, 1)
                u = i - 2
                if 0 <= u < U:
                    t, e = u // E0, u % E0
                    pe.wait_ge(hid_ready.sem, hid_ready(u + 1))
                    if e == 0 and t >= 2:
                        pe.wait_ge(y_added.sem, y_added(t - 1))
                    half = 64 * (e % 2)
                    nc.tensor.matmul(ps[half:half + 64, Y + t % 2, :], tw.w("l0_w3")[:, e * D:(e + 1) * D],
                                     hid[:, u % 2, :], start=(e < 2), stop=(e >= E0 - 2)).then_inc(down.sem, 1)
                if i < U:
                    t, e = i // E0, i % E0
                    nc.tensor.matmul(ps[:, 4 + i % 2, :], tw.sel128[:, e, :], tw.ct[:, t * BANK:(t + 1) * BANK],
                                     start=True, stop=True).then_inc(spread.sem, 1)
                t = (i - 3) // E0 - 1
                if (i - 3) % E0 == 0 and 0 <= t < G:
                    pe.wait_ge(y_copied.sem, y_copied(t + 1))
                    for k in range(TPG):
                        mm = nc.tensor.matmul(ps[:, Y + t % 2, k * D:(k + 1) * D], yt[:, t % 2, k * P:(k + 1) * P],
                                              tw.w("fold"), start=True, stop=True)
                    mm.then_inc(y_ready.sem, 1)

        @block.scalar
        def _(act):
            for i in range(U + 4):
                if i < U:
                    act.wait_ge(up.sem, up(i + 1))
                    if i >= 2:
                        act.wait_ge(gated.sem, gated(i - 1))
                    nc.scalar.activation(sg[:, i % 2, :], ps[:, i % 2, :], ACT.Silu).then_inc(silu.sem, 1)
                t = (i - 2) // E0 - 1
                if (i - 2) % E0 == 0 and 0 <= t < G:
                    act.wait_ge(down.sem, down(E0 * (t + 1)))
                    nc.scalar.copy(yt[:, t % 2, :], ps[:, Y + t % 2, :]).then_inc(y_copied.sem, 1)

        @block.vector
        def _(dve):
            for i in range(U + 4):
                if i < U:
                    dve.wait_ge(silu.sem, silu(i + 1))
                    dve.wait_ge(up2.sem, up2(i + 1))
                    nc.vector.tensor_tensor(gt[:, i % 2, :], sg[:, i % 2, :], ps[:, 2 + i % 2, :], ALU.mult)\
                        .then_inc(gated.sem, 1)
                    dve.wait_ge(gated.sem, gated(i + 1))
                    dve.wait_ge(spread.sem, spread(i + 1))
                    if i >= 2:
                        dve.wait_ge(down.sem, down(i - 1))
                    nc.vector.tensor_tensor(hid[:, i % 2, :], gt[:, i % 2, :], ps[:, 4 + i % 2, :], ALU.mult)\
                        .then_inc(hid_ready.sem, 1)
                t = (i - 3) // E0 - 1
                if (i - 3) % E0 == 0 and 0 <= t < G:
                    dve.wait_ge(y_ready.sem, y_ready(t + 1))
                    rows = h[:, TPG * t:TPG * t + TPG, :]
                    nc.vector.tensor_tensor(rows, rows, ps[:, Y + t % 2, 0:TPG * D].rearrange("p (k d) -> p k d", d=D),
                                            ALU.add).then_inc(y_added.sem, 1)
    for s in (up, up2, spread, silu, gated, hid_ready, down):
        s.passed(U)
    for s in (y_copied, y_ready, y_added):
        s.passed(G)


def pair_experts_stage(tw, h, pairs, w1, b1, func, mid, w3, b3, extra, shared=None):
    nc, ps = tw.nc, tw.ps
    NS = pairs + (1 if shared else 0)
    U = G * NS
    up, act1, mid_ready, act2, hid_ready, down = (
        tw.counter(x) for x in ("xp_up", "xp_act1", "xp_mid", "xp_act2", "xp_hidden", "xp_down"))
    y_copied, y_ready, y_added, y_kept = (tw.counter(x) for x in ("x_ycopied", "x_yready", "x_yadded", "xp_kept"))
    Y = 6
    with ExitStack() as ctx:
        a1 = tw.sb("xp_a1", [P, 2, 2, BANK], ctx=ctx)
        a2 = tw.sb("xp_a2", [P, 2, BANK], ctx=ctx)
        hid = tw.sb("xp_hid", [P, 2, BANK], ctx=ctx)
        yt = tw.sb("xp_yt", [P, 2, BANK], ctx=ctx)
        block = ctx.enter_context(nc.Block())

        def is_shared(u):
            return u % NS == pairs

        routed_to = [sum(not is_shared(v) for v in range(u + 1)) for u in range(U)]
        MID, LAG = 5, (1 if mid is not None else 0)

        def spread_bank(u):
            return 4 if mid is not None else 4 + u % 2

        def ups(u):
            if is_shared(u):
                return [shared["w1"]]
            w = w1(u % NS)
            return w if isinstance(w, list) else [w]

        @block.tensor
        def _(pe):
            for i in range(U + 4):
                if i < U:
                    t = i // NS
                    cols = slice(t * BANK, (t + 1) * BANK)
                    if i >= 2:
                        pe.wait_ge(act1.sem, act1(i - 1))
                    for k, (hi, lo) in enumerate(ups(i)):
                        mm = nc.tensor.matmul(ps[:, 2 * (i % 2) + k, :], hi, tw.xt[:, cols], start=True, stop=False)
                        mm = nc.tensor.matmul(ps[:, 2 * (i % 2) + k, :], lo, tw.xt[:, cols], start=False, stop=True)
                    mm.then_inc(up.sem, 1)
                u = i - 1
                if mid is not None and 0 <= u < U:
                    pe.wait_ge(act1.sem, act1(u + 1))
                    if u >= 1:
                        if is_shared(u - 1):
                            pe.wait_ge(hid_ready.sem, hid_ready(u))
                        else:
                            pe.wait_ge(act2.sem, act2(routed_to[u - 1]))
                    if is_shared(u):
                        mm = nc.tensor.matmul(ps[:, MID, :], shared["w2"], a1[:, u % 2, 0, :], start=True, stop=True)
                    else:
                        ms = mid[0](u % NS)
                        if isinstance(ms, list):
                            for k, m in enumerate(ms):
                                mm = nc.tensor.matmul(ps[64 * k:64 * k + 64, MID, :], m, a1[:, u % 2, k, :],
                                                      start=True, stop=True)
                        else:
                            mm = nc.tensor.matmul(ps[:, MID, :], ms, a1[:, u % 2, 0, :], start=True, stop=True)
                    mm.then_inc(mid_ready.sem, 1)
                u = i - 2
                if 0 <= u < U:
                    t, q = u // NS, u % NS
                    pe.wait_ge(hid_ready.sem, hid_ready(u + 1))
                    if q == 0 and t >= 2:
                        pe.wait_ge(y_added.sem, y_added(t - 1))
                    half = 64 * (q % 2)
                    w = shared["w3"] if is_shared(u) else w3(q)
                    nc.tensor.matmul(ps[half:half + 64, Y + t % 2, :], w, hid[:, u % 2, :],
                                     start=(q < 2), stop=(q >= NS - 2)).then_inc(down.sem, 1)
                u = i - LAG
                if 0 <= u < U and not is_shared(u):
                    t, q = u // NS, u % NS
                    cols = slice(t * BANK, (t + 1) * BANK)
                    nc.tensor.matmul(ps[:, spread_bank(u), :],
                                     tw.sel64[:, 2 * q:2 * q + 2, :].rearrange("p a b -> p (a b)"),
                                     tw.ct[:, cols], start=True, stop=True).then_inc(tw.spread_ready.sem, 1)
                t = (i - 3) // NS - 1
                if (i - 3) % NS == 0 and 0 <= t < G:
                    pe.wait_ge(y_copied.sem, y_copied(t + 1))
                    for k in range(TPG):
                        dst = ps[:, Y + t % 2, k * D:(k + 1) * D]
                        nc.tensor.matmul(dst, yt[:, t % 2, k * P:(k + 1) * P], tw.w("fold"), start=True, stop=False)
                        c = t * BANK + k * P
                        mm = nc.tensor.matmul(dst, tw.ct[:, c:c + P].bitcast(F32), b3, start=False, stop=True)
                    mm.then_inc(y_ready.sem, 1)

        @block.scalar
        def _(act):
            for i in range(U + 4):
                if i < U:
                    act.wait_ge(up.sem, up(i + 1))
                    if i >= 2:
                        if mid is None:
                            act.wait_ge(hid_ready.sem, hid_ready(i - 1))
                        else:
                            act.wait_ge(mid_ready.sem, mid_ready(i - 1))
                    bs = [shared["b1"]] if is_shared(i) else b1(i % NS)
                    for k, b in enumerate(bs):
                        ins = nc.scalar.activation(a1[:, i % 2, k, :], ps[:, 2 * (i % 2) + k, :], func, bias=b)
                    ins.then_inc(act1.sem, 1)
                u = i - 1
                if mid is not None and 0 <= u < U and not is_shared(u):
                    act.wait_ge(mid_ready.sem, mid_ready(u + 1))
                    if u >= 2:
                        act.wait_ge(hid_ready.sem, hid_ready(u - 1))
                    nc.scalar.activation(a2[:, u % 2, :], ps[:, MID, :], ACT.Relu, bias=mid[1](u % NS))\
                        .then_inc(act2.sem, 1)
                t = (i - 2) // NS - 1
                if (i - 2) % NS == 0 and 0 <= t < G:
                    act.wait_ge(down.sem, down(NS * (t + 1)))
                    nc.scalar.copy(yt[:, t % 2, :], ps[:, Y + t % 2, :]).then_inc(y_copied.sem, 1)

        @block.vector
        def _(dve):
            for i in range(U + 5):
                u = i - 1
                if 0 <= u < U:
                    if u >= 2:
                        dve.wait_ge(down.sem, down(u - 1))
                    if is_shared(u):
                        dve.wait_ge(mid_ready.sem, mid_ready(u + 1))
                        nc.vector.tensor_scalar(hid[:, u % 2, :], ps[:, MID, :], shared["b2"], 0.0, ALU.add,
                                                ALU.max).then_inc(hid_ready.sem, 1)
                    else:
                        if mid is None:
                            dve.wait_ge(act1.sem, act1(u + 1))
                        else:
                            dve.wait_ge(act2.sem, act2(routed_to[u]))
                        dve.wait_ge(tw.spread_ready.sem, tw.spread_ready(routed_to[u]))
                        source = a1[:, u % 2, 0, :] if mid is None else a2[:, u % 2, :]
                        nc.vector.tensor_tensor(hid[:, u % 2, :], source, ps[:, spread_bank(u), :], ALU.mult)\
                            .then_inc(hid_ready.sem, 1)
                t = (i - 4) // NS - 1
                if (i - 4) % NS == 0 and 0 <= t < G:
                    rows = h[:, TPG * t:TPG * t + TPG, :]
                    if extra is not None:
                        nc.vector.tensor_tensor(rows, rows, extra(t), ALU.add).then_inc(y_kept.sem, 1)
                        dve.wait_ge(y_kept.sem, y_kept(t + 1))
                    dve.wait_ge(y_ready.sem, y_ready(t + 1))
                    nc.vector.tensor_tensor(rows, rows, ps[:, Y + t % 2, 0:TPG * D].rearrange("p (k d) -> p k d", d=D),
                                            ALU.add).then_inc(y_added.sem, 1)
    for s in (up, act1, hid_ready, down):
        s.passed(U)
    if mid is not None:
        mid_ready.passed(U)
        act2.passed(G * pairs)
    tw.spread_ready.passed(G * pairs)
    for s in (y_copied, y_ready, y_added):
        s.passed(G)
    if extra is not None:
        y_kept.passed(G)




def linear_attention_stage(tw, x, layer):
    nc, ps = tw.nc, tw.ps
    DH = D // HEADS2
    scale = float(DH) ** -0.25
    kp, qp, kmax, kneg, ek, ekt, ekc = (tw.counter(x) for x in (
        "la_keys", "la_qv", "la_kmax", "la_kneg", "la_ek", "la_ekt", "la_ekc"))
    vc, qm, qd, qe, qs, qi, qn = (tw.counter(x) for x in (
        "la_vc", "la_qmax", "la_qdiff", "la_qexp", "la_qsum", "la_qinv", "la_qn"))
    ctx_ready, ctx_masked, cw_ready, cw_scaled, kinv, qt, qtc, y, yb = (tw.counter(x) for x in (
        "la_ctx", "la_masked", "la_cw", "la_cws", "la_kinv", "la_qt", "la_qtc", "la_y", "la_yb"))
    k_hi, k_lo = tw.mid_hi[:, tw.mid[f"l2_k{layer}"]], tw.mid_lo[:, tw.mid[f"l2_k{layer}"]]
    qv = [p[:, tw.mid[f"l2_qv{layer}"]] for p in (tw.mid_hi, tw.mid_lo)]
    HT = NTB // 2
    with ExitStack() as ctx:
        sb = lambda name, shape: tw.sb("la_" + name, shape, ctx=ctx)
        eks = sb("ek", [P, N])
        ekts = sb("ekt", [P, NTB, P])
        vs = sb("v", [P, NTB, B, D])
        qc = sb("qc", [P, NT, D])
        qexp = sb("qexp", [P, NT, D])
        qns = sb("qn", [P, NTB, B, D])
        qts = sb("qt", [P, N])
        qmx = sb("qmx", [P, NT * HEADS2])
        qsm = sb("qsm", [P, NT * HEADS2])
        qiv = sb("qiv", [P, NT * HEADS2])
        km = sb("km", [P, 2])
        ks = sb("ks", [P, 2])
        cms = sb("cm", [P, P])
        block = ctx.enter_context(nc.Block())

        @block.tensor
        def _(pe):
            for g in range(G):
                nc.tensor.matmul(ps[:, g, :], k_hi, tw.xt[:, g * BANK:(g + 1) * BANK], start=True, stop=False)
                nc.tensor.matmul(ps[:, g, :], k_lo, tw.xt[:, g * BANK:(g + 1) * BANK], start=False, stop=True)\
                    .then_inc(kp.sem, 1)
            for g in range(G):
                for k in range(TPG):
                    t = TPG * g + k
                    for n, part in enumerate(qv):
                        mm = nc.tensor.matmul(ps[:, 4 + g, k * P:(k + 1) * P], tw.xt[:, t * P:(t + 1) * P], part,
                                              start=(n == 0), stop=(n == 1))
                mm.then_inc(qp.sem, 1)
            pe.wait_ge(ek.sem, ek(2))
            for c in range(2):
                for k in range(HT):
                    i = HT * c + k
                    mm = nc.tensor.transpose(ps[:, c, k * P:(k + 1) * P], eks[:, i * P:(i + 1) * P], tw.w("ident"))
                mm.then_inc(ekt.sem, 1)
            pe.wait_ge(ekc.sem, ekc(2))
            pe.wait_ge(vc.sem, vc(G))
            for i in range(NTB):
                mm = nc.tensor.matmul(ps[:, 2, 0:P], vs[:, i, :, :].rearrange("p b d -> p (b d)"), ekts[:, i, :],
                                      start=(i == 0), stop=(i == NTB - 1))
            mm.then_inc(ctx_ready.sem, 1)
            pe.wait_ge(qn.sem, qn(G))
            for c in range(2):
                for k in range(HT):
                    i = HT * c + k
                    mm = nc.tensor.transpose(ps[:, 4 + c, k * P:(k + 1) * P],
                                             qns[:, i, :, :].rearrange("p b d -> p (b d)"), tw.w("ident"))
                mm.then_inc(qt.sem, 1)
            pe.wait_ge(ctx_masked.sem, ctx_masked(1))
            nc.tensor.matmul(ps[:, 3, 0:D], cms[:, :], tw.w(f"l2_wo{layer}"), start=True, stop=True)\
                .then_inc(cw_ready.sem, 1)
            pe.wait_ge(cw_scaled.sem, cw_scaled(2))
            for c in range(2):
                pe.wait_ge(qtc.sem, qtc(c + 1))
                for k in range(HT):
                    i = HT * c + k
                    mm = nc.tensor.matmul(ps[:, 6 + c, k * P:(k + 1) * P], qts[:, i * P:(i + 1) * P], tw.cw_block[:, :],
                                          start=True, stop=True)
                mm.then_inc(y.sem, 1)

        @block.vector
        def _(dve):
            for b in range(B):
                r = slice(64 * b, 64 * b + 64)
                dve.wait_ge(kp.sem, kp(2 * b + 2))
                nc.vector.tensor_reduce(km[r, 0:1], ps[r, 2 * b:2 * b + 2, :], AX.XY, ALU.max, negate=True)\
                    .then_inc(kmax.sem, 1)
            dve.wait_ge(kmax.sem, kmax(2))
            nc.vector.tensor_scalar(km[:, 1:2], km[:, 0:1], scale, None, ALU.mult).then_inc(kneg.sem, 1)
            for g in range(G):
                dve.wait_ge(qp.sem, qp(g + 1))
                heads = slice(TPG * HEADS2 * g, TPG * HEADS2 * (g + 1))
                q = ps[:, 4 + g, :].rearrange("p (k c d) -> p k c d", k=TPG, c=2)[:, :, 0, :]
                q4 = q.rearrange("p k (h d) -> p k h d", d=DH)
                nc.vector.reduce_max(qmx[:, heads].rearrange("p (k h) -> p k h", k=TPG), q4, AX.X).then_inc(qm.sem, 1)
                dve.wait_ge(qm.sem, qm(g + 1))
                mx = qmx[:, heads].rearrange("p (k h) -> p k h", k=TPG).unsqueeze(3).to_broadcast([P, TPG, HEADS2, DH])
                nc.vector.tensor_tensor(qc[:, TPG * g:TPG * g + TPG, :].rearrange("p k (h d) -> p k h d", d=DH), q4, mx,
                                        ALU.subtract).then_inc(qd.sem, 1)
            for c in range(2):
                dve.wait_ge(ekt.sem, ekt(c + 1))
                nc.vector.tensor_copy(ekts[:, HT * c:HT * c + HT, :].rearrange("p k c -> p (k c)"), ps[:, c, :])\
                    .then_inc(ekc.sem, 1)
            for g in range(G):
                heads = slice(TPG * HEADS2 * g, TPG * HEADS2 * (g + 1))
                dve.wait_ge(qe.sem, qe(g + 1))
                e = qexp[:, TPG * g:TPG * g + TPG, :].rearrange("p k (h d) -> p (k h) d", d=DH)
                nc.vector.reduce_sum(qsm[:, heads], e, AX.X).then_inc(qs.sem, 1)
                dve.wait_ge(qs.sem, qs(g + 1))
                nc.vector.reciprocal(qiv[:, heads], qsm[:, heads]).then_inc(qi.sem, 1)
                dve.wait_ge(qi.sem, qi(g + 1))
                b, i0 = TPG * g // NTB, TPG * g % NTB
                dst = qns[:, i0:i0 + TPG, b, :].rearrange("p k (h d) -> p k h d", d=DH)
                iv = qiv[:, heads].rearrange("p (k h) -> p k h", k=TPG).unsqueeze(3).to_broadcast([P, TPG, HEADS2, DH])
                nc.vector.tensor_tensor(dst, qexp[:, TPG * g:TPG * g + TPG, :].rearrange("p k (h d) -> p k h d", d=DH),
                                        iv, ALU.mult).then_inc(qn.sem, 1)
            dve.wait_ge(ek.sem, ek(2))
            nc.vector.reciprocal(ks[:, 1:2], ks[:, 0:1]).then_inc(kinv.sem, 1)
            dve.wait_ge(ctx_ready.sem, ctx_ready(1))
            nc.vector.tensor_tensor(cms[:, :], ps[:, 2, 0:P], tw.w("head_mask"), ALU.mult).then_inc(ctx_masked.sem, 1)
            dve.wait_ge(kinv.sem, kinv(1))
            dve.wait_ge(cw_ready.sem, cw_ready(1))
            for b in range(B):
                r = slice(64 * b, 64 * b + 64)
                nc.vector.tensor_scalar(tw.cw_block[r, 64 * b:64 * b + 64], ps[r, 3, 0:D], ks[r, 1:2], None, ALU.mult)\
                    .then_inc(cw_scaled.sem, 1)
            for c in range(2):
                dve.wait_ge(y.sem, y(c + 1))
                dve.wait_ge(yb.sem, yb(1))
                for b in range(B):
                    rows = x[:, NTB * b + HT * c:NTB * b + HT * c + HT, :]
                    src = ps[:, 6 + c, :].rearrange("p (k b d) -> p k b d", k=HT, b=B)[:, :, b, :]
                    nc.vector.tensor_tensor(rows, rows, src, ALU.add)

        @block.scalar
        def _(act):
            act.wait_ge(kneg.sem, kneg(1))
            for b in range(B):
                r = slice(64 * b, 64 * b + 64)
                nc.scalar.activation(eks[r, :], ps[r, 2 * b:2 * b + 2, :].rearrange("p a b -> p (a b)"), ACT.Exp,
                                     bias=km[r, 1:2], scale=scale, accum_out=ks[r, 0:1]).then_inc(ek.sem, 1)
            for g in range(G):
                act.wait_ge(qd.sem, qd(g + 1))
                b, i0 = TPG * g // NTB, TPG * g % NTB
                v = ps[:, 4 + g, :].rearrange("p (k c d) -> p k c d", k=TPG, c=2)[:, :, 1, :]
                nc.scalar.copy(vs[:, i0:i0 + TPG, b, :], v).then_inc(vc.sem, 1)
                nc.scalar.activation(qexp[:, TPG * g:TPG * g + TPG, :], qc[:, TPG * g:TPG * g + TPG, :], ACT.Exp,
                                     scale=scale).then_inc(qe.sem, 1)
            for c in range(2):
                act.wait_ge(qt.sem, qt(c + 1))
                nc.scalar.copy(qts[:, c * BANK:(c + 1) * BANK], ps[:, 4 + c, :]).then_inc(qtc.sem, 1)

        @block.gpsimd
        def _(pool):
            pool.tensor_tensor(x[:, :, :], x[:, :, :], rows_over(tw.r(f"l2_bo{layer}"), NT), ALU.add)\
                .then_inc(yb.sem, 1)
    for s, n in ((kp, G), (qp, G), (kmax, 2), (kneg, 1), (ek, 2), (ekt, 2), (ekc, 2), (vc, G), (qm, G), (qd, G), (qe, G),
                 (qs, G), (qi, G), (qn, G), (ctx_ready, 1), (ctx_masked, 1), (cw_ready, 1), (cw_scaled, 2), (kinv, 1),
                 (qt, 2), (qtc, 2), (y, 2), (yb, 1)):
        s.passed(n)


def gelu_mlp_stage(tw, x, layer):
    nc, ps = tw.nc, tw.ps
    U = 2 * G
    up, gelu, y, yb, added = (tw.counter(s) for s in ("ml_up", "ml_gelu", "ml_y", "ml_yb", "ml_added"))
    w1 = tw.mid[f"l2_w1{layer}"]
    b1, w2 = tw.w(f"l2_b1{layer}"), tw.w(f"l2_w2{layer}")
    with ExitStack() as ctx:
        hid = tw.sb("ml_hid", [P, U, BANK], ctx=ctx)
        block = ctx.enter_context(nc.Block())

        @block.tensor
        def _(pe):
            for i in range(U + 3):
                if i < U:
                    t, c = i // 2, i % 2
                    if i >= 4:
                        pe.wait_ge(gelu.sem, gelu(i - 3))
                    for n, part in enumerate((tw.mid_hi, tw.mid_lo)):
                        mm = nc.tensor.matmul(ps[:, i % 4, :], part[:, w1.start + c * P:w1.start + (c + 1) * P],
                                              tw.xt[:, t * BANK:(t + 1) * BANK], start=(n == 0), stop=(n == 1))
                    mm.then_inc(up.sem, 1)
                t = (i - 4) // 2
                if i >= 4 and i % 2 == 0:
                    pe.wait_ge(gelu.sem, gelu(2 * t + 2))
                    for k in range(TPG):
                        for c in range(2):
                            mm = nc.tensor.matmul(ps[:, 4 + t, k * D:(k + 1) * D], hid[:, 2 * t + c, k * P:(k + 1) * P],
                                                  w2[:, c * D:(c + 1) * D], start=(c == 0), stop=(c == 1))
                    mm.then_inc(y.sem, 1)

        @block.scalar
        def _(act):
            for i in range(U):
                act.wait_ge(up.sem, up(i + 1))
                nc.scalar.activation(hid[:, i, :], ps[:, i % 4, :], ACT.Gelu, bias=b1[:, i % 2:i % 2 + 1])\
                    .then_inc(gelu.sem, 1)

        @block.gpsimd
        def _(pool):
            pool.tensor_tensor(x[:, :, :], x[:, :, :], rows_over(tw.r(f"l2_b2{layer}"), NT), ALU.add)\
                .then_inc(yb.sem, 1)

        @block.vector
        def _(dve):
            dve.wait_ge(yb.sem, yb(1))
            for t in range(G):
                dve.wait_ge(y.sem, y(t + 1))
                rows = x[:, TPG * t:TPG * t + TPG, :]
                nc.vector.tensor_tensor(rows, rows, ps[:, 4 + t, 0:TPG * D].rearrange("p (k d) -> p k d", d=D), ALU.add)
    for s, n in ((up, U), (gelu, U), (y, G), (yb, 1)):
        s.passed(n)




def relu_stage(tw, hi, lo, bias, dst):
    nc, ps = tw.nc, tw.ps
    made = tw.counter("re_made")
    with ExitStack() as ctx:
        block = ctx.enter_context(nc.Block())

        @block.tensor
        def _(pe):
            for g in range(G):
                cols = slice(g * BANK, (g + 1) * BANK)
                nc.tensor.matmul(ps[:, g, :], hi, tw.xt[:, cols], start=True, stop=False)
                nc.tensor.matmul(ps[:, g, :], lo, tw.xt[:, cols], start=False, stop=True).then_inc(made.sem, 1)

        @block.scalar
        def _(act):
            for g in range(G):
                act.wait_ge(made.sem, made(g + 1))
                nc.scalar.activation(dst[:, g * BANK:(g + 1) * BANK], ps[:, g, :], ACT.Relu, bias=bias)
    made.passed(G)


def scale_shift_stage(tw, x, scale, shift):
    nc = tw.nc
    with nc.Block() as block:
        @block.vector
        def _(dve):
            nc.vector.scalar_tensor_tensor(out=x[:, :, :], in0=x[:, :, :], scalar=scale, in1=rows_over(shift, NT),
                                           op0=ALU.mult, op1=ALU.add)


def add_stage(tw, x, y):
    nc = tw.nc
    with nc.Block() as block:
        @block.vector
        def _(dve):
            nc.vector.tensor_tensor(x[:, :, :], x[:, :, :], y, ALU.add)


def score_matrices_stage(tw, qk, a_hi, a_lo):
    nc, ps = tw.nc, tw.ps
    landed, made, hi_made = (tw.counter(x) for x in ("sm_landed", "sm_made", "sm_hi"))
    with ExitStack() as ctx:
        w = tw.sb("sm_qk", [P, 2, HEADS // 2, P], ctx=ctx)
        block = ctx.enter_context(nc.Block())

        @block.sync
        def _(sp):
            sp.dma_start(w[:, :, :, :].rearrange("p a b c -> p (a b c)"), qk).then_inc(landed.sem, 16)

        @block.tensor
        def _(pe):
            pe.wait_ge(landed.sem, landed(16))
            for hd in range(HEADS):
                r = slice(64 * (hd % 2), 64 * (hd % 2) + 64)
                mm = nc.tensor.matmul(ps[:, hd, 0:P], w[r, 0, hd // 2, :], w[r, 1, hd // 2, :], start=True, stop=True)
                mm.then_inc(made.sem, 1)

        @block.scalar
        def _(act):
            act.wait_ge(made.sem, made(HEADS))
            nc.scalar.copy(a_hi[:, :, :], ps[:, :, 0:P]).then_inc(hi_made.sem, 1)

        @block.vector
        def _(dve):
            dve.wait_ge(hi_made.sem, hi_made(1))
            nc.vector.tensor_tensor(a_lo[:, :, :], ps[:, :, 0:P], a_hi[:, :, :].bitcast(F32), ALU.subtract)
    landed.passed(16)
    made.passed(HEADS)
    hi_made.passed(1)


def vit_tower_kernel(nc, x, wk, early, mid, late, full, row, toeplitz, qk, out, upto=99):
    with ExitStack() as ctx:
        tw = Tower(nc, ctx)
        tw.ps = ctx.enter_context(nc.psum_tensor("ps", [P, 8, BANK], F32))
        h = tw.h = tw.sb("h", [P, NT, D])
        tw.xt = tw.sb("xt", [P, T], F32R)
        tw.w_full = tw.sb("w_full", [P, tw.full.n])
        tw.w_row = tw.sb("w_row", [P, tw.row.n])
        tw.minus_half = tw.sb("minus_half", [P, NT])
        tw.late_hi = tw.sb("late_hi", [P, tw.late.n], F32R)
        tw.late_lo = tw.sb("late_lo", [P, tw.late.n], F32R)
        tw.early_landed, tw.full_landed, tw.row_landed, tw.later_landed, tw.later_hi, tw.strips_landed, tw.out_landed = (
            nc.alloc_semaphore(name) for name in ("early_landed", "full_landed", "row_landed", "later_landed",
                                                  "later_hi", "strips_landed", "out_landed"))
        tw.spread_ready = tw.counter("xp_spread")

        def xt_tile(t):
            return tw.xt[:, t * P:(t + 1) * P]

        def parts(pack, lay, name):
            hi, lo = pack
            return hi[:, lay[name]], lo[:, lay[name]]

        mids = ctx.enter_context(ExitStack())
        tw.xn = tw.sb("xn", [P, NT, D], ctx=mids)
        tw.mid_hi = tw.sb("mid_hi", [P, tw.mid.n], F32R, ctx=mids)
        tw.mid_lo = tw.sb("mid_lo", [P, tw.mid.n], F32R, ctx=mids)
        MID, LATE = (tw.mid_hi, tw.mid_lo), (tw.late_hi, tw.late_lo)

        with ExitStack() as l0:
            tw.early_hi = tw.sb("early_hi", [P, tw.early.n], F32R, ctx=l0)
            tw.early_lo = tw.sb("early_lo", [P, tw.early.n], F32R, ctx=l0)
            EARLY = (tw.early_hi, tw.early_lo)
            embed_stage(tw, x, wk, early, full, row)
            if upto >= 1:
                norm_stage(tw, h, keep=tw.xn)
                with ExitStack() as at:
                    qh = tw.sb("a0_qh", [P, T], F32R, ctx=at)
                    ql = tw.sb("a0_ql", [P, T], F32R, ctx=at)
                    wh, wl = parts(EARLY, tw.early, "l0_attn")
                    project_stage(tw, [(wh, wl, g * BANK, None, "queries",
                                        (qh[:, g * BANK:(g + 1) * BANK], ql[:, g * BANK:(g + 1) * BANK]))
                                       for g in range(G)])
                    groups = [((0, 1), [b * N + nh * BANK for b in range(B)], [b * N for b in range(B)], 4 * nh)
                              for nh in range(2)]
                    attention_stage(tw, "a0", groups, 1.0 / 8.0, lambda g, j: qh, lambda g, j: ql, tw.xt,
                                    lambda m, w: tw.xn[:, NTB * m + w, :], lambda g: tw.w("ident"), None, "add",
                                    lambda g, j: h[:, NTB * j + 4 * g:NTB * j + 4 * g + 4, :])
            if upto >= 2:
                norm_stage(tw, h)
                tw.ct = tw.sb("ct0", [P, T], F32R, ctx=l0)
                tw.sel128 = tw.sb("sel128", [P, E0, H0], F32R, ctx=l0)
                route_stage(tw, E0, xt_tile, parts(EARLY, tw.early, "l0_gate"), tw.r("l0_gate_b"), False,
                            tw.sel128)
                swiglu_experts_stage(tw, h, [(mid, tw.mid_hi, tw.mid_lo), (late, tw.late_hi, tw.late_lo)])

        if upto >= 3:
            with ExitStack() as l1:
                strips = tw.sb("bias_strips", [P, 3, 7 * P], ctx=l1)
                load_strips_stage(tw, toeplitz, strips)
                norm_stage(tw, h, keep=tw.xn, turn=False)
                norm_stage(tw, tw.xn, tw.r("l1_ln1_g"), tw.r("l1_ln1_b"), keep=tw.xn)
                qh = tw.sb("a1_qh", [P, T], F32R, ctx=l1)
                ql = tw.sb("a1_ql", [P, T], F32R, ctx=l1)
                kk = tw.sb("a1_k", [P, T], F32R, ctx=l1)
                vt = tw.sb("a1_v", [P, NT, D], ctx=l1)
                ob = tw.sb("a1_out", [P, NT, D], ctx=l1)
                jobs = []
                for g in range(G):
                    cols = slice(g * BANK, (g + 1) * BANK)
                    jobs.append((*parts(MID, tw.mid, "l1_q"), g * BANK, tw.w("l1_qb"), "queries",
                                 (qh[:, cols], ql[:, cols])))
                    jobs.append((*parts(MID, tw.mid, "l1_k"), g * BANK, tw.w("l1_kb"), "keys", (kk[:, cols],)))
                project_stage(tw, jobs)
                value_stage(tw, *parts(MID, tw.mid, "l1_v"), D, range(NT), lambda t: vt[:, t, :], tw.r("l1_vb"))
                groups = [((0, 1), [b * N + nh * BANK for b in range(B)], [b * N for b in range(B)], 4 * nh)
                          for nh in range(2)]
                attention_stage(tw, "a1", groups, 1.0, lambda g, j: qh, lambda g, j: ql, kk,
                                lambda m, w: vt[:, NTB * m + w, :], lambda g: tw.w("l1_post"), strips, "store",
                                lambda g, j: ob[:, NTB * j + 4 * g:NTB * j + 4 * g + 4, :])
                scale_shift_stage(tw, ob, tw.r("l1_scale"), tw.r("l1_proj_b"))
                norm_stage(tw, ob, tw.r("l1_ln2_g"), tw.r("l1_ln2_b"), keep=ob, turn=False)
                add_stage(tw, h, ob[:, :, :])
        if upto >= 4:
            with ExitStack() as f1:
                tw.ct = tw.sb("ct1", [P, T], F32R, ctx=f1)
                tw.sel64 = tw.sb("sel64_1", [P, E1, D], F32R, ctx=f1)
                norm_stage(tw, h, keep=tw.xn)
                route_stage(tw, E1, xt_tile, parts(MID, tw.mid, "l1_gate"), None, False, tw.sel64)
                w1 = tw.mid["l1_w1"].start
                pair_experts_stage(
                    tw, h, E1 // 2,
                    lambda q: tuple(p[:, w1 + q * P:w1 + (q + 1) * P] for p in MID),
                    lambda q: [tw.w("l1_b1")[:, q:q + 1]], ACT.Gelu, None,
                    lambda q: tw.w("l1_w2")[:, q * D:(q + 1) * D], tw.w("l1_b2"),
                    lambda t: tw.xn[:, TPG * t:TPG * t + TPG, :])

        if upto >= 5:
            with ExitStack() as l2:
                x2 = tw.sb("x2", [P, NT, D], ctx=l2)
                tw.cw_block = tw.sb("cw_block", [P, P], ctx=l2)
                clear_stage(tw, tw.cw_block)
                norm_stage(tw, h, keep=x2, turn=False)
                for layer in range(LAYERS):
                    norm_stage(tw, x2, tw.r(f"l2_ln1_g{layer}"), tw.r(f"l2_ln1_b{layer}"), keep=tw.xn)
                    linear_attention_stage(tw, x2, layer)
                    norm_stage(tw, x2, tw.r(f"l2_ln2_g{layer}"), tw.r(f"l2_ln2_b{layer}"), keep=tw.xn)
                    gelu_mlp_stage(tw, x2, layer)
                add_stage(tw, h, x2[:, :, :])
        if upto >= 6:
            with ExitStack() as f2:
                tw.ct = tw.sb("ct2", [P, T], F32R, ctx=f2)
                tw.sel64 = tw.sb("sel64_2", [P, E2, D], F32R, ctx=f2)
                rh = tw.sb("router_hidden", [P, T], ctx=f2)
                norm_stage(tw, h)
                relu_stage(tw, *parts(MID, tw.mid, "l2_router"), tw.w("l2_rb1"), rh)
                route_stage(tw, E2, lambda t: rh[:, t * P:(t + 1) * P], tw.w("l2_rw2"), tw.r("l2_rb2"), True,
                            tw.sel64)
                w1 = tw.mid["l2_e1"].start
                pair_experts_stage(
                    tw, h, E2 // 2,
                    lambda q: tuple(p[:, w1 + q * P:w1 + (q + 1) * P] for p in MID),
                    lambda q: [tw.w("l2_eb1")[:, q:q + 1]], ACT.Relu,
                    (lambda q: tw.w("l2_e2")[:, q * P:(q + 1) * P], lambda q: tw.w("l2_eb2")[:, q:q + 1]),
                    lambda q: tw.w("l2_e3")[:, q * D:(q + 1) * D], tw.w("l2_eb3"), None)
        mids.close()

        tw.xn = tw.sb("xn3", [P, NT, D]) if upto >= 7 else None
        if upto >= 7:
            norm_stage(tw, h)
            with ExitStack() as l3:
                a_hi = tw.sb("a3_hi", [P, HEADS, P], F32R, ctx=l3)
                a_lo = tw.sb("a3_lo", [P, HEADS, P], F32R, ctx=l3)
                score_matrices_stage(tw, qk, a_hi, a_lo)
                qh = tw.sb("a3_qh", [P, 2 * PREPARED, BANK], F32R, ctx=l3)
                ql = tw.sb("a3_ql", [P, 2 * PREPARED, BANK], F32R, ctx=l3)
                vt = tw.sb("a3_v", [P, NT, HEADS * D], ctx=l3)
                pairs = HEADS // 2
                groups = [((HEADS * b + 2 * k, HEADS * b + 2 * k + 1), [0, 0], [b * N, b * N], 4 * nh)
                          for b in range(B) for nh in range(2) for k in range(pairs)]

                def project(g, j):
                    m = 2 * (g % pairs) + j
                    return (a_hi[:, m, :], a_lo[:, m, :]), g // pairs * BANK

                def queries(which):
                    return lambda g, j: which[:, 2 * (g % PREPARED) + j, :]

                q_hi, q_lo = queries(qh), queries(ql)
                value_stage(tw, *parts(LATE, tw.late, "l3_v"), HEADS * D, range(NT), lambda t: vt[:, t, :])
                jobs = [(project(g, j), "queries", (q_hi(g, j), q_lo(g, j))) for g in range(PREPARED) for j in range(2)]
                project_stage(tw, [(*w, c, None, kind, dst) for (w, c), kind, dst in jobs])
                attention_stage(tw, "a3", groups, float(1.0 / np.sqrt(D / HEADS).astype(np.float32)),
                                q_hi, q_lo, tw.xt,
                                lambda m, w: vt[:, NTB * (m // HEADS) + w, (m % HEADS) * D:(m % HEADS + 1) * D],
                                lambda g: tw.w("l3_post")[:, g % pairs * P:(g % pairs + 1) * P], None, "add",
                                lambda g, j: h[:, TPG * (g // pairs):TPG * (g // pairs) + TPG, :], project)
            add_stage(tw, h, rows_over(tw.r("l3_bout"), NT))
        if upto >= 8:
            with ExitStack() as f3:
                tw.ct = tw.sb("ct3", [P, T], F32R, ctx=f3)
                tw.sel64 = tw.sb("sel64_3", [P, E3, D], F32R, ctx=f3)
                norm_stage(tw, h)
                route_stage(tw, E3, xt_tile, parts(LATE, tw.late, "l3_gate"), tw.r("l3_gate_b"), True,
                            tw.sel64)
                w1 = tw.late["l3_e1"].start
                pair_experts_stage(
                    tw, h, E3 // 2,
                    lambda q: [tuple(p[:, w1 + e * P:w1 + (e + 1) * P] for p in LATE) for e in (2 * q, 2 * q + 1)],
                    lambda q: [tw.w("l3_eb1")[:, e:e + 1] for e in (2 * q, 2 * q + 1)], ACT.Relu,
                    (lambda q: [tw.w("l3_e2")[:, e * D:(e + 1) * D] for e in (2 * q, 2 * q + 1)],
                     lambda q: tw.w("l3_eb2")[:, q:q + 1]),
                    lambda q: tw.w("l3_e3")[:, q * D:(q + 1) * D], tw.w("l3_eb3"),
                    lambda t: rows_over(tw.r("l3_sb3"), TPG),
                    shared=dict(w1=parts(LATE, tw.late, "l3_s1"), b1=tw.w("l3_sb1"), w2=tw.w("l3_s2"),
                                b2=tw.w("l3_sb2"), w3=tw.w("l3_s3")))
        store_stage(tw, h, out)


def load_strips_stage(tw, toeplitz, strips):
    nc = tw.nc
    with nc.Block() as block:
        @block.sync
        def _(sp):
            sp.dma_start(strips[:, :, :], toeplitz).then_inc(tw.strips_landed, 16)
            sp.wait_ge(tw.strips_landed, 16)


def clear_stage(tw, tile):
    with tw.nc.Block() as block:
        @block.vector
        def _(dve):
            tw.nc.vector.memset(tile[:, :], 0.0)


def store_stage(tw, h, out):
    with tw.nc.Block() as block:
        @block.sync
        def _(sp):
            for b in range(B):
                sp.dma_start(out[b].rearrange("(v p k) j -> p v (k j)", v=4, k=2),
                             h[:, NTB * b:NTB * (b + 1), :].rearrange("p (v k) j -> p v (k j)", k=2))\
                    .then_inc(tw.out_landed, 16)
            sp.wait_ge(tw.out_landed, 16 * B)




def twice(a):
    return np.concatenate([a, a], axis=-1)


def pad_to(a, rows, cols):
    out = np.zeros((rows, cols), a.dtype)
    out[:a.shape[0], :a.shape[1]] = a
    return out


def blocks_of(a, b):
    out = np.zeros((a.shape[0] + b.shape[0], a.shape[1] + b.shape[1]), a.dtype)
    out[:a.shape[0], :a.shape[1]] = a
    out[a.shape[0]:, a.shape[1]:] = b
    return out


def side_by_side(a):
    return np.concatenate(list(a), axis=1)


def stacked_pairs(a):
    return np.concatenate([np.concatenate([a[i], a[i + 1]], 0) for i in range(0, len(a), 2)], 1)


def pair_columns(a):
    return np.ascontiguousarray(a.reshape(len(a) // 2, 2 * D).T)


def by_expert(a):
    out = np.zeros((P, a.shape[1]), a.dtype)
    out[:len(a)] = a
    out[D:D + len(a)] = a
    return out


def pack(layout, parts, rows):
    f = np.zeros((rows, layout.n), np.float32)
    for name, a in parts.items():
        c = layout[name]
        assert a.shape == (rows, c.stop - c.start), (name, a.shape)
        f[:, c] = a
    assert set(parts) == set(layout.at)
    return f


def lay_out(i):
    k, t = np.arange(FREQ)[:, None], np.arange(PATCH)[None, :]
    nf = FREQ // 2
    dft = np.where(k < nf, np.cos(2 * np.pi * k * t / PATCH), -np.sin(2 * np.pi * (k - nf) * t / PATCH))
    dft = (dft / np.sqrt(PATCH)).astype(np.float32)
    w = pad_to(i["L0_tok_W"], TAP_SETS * TAP_FEATURES, FREQ * C).reshape(TAP_SETS, TAP_ROWS, C)
    spread = np.zeros((TAP_FEATURES, FREQ, 2, TAP_FEATURES, 2, 4), np.float32)
    for j in range(TAP_FEATURES):
        spread[j, :, :, j] = dft.reshape(FREQ, 2, 2, 4).transpose(0, 2, 1, 3)
    arrays = {"x": i["x"], "wk": np.concatenate([w.transpose(1, 0, 2).reshape(TAP_ROWS, TAP_SETS * C),
                                                 spread.reshape(TAP_ROWS, -1)], 1)}
    arrays["early"] = pack(split_layout_early(), {
        "l0_attn": twice(i["L0_attn_W"]), "l0_gate": i["L0_ffn_gate_w"],
        "l0_w1": side_by_side(i["L0_ffn_w1"]), "l0_w2": side_by_side(i["L0_ffn_w2"])}, D)
    qkv, qkvb = i["L1_attn_qkv_w"], i["L1_attn_qkv_b"]
    mid = {"l1_q": twice(qkv[:, 0:D]), "l1_k": twice(qkv[:, D:2 * D]), "l1_v": qkv[:, 2 * D:3 * D],
           "l1_gate": i["L1_ffn_router_w"].T, "l1_w1": side_by_side(i["L1_ffn_w1"]),
           "l2_router": pad_to(i["L2_ffn_router_w1"], D, P), "l2_e1": side_by_side(i["L2_ffn_expert_w1"])}
    for n in range(LAYERS):
        mid[f"l2_k{n}"] = twice(i["L2_attn_Wk"][n])
        mid[f"l2_qv{n}"] = np.concatenate([i["L2_attn_Wq"][n], i["L2_attn_Wv"][n]], 1)
        mid[f"l2_w1{n}"] = i["L2_attn_W1"][n]
    arrays["mid"] = pack(split_layout_mid(), mid, D)
    arrays["late"] = pack(split_layout_late(), {
        "l3_v": i["L3_attn_WV"], "l3_gate": i["L3_ffn_gW"], "l3_s1": pad_to(i["L3_ffn_sW1"], D, P),
        "l3_e1": side_by_side(i["L3_ffn_eW1"])}, D)
    eye = np.eye(P, dtype=np.float32)
    row, col = np.arange(P)[:, None], np.arange(P)[None, :]
    full = {"ident": eye, "fold": eye[:, :D] + eye[:, D:],
            "expert_rows": (row % D == np.arange(E0)[None, :]).astype(np.float32),
            "iota": np.broadcast_to(np.arange(16, dtype=np.float32), (P, 16)),
            "head_mask": (row // HEADS2 == col // HEADS2).astype(np.float32),
            "l0_w3": side_by_side(i["L0_ffn_w3"]),
            "l1_qb": twice(qkvb[0:D])[:, None], "l1_kb": twice(qkvb[D:2 * D])[:, None],
            "l1_post": blocks_of(i["L1_attn_proj_w"], i["L1_attn_proj_w"]),
            "l1_w2": stacked_pairs(i["L1_ffn_w2"]), "l1_b1": pair_columns(i["L1_ffn_b1"]),
            "l1_b2": by_expert(i["L1_ffn_b2"]),
            "l2_rb1": pad_to(i["L2_ffn_router_b1"][:, None], P, 1), "l2_rw2": pad_to(i["L2_ffn_router_w2"], P, E2),
            "l2_e2": side_by_side([blocks_of(i["L2_ffn_expert_w2"][e], i["L2_ffn_expert_w2"][e + 1])
                                   for e in range(0, E2, 2)]),
            "l2_e3": stacked_pairs(i["L2_ffn_expert_w3"]), "l2_eb1": pair_columns(i["L2_ffn_expert_b1"]),
            "l2_eb2": pair_columns(i["L2_ffn_expert_b2"]), "l2_eb3": by_expert(i["L2_ffn_expert_b3"]),
            "l3_post": side_by_side([blocks_of(i["L3_attn_Wout"][P * k:P * k + D], i["L3_attn_Wout"][P * k + D:P * k + P])
                                     for k in range(HEADS // 2)]),
            "l3_s2": pad_to(i["L3_ffn_sW2"], P, P), "l3_s3": i["L3_ffn_sW3"],
            "l3_sb1": pad_to(i["L3_ffn_sb1"][:, None], P, 1), "l3_sb2": i["L3_ffn_sb2"][:, None],
            "l3_e2": side_by_side(i["L3_ffn_eW2"]), "l3_e3": stacked_pairs(i["L3_ffn_eW3"]),
            "l3_eb1": i["L3_ffn_eb1"].T, "l3_eb2": pair_columns(i["L3_ffn_eb2"]), "l3_eb3": by_expert(i["L3_ffn_eb3"])}
    for n in range(LAYERS):
        full[f"l2_wo{n}"] = np.concatenate([i["L2_attn_Wo"][n]] * 2, 0)
        full[f"l2_w2{n}"] = np.concatenate([i["L2_attn_W2"][n][0:P], i["L2_attn_W2"][n][P:FF]], 1)
        full[f"l2_b1{n}"] = i["L2_attn_b1"][n].reshape(2, P).T
    arrays["full"] = pack(full_layout(), full, P)
    rows = {"l0_gate_b": i["L0_ffn_gate_b"], "l1_vb": qkvb[2 * D:], "l1_scale": i["L1_attn_scale"].reshape(1),
            "l1_proj_b": i["L1_attn_proj_b"], "l2_rb2": i["L2_ffn_router_b2"], "l3_bout": i["L3_attn_bout"],
            "l3_sb3": i["L3_ffn_sb3"], "l3_gate_b": i["L3_ffn_gb"]}
    for n in ("ln1_g", "ln1_b", "ln2_g", "ln2_b"):
        rows["l1_" + n] = i["L1_attn_" + n]
    for k in range(LAYERS):
        for n in ("ln1_g", "ln1_b", "bo", "ln2_g", "ln2_b", "b2"):
            rows[f"l2_{n}{k}"] = i["L2_attn_" + n][k]
    arrays["row"] = pack(row_layout(), {k: v[None, :] for k, v in rows.items()}, 1)[0]
    p, q, c = (np.arange(n) for n in (P, 3, 7 * P))
    distance = 2 * (c[None, None, :] - 3 * P - p[:, None, None]) + q[None, :, None] - 1
    arrays["toeplitz"] = i["L1_attn_bias_table"][np.minimum(distance + N - 1, len(i["L1_attn_bias_table"]) - 1)]

    def head_rows(w):
        t = w.T.reshape(HEADS // 2, P, D).transpose(1, 0, 2)
        return twice(t).reshape(P, HEADS // 2 * P)

    arrays["qk"] = np.concatenate([head_rows(i["L3_attn_WQ"]), head_rows(i["L3_attn_WK"])], 1)
    return {k: np.ascontiguousarray(v) for k, v in arrays.items()}


def kernel(**inputs):
    import concourse.bacc as _bacc
    from concourse.bass_utils import run_bass_kernel_spmd as _run

    arrays = lay_out({k: np.asarray(v) for k, v in inputs.items()})
    nc = _bacc.Bacc("TRN2", target_bir_lowering=False, num_devices=1)
    args = {k: nc.dram_tensor("in_" + k, a.shape, mybir.dt.from_np(a.dtype), kind="ExternalInput").ap()
            for k, a in arrays.items()}
    out = nc.dram_tensor("out_h", (B, N, D), F32, kind="ExternalOutput").ap()
    vit_tower_kernel(nc, out=out, **args)
    r = _run(nc, [{"in_" + k: a for k, a in arrays.items()}], core_ids=[0])
    return r.results[0]["out_h"]
```

```python
from contextlib import ExitStack

import numpy as np
import concourse.bass as bass
from concourse import mybir

F32 = mybir.dt.float32
F32R = mybir.dt.float32r
U32 = mybir.dt.uint32
ACT = mybir.ActivationFunctionType
ALU = mybir.AluOpType
AX = mybir.AxisListType

P = 128
B, C, TIME, V = 2, 64, 128, 64
D = 64
PATCH, STRIDE = 16, 8
NPATCH = TIME // STRIDE
N = V * NPATCH
T = B * N
NT = T // P
NTB = NT // B
BANK = 512
G = T // BANK
TPG = BANK // P
FREQ = 2 * (PATCH // 2 + 1)
TAP_FEATURES = P // FREQ
TAP_ROWS = TAP_FEATURES * FREQ
TAP_SETS = -(-D // TAP_FEATURES)
EPS = 1e-5
E0, H0 = 16, 128
E1 = 8
LAYERS, FF, HEADS2 = 4, 256, 8
E2, R2 = 6, 32
HEADS = 8
E3 = 4
PREPARED = 4
W2P = 2 * E2


class Layout:

    def __init__(self):
        self.at, self.n = {}, 0

    def add(self, name, cols):
        self.at[name] = (self.n, self.n + cols)
        self.n += cols

    def __getitem__(self, name):
        return slice(*self.at[name])


def split_layout_early():
    w = Layout()
    w.add("l0_attn", 128)
    w.add("l0_gate", E0)
    w.add("l0_w1", E0 * H0)
    w.add("l0_w2", E0 * H0)
    return w


def split_layout_mid():
    w = Layout()
    w.add("l1_q", 128)
    w.add("l1_k", 128)
    w.add("l1_v", 64)
    w.add("l1_gate", E1)
    w.add("l1_w1", E1 * D)
    for i in range(LAYERS):
        w.add(f"l2_k{i}", 128)
        w.add(f"l2_qv{i}", 128)
        w.add(f"l2_w1{i}", FF)
    w.add("l2_router", 128)
    w.add("l2_e1", E2 * D)
    return w


def split_layout_late():
    w = Layout()
    w.add("l3_v", HEADS * D)
    w.add("l3_gate", E3)
    w.add("l3_s1", 128)
    w.add("l3_e1", E3 * 128)
    return w


def full_layout():
    w = Layout()
    w.add("ident", 128)
    w.add("fold", D)
    w.add("expert_rows", E0)
    w.add("iota", 16)
    w.add("head_mask", 128)
    w.add("l0_w3", E0 * D)
    w.add("l1_qb", 1)
    w.add("l1_kb", 1)
    w.add("l1_post", 128)
    w.add("l1_w2", E1 // 2 * D)
    w.add("l1_b1", E1 // 2)
    w.add("l1_b2", D)
    for i in range(LAYERS):
        w.add(f"l2_wo{i}", D)
        w.add(f"l2_w2{i}", 2 * D)
        w.add(f"l2_b1{i}", 2)
    w.add("l2_rb1", 1)
    w.add("l2_rw2", E2)
    w.add("l2_e2", E2 // 2 * 128)
    w.add("l2_e3", E2 // 2 * D)
    w.add("l2_eb1", E2 // 2)
    w.add("l2_eb2", E2 // 2)
    w.add("l2_eb3", D)
    w.add("l3_post", HEADS // 2 * 128)
    w.add("l3_s2", 128)
    w.add("l3_s3", D)
    w.add("l3_sb1", 1)
    w.add("l3_sb2", 1)
    w.add("l3_e2", E3 * D)
    w.add("l3_e3", E3 // 2 * D)
    w.add("l3_eb1", E3)
    w.add("l3_eb2", E3 // 2)
    w.add("l3_eb3", D)
    return w


def row_layout():
    w = Layout()
    w.add("l0_gate_b", E0)
    for x in ("ln1_g", "ln1_b", "vb", "proj_b", "ln2_g", "ln2_b"):
        w.add("l1_" + x, D)
    w.add("l1_scale", 1)
    for i in range(LAYERS):
        for x in ("ln1_g", "ln1_b", "bo", "ln2_g", "ln2_b", "b2"):
            w.add(f"l2_{x}{i}", D)
    w.add("l2_rb2", E2)
    w.add("l3_bout", D)
    w.add("l3_sb3", D)
    w.add("l3_gate_b", E3)
    return w


class Signal:

    def __init__(self, nc, name):
        self.sem, self.base = nc.alloc_semaphore(name), 0

    def __call__(self, n):
        return self.base + n

    def passed(self, n):
        self.base += n


def wide(ap, n):
    return ap.unsqueeze(2).to_broadcast([ap.shape[0], ap.shape[1], n])


def rows_over(ap, n):
    return ap.unsqueeze(1).to_broadcast([ap.shape[0], n, ap.shape[1]])


class Tower:

    def __init__(self, nc, ctx):
        self.nc, self.ctx, self.counters, self.named = nc, ctx, {}, {}
        self.full, self.row = full_layout(), row_layout()
        self.early, self.mid, self.late = split_layout_early(), split_layout_mid(), split_layout_late()

    def sb(self, name, shape, dt=F32, ctx=None):
        self.named[name] = self.named.get(name, 0) + 1
        if self.named[name] > 1:
            name = f"{name}_{self.named[name]}"
        return (ctx or self.ctx).enter_context(self.nc.sbuf_tensor(name, shape, dt))

    def counter(self, name):
        if name not in self.counters:
            self.counters[name] = Signal(self.nc, name)
        return self.counters[name]

    def w(self, name):
        return self.w_full[:, self.full[name]]

    def r(self, name):
        return self.w_row[:, self.row[name]]




def embed_stage(tw, x, wk, early, full, row):
    nc, h = tw.nc, tw.h
    NB = NPATCH + 1
    wk_landed = nc.alloc_semaphore("wk_landed")
    x_landed = [nc.alloc_semaphore(f"x_landed{b}") for b in range(B)]
    taps_ready = nc.alloc_semaphore("taps_ready")
    taps_copied = nc.alloc_semaphore("taps_copied")
    conv_ready = nc.alloc_semaphore("conv_ready")
    conv_copied = nc.alloc_semaphore("conv_copied")
    turned = nc.alloc_semaphore("embed_turned")
    hi_made = nc.alloc_semaphore("early_hi_made")
    with ExitStack() as ctx:
        xs = tw.sb("series", [P, B, NB, 4, V], ctx=ctx)
        wks = tw.sb("wk_rows", [TAP_ROWS, TAP_SETS * C + PATCH * TAP_FEATURES], ctx=ctx)
        taps = tw.sb("taps", [P, 2, 4, D], ctx=ctx)
        ht = tw.sb("embed_t", [P, B, V, NPATCH // 2], ctx=ctx)
        raw = tw.sb("early_raw", [P, tw.early.n], ctx=ctx)

        def piece(k):
            return slice(k * tw.early.n // 8, (k + 1) * tw.early.n // 8)

        block = ctx.enter_context(nc.Block())

        @block.sync
        def _(sp):
            sp.dma_start(wks[:, :], wk).then_inc(wk_landed, 16)
            for b in range(B):
                blocks = x[b].rearrange("c (m u s) v -> u c m (s v)", u=2, s=4)
                for u in range(2):
                    rows = xs[64 * u:64 * u + 64, b]
                    sp.dma_start(rows[:, 0:NPATCH].rearrange("c m s v -> c m (s v)"),
                                 blocks[u]).then_inc(x_landed[b], 16)
                    sp.dma_start(rows[:, NPATCH], x[b, :, TIME - 1:TIME, :].to_broadcast([C, 4, V]))\
                        .then_inc(x_landed[b], 16)
            sp.dma_start(tw.w_full[:, :], full).then_inc(tw.full_landed, 16)
            for half in range(2):
                sp.dma_start(raw[64 * half:64 * half + 64, :], early).then_inc(tw.early_landed, 16)
            sp.dma_start(tw.w_row[:, :], row.partition_broadcast(P)).then_inc(tw.row_landed, 16)

        @block.gpsimd
        def _(pool):
            for k in range(5, 8):
                pool.wait_ge(hi_made, k - 4)
                pool.tensor_tensor(tw.early_lo[:, piece(k)], raw[:, piece(k)], tw.early_hi[:, piece(k)].bitcast(F32),
                                   ALU.subtract)

        @block.scalar
        def _(act):
            for b in range(B):
                act.wait_ge(conv_ready, b + 1)
                nc.scalar.copy(ht[:, b].rearrange("p v n -> p n v"),
                               tw.ps[:, b, :].rearrange("p (n v) -> p n v", v=V)).then_inc(conv_copied, 1)
            act.wait_ge(tw.early_landed, 32)
            for k in (5, 6, 7, 0, 1, 2, 3, 4):
                nc.scalar.copy(tw.early_hi[:, piece(k)], raw[:, piece(k)]).then_inc(hi_made, 1)

        @block.tensor
        def _(pe):
            pe.wait_ge(wk_landed, 16)
            width = TAP_FEATURES * PATCH // 2
            for n in range(TAP_SETS):
                for u in range(2):
                    dft = wks[:, TAP_SETS * C + u * width:TAP_SETS * C + (u + 1) * width]
                    bank, c = 4 + n // 5, n % 5 * width
                    mm = nc.tensor.matmul(tw.ps[64 * u:64 * u + 64, bank, c:c + width],
                                          wks[:, n * C:(n + 1) * C], dft, start=True, stop=True)
                if n % 5 == 4:
                    mm.then_inc(taps_ready, 1)
            pe.wait_ge(taps_copied, 2)
            for b in range(B):
                pe.wait_ge(x_landed[b], 16 * 4)
                for k in range(8):
                    hh, s = k // 4, k % 4
                    for par in range(2):
                        first = hh + par
                        mm = nc.tensor.matmul(tw.ps[64 * par:64 * par + 64, b, :],
                                              taps[:, hh, s, :], xs[:, b, first:first + 15:2, s, :],
                                              start=(k == 0), stop=(k == 7))
                mm.then_inc(conv_ready, 1)
            pe.wait_ge(tw.full_landed, 16)
            for b in range(B):
                pe.wait_ge(conv_copied, b + 1)
                for vhi in range(4):
                    mm = nc.tensor.transpose(tw.ps[:, 2 + b, vhi * P:(vhi + 1) * P],
                                             ht[:, b, 16 * vhi:16 * vhi + 16, :].rearrange("p v n -> p (v n)"),
                                             tw.w("ident"))
                mm.then_inc(turned, 1)

        @block.vector
        def _(dve):
            nc.vector.memset(tw.minus_half[:, :], -0.5)
            for n in range(2):
                dve.wait_ge(taps_ready, n + 1)
                j0, nj = 5 * TAP_FEATURES * n, min(5 * TAP_FEATURES, D - 5 * TAP_FEATURES * n)
                nc.vector.tensor_copy(taps[:, :, :, j0:j0 + nj],
                                      tw.ps[:, 4 + n, 0:8 * nj].rearrange("p (j h s) -> p h s j", h=2, s=4))\
                    .then_inc(taps_copied, 1)
            for b in range(B):
                dve.wait_ge(turned, b + 1)
                nc.vector.tensor_copy(h[:, 8 * b:8 * b + 8, :].rearrange("p t j -> p (t j)"), tw.ps[:, 2 + b, :])
            for k in range(5):
                dve.wait_ge(hi_made, k + 4)
                nc.vector.tensor_tensor(tw.early_lo[:, piece(k)], raw[:, piece(k)], tw.early_hi[:, piece(k)].bitcast(F32),
                                        ALU.subtract)
            dve.wait_ge(tw.row_landed, 16)




def norm_stage(tw, src, gamma=None, beta=None, keep=None, turn=True, router=None, load=None):
    nc = tw.nc
    sums, centred, squared, spread = (tw.counter(x) for x in ("ln_sums", "ln_centred", "ln_squared", "ln_spread"))
    eps_added, rooted, normed = (tw.counter(x) for x in ("ln_eps_added", "ln_rooted", "ln_normed"))
    hi_made, lo_made, turned = (tw.counter(x) for x in ("ln_hi_made", "ln_lo_made", "ln_turned"))
    xt_copied, xt_last = tw.counter("ln_xt_copied"), tw.counter("ln_xt_last")
    affine = gamma is not None
    x = keep if keep is not None else tw.xn
    steps = 3 if affine else 1
    dst = (lambda g: x[:, TPG * g:TPG * g + TPG, :])
    with ExitStack() as ctx:
        total, var, rstd = (tw.sb("ln_" + n, [P, NT], ctx=ctx) for n in ("total", "var", "rstd"))
        xc = tw.sb("ln_xc", [P, NT, D], ctx=ctx)
        sq = tw.sb("ln_sq", [P, NT, D], ctx=ctx)
        pair = tw.sb("ln_pair", [P, NT, 2 * D], ctx=ctx)
        if router:
            router.place(ctx)
        block = ctx.enter_context(nc.Block())

        if load:
            @block.sync
            def _(sp):
                tile, source, landed = load
                sp.dma_start(tile, source).then_inc(landed, 16)

        @block.vector
        def _(dve):
            if router:
                router.copy_gates()
            for i in range(-1, G + 4):
                if 0 <= i < G:
                    t = slice(TPG * i, TPG * i + TPG)
                    dve.wait_ge(sums.sem, sums(i + 1))
                    nc.vector.scalar_tensor_tensor(out=xc[:, t, :], in0=wide(total[:, t], D), scalar=-1.0 / D,
                                                   in1=src[:, t, :], op0=ALU.mult, op1=ALU.add)\
                        .then_inc(centred.sem, 1)
                g = i - 1
                if 0 <= g < G:
                    t = slice(TPG * g, TPG * g + TPG)
                    dve.wait_ge(squared.sem, squared(g + 1))
                    nc.vector.reduce_sum(var[:, t], sq[:, t, :], AX.X).then_inc(spread.sem, 1)
                if i + 1 < G:
                    t = slice(TPG * (i + 1), TPG * (i + 1) + TPG)
                    nc.vector.reduce_sum(total[:, t], src[:, t, :], AX.X).then_inc(sums.sem, 1)
                g = i - 3
                if 0 <= g < G:
                    t = slice(TPG * g, TPG * g + TPG)
                    dve.wait_ge(rooted.sem, rooted(g + 1))
                    nc.vector.tensor_tensor(dst(g), xc[:, t, :], wide(rstd[:, t], D), ALU.mult)\
                        .then_inc(normed.sem, 1)
                g = i - 1
                if 0 <= g < G:
                    t = slice(TPG * g, TPG * g + TPG)
                    dve.wait_ge(spread.sem, spread(g + 1))
                    nc.vector.tensor_scalar(var[:, t], var[:, t], EPS, None, ALU.add).then_inc(eps_added.sem, 1)
                g = i - 3
                if affine and 0 <= g < G:
                    dve.wait_ge(normed.sem, normed(steps * g + 1))
                    nc.vector.tensor_tensor(dst(g), dst(g), rows_over(gamma, TPG), ALU.mult)\
                        .then_inc(normed.sem, 1)
                    dve.wait_ge(normed.sem, normed(steps * g + 2))
                    nc.vector.tensor_tensor(dst(g), dst(g), rows_over(beta, TPG), ALU.add).then_inc(normed.sem, 1)
                g = i - 4
                if turn and 0 <= g < G:
                    t = slice(TPG * g, TPG * g + TPG)
                    dve.wait_ge(hi_made.sem, hi_made(g + 1))
                    nc.vector.tensor_tensor(pair[:, t, D:2 * D], dst(g), pair[:, t, 0:D], ALU.subtract)\
                        .then_inc(lo_made.sem, 1)
            if turn:
                dve.wait_ge(turned.sem, turned(G))
                nc.vector.tensor_copy(tw.xt[:, T - BANK:T], tw.ps[:, G - 1, :]).then_inc(xt_last.sem, 1)
            if router:
                router.choose(dve)

        @block.scalar
        def _(act):
            for g in range(G):
                t = slice(TPG * g, TPG * g + TPG)
                act.wait_ge(centred.sem, centred(g + 1))
                nc.scalar.activation(sq[:, t, :], xc[:, t, :], ACT.Square, scale=float(D) ** -0.5)\
                    .then_inc(squared.sem, 1)
            if turn:
                for g in range(G):
                    t = slice(TPG * g, TPG * g + TPG)
                    act.wait_ge(normed.sem, normed(steps * (g + 1)))
                    nc.scalar.copy(pair[:, t, 0:D].bitcast(F32R), dst(g)).then_inc(hi_made.sem, 1)
                    if g >= 2:
                        act.wait_ge(turned.sem, turned(g - 1))
                        nc.scalar.copy(tw.xt[:, BANK * (g - 2):BANK * (g - 1)], tw.ps[:, g - 2, :])\
                            .then_inc(xt_copied.sem, 1)
                act.wait_ge(turned.sem, turned(G - 1))
                nc.scalar.copy(tw.xt[:, BANK * (G - 2):BANK * (G - 1)], tw.ps[:, G - 2, :]).then_inc(xt_copied.sem, 1)
            if router:
                router.exponentials(act)

        @block.gpsimd
        def _(pool):
            for g in range(G):
                t = slice(TPG * g, TPG * g + TPG)
                pool.wait_ge(eps_added.sem, eps_added(g + 1))
                pool.tensor_tensor(rstd[:, t], var[:, t], tw.minus_half[:, t], ALU.pow)\
                    .then_inc(rooted.sem, 1)
            if router:
                router.clear(pool)

        if turn:
            @block.tensor
            def _(pe):
                for i in range(G + 3):
                    if i < G:
                        pe.wait_ge(lo_made.sem, lo_made(i + 1))
                        for k in range(TPG):
                            mm = nc.tensor.transpose(tw.ps[:, i, k * P:(k + 1) * P], pair[:, TPG * i + k, :],
                                                     tw.w("ident"))
                        mm.then_inc(turned.sem, 1)
                    g = i - 2
                    if router and 0 <= g < G:
                        if g < G - 1:
                            pe.wait_ge(xt_copied.sem, xt_copied(g + 1))
                        else:
                            pe.wait_ge(xt_last.sem, xt_last(1))
                        router.score(pe, g)
                if router:
                    router.turn(pe)
    for s in (sums, centred, squared, spread, eps_added, rooted):
        s.passed(G)
    normed.passed(steps * G)
    if turn:
        for s in (hi_made, lo_made, turned):
            s.passed(G)
        xt_copied.passed(G - 1)
        xt_last.passed(1)
    if router:
        router.passed()




def attention_stage(tw, name, groups, scale, q_hi, q_lo, keys, value, post, bias_strips, finish, out,
                    project=None):
    nc, ps = tw.nc, tw.ps
    U = 8 * len(groups)
    NG = len(groups)
    s_ready, biased, maxed, p_ready = (tw.counter(x) for x in ("s_ready", "s_biased", "s_maxed", "p_ready"))
    p_turned, pt_first, pt_second = (tw.counter(x) for x in ("p_turned", "pt_first", "pt_second"))
    o_ready, o_copied, y_ready, y_scaled, inv_ready, y_added = (
        tw.counter(x) for x in ("o_ready", "o_copied", "y_ready", "y_scaled", "inv_ready", "y_added"))
    unscaled = tw.counter("s_unscaled")
    S_BANK, T_BANK, O_BANK = 0, 4, 6
    nq_made, nq_hi, nq_lo = (tw.counter(x) for x in ("nq_made", "nq_hi", "nq_lo"))
    projected = 2 * (NG - PREPARED) if project else 0

    def query_job(i, lag):
        g, w = (i - lag - 21) // 8, (i - lag - 21) % 8
        return 2 * g + w // 2 if w in (0, 2) and 0 <= 2 * g + w // 2 < projected else None

    HALF = N // 2
    n_add = 2 if finish != "store" else 0
    with ExitStack() as ctx:
        prob = tw.sb(name + "_prob", [P, 2, N], ctx=ctx)
        prob_t = tw.sb(name + "_prob_t", [P, 2, 2, NTB, HALF], ctx=ctx)
        nmax = tw.sb(name + "_nmax", [P, U], ctx=ctx)
        raw_max = tw.sb(name + "_raw_max", [P, U], ctx=ctx)
        total = tw.sb(name + "_total", [P, NG, 4, 2], ctx=ctx)
        inv = tw.sb(name + "_inv", [P, NG, 4, 2], ctx=ctx)
        o_sb = tw.sb(name + "_o", [P, 2, BANK], ctx=ctx)
        y_sb = tw.sb(name + "_y", [P, 2, 4, 2, D], ctx=ctx)
        if bias_strips is not None:
            logits = tw.sb(name + "_logits", [P, 2, N], ctx=ctx)
        block = ctx.enter_context(nc.Block())

        def parts(u):
            return u // 8, u % 8 // 4, u % 4

        @block.tensor
        def _(pe):
            for i in range(U + 21):
                if i < U:
                    g, j, nt = parts(i)
                    _, q0, k0, _ = groups[g]
                    if project and g >= PREPARED and i % 8 == 0:
                        pe.wait_ge(nq_lo.sem, nq_lo(2 * (g - PREPARED) + 2))
                    if i >= 2:
                        if bias_strips is None:
                            pe.wait_ge(p_ready.sem, p_ready(i - 1))
                        else:
                            pe.wait_ge(biased.sem, biased(i - 1))
                    for mh in range(2):
                        for k, q in enumerate((q_hi, q_lo)):
                            mm = nc.tensor.matmul(ps[:, S_BANK + 2 * (i % 2) + mh, :],
                                                  q(g, j)[:, q0[j] + nt * P:q0[j] + nt * P + P],
                                                  keys[:, k0[j] + mh * BANK:k0[j] + mh * BANK + BANK],
                                                  start=(k == 0), stop=(k == 1))
                    mm.then_inc(s_ready.sem, 1)
                if 2 <= i < U + 2:
                    u = i - 2
                    pe.wait_ge(p_ready.sem, p_ready(u + 1))
                    for half in range(2):
                        if u >= 1:
                            copied = pt_second if half else pt_first
                            pe.wait_ge(copied.sem, copied(u))
                        for k in range(4):
                            mm = nc.tensor.transpose(ps[:, T_BANK + half, k * P:(k + 1) * P],
                                                     prob[:, u % 2, (4 * half + k) * P:(4 * half + k + 1) * P],
                                                     tw.w("ident"))
                        mm.then_inc(p_turned.sem, 1)
                g, w = (i - 10) // 8, (i - 10) % 8
                if 0 <= g < NG:
                    members = groups[g][0]
                    if w == 0:
                        pe.wait_ge(pt_first.sem, pt_first(8 * (g + 1)))
                        pe.wait_ge(pt_second.sem, pt_second(8 * (g + 1)))
                        if g >= 2:
                            pe.wait_ge(y_scaled.sem, y_scaled(g - 1))
                            if 2 * (g - 1) <= projected:
                                pe.wait_ge(nq_lo.sem, nq_lo(2 * (g - 1)))
                    for j in range(2):
                        mm = nc.tensor.matmul(ps[64 * j:64 * j + 64, O_BANK + g % 2, :], value(members[j], w),
                                              prob_t[:, g % 2, j, w, :], start=(w == 0), stop=(w == 7))
                    if w == 7:
                        mm.then_inc(o_ready.sem, 1)
                g = (i - 19) // 8
                if (i - 19) % 8 == 0 and 0 <= g < NG:
                    pe.wait_ge(o_copied.sem, o_copied(g + 1))
                    for nt in range(4):
                        mm = nc.tensor.matmul(ps[:, O_BANK + g % 2, nt * P:(nt + 1) * P],
                                              o_sb[:, g % 2, nt * P:(nt + 1) * P], post(g), start=True, stop=True)
                    mm.then_inc(y_ready.sem, 1)
                n = query_job(i, 0)
                if n is not None:
                    pe.wait_ge(y_scaled.sem, y_scaled(n // 2 + 1))
                    if n >= 1:
                        pe.wait_ge(nq_lo.sem, nq_lo(n))
                    (wh, wl), c = project(n // 2 + PREPARED, n % 2)
                    for k, part in enumerate((wh, wl)):
                        mm = nc.tensor.matmul(ps[:, O_BANK + n // 2 % 2, :], part, tw.xt[:, c:c + BANK],
                                              start=(k == 0), stop=(k == 1))
                    mm.then_inc(nq_made.sem, 1)

        @block.scalar
        def _(act):
            for i in range(U + 21):
                if 2 <= i < U + 2:
                    u = i - 2
                    g, j, nt = parts(u)
                    act.wait_ge(p_turned.sem, p_turned(2 * u + 2))
                    if g >= 2 and u % 8 == 0:
                        act.wait_ge(o_ready.sem, o_ready(g - 1))
                    if bias_strips is not None:
                        nc.scalar.copy(prob_t[:, g % 2, j, 0:4, nt * P:(nt + 1) * P],
                                       ps[:, T_BANK, :].rearrange("p (a b) -> p a b", a=4)).then_inc(pt_first.sem, 1)
                    nc.scalar.copy(prob_t[:, g % 2, j, 4:8, nt * P:(nt + 1) * P],
                                   ps[:, T_BANK + 1, :].rearrange("p (a b) -> p a b", a=4)).then_inc(pt_second.sem, 1)
                if i < U:
                    g, j, nt = parts(i)
                    act.wait_ge(maxed.sem, maxed(i + 1))
                    if i >= 2:
                        act.wait_ge(p_turned.sem, p_turned(2 * (i - 1)))
                    source = ps[:, S_BANK + 2 * (i % 2):S_BANK + 2 * (i % 2) + 2, :].rearrange("p a b -> p (a b)")
                    if bias_strips is not None:
                        source = logits[:, i % 2, :]
                    nc.scalar.activation(prob[:, i % 2, :], source, ACT.Exp, bias=nmax[:, i:i + 1], scale=scale,
                                         accum_out=total[:, g, nt, j:j + 1]).then_inc(p_ready.sem, 1)
                g = (i - 18) // 8
                if (i - 18) % 8 == 0 and 0 <= g < NG:
                    act.wait_ge(o_ready.sem, o_ready(g + 1))
                    if g >= 2:
                        act.wait_ge(y_ready.sem, y_ready(g - 1))
                    nc.scalar.copy(o_sb[:, g % 2, :], ps[:, O_BANK + g % 2, :]).then_inc(o_copied.sem, 1)
                n = query_job(i, 0)
                if n is not None:
                    act.wait_ge(nq_made.sem, nq_made(n + 1))
                    nc.scalar.copy(q_hi(n // 2 + PREPARED, n % 2), ps[:, O_BANK + n // 2 % 2, :]).then_inc(nq_hi.sem, 1)

        @block.vector
        def _(dve):
            for i in range(U + 21):
                if i < U:
                    g, j, nt = parts(i)
                    dve.wait_ge(s_ready.sem, s_ready(i + 1))
                    source = ps[:, S_BANK + 2 * (i % 2):S_BANK + 2 * (i % 2) + 2, :].rearrange("p a b -> p (a b)")
                    if bias_strips is not None:
                        qt = groups[g][3] + nt
                        vhi, par = qt // 2, qt % 2
                        if i >= 2:
                            dve.wait_ge(p_ready.sem, p_ready(i - 1))
                        if i == 0:
                            dve.wait_ge(tw.strips_landed, 16)
                        for kpar in range(2):
                            strip = bias_strips[:, kpar - par + 1, (3 - vhi) * P:(7 - vhi) * P]
                            view = logits[:, i % 2, :].rearrange("p (a k b) -> p a k b", a=4, k=2)[:, :, kpar, :]
                            scores = source.rearrange("p (a k b) -> p a k b", a=4, k=2)[:, :, kpar, :]
                            ins = nc.vector.tensor_tensor(view, scores, strip.rearrange("p (a b) -> p a b", a=4),
                                                          ALU.add)
                        ins.then_inc(biased.sem, 1)
                        dve.wait_ge(biased.sem, biased(i + 1))
                        source = logits[:, i % 2, :]
                    if scale == 1.0:
                        nc.vector.tensor_reduce(nmax[:, i:i + 1], source, AX.X, ALU.max, negate=True)\
                            .then_inc(maxed.sem, 1)
                    else:
                        nc.vector.tensor_reduce(raw_max[:, i:i + 1], source, AX.X, ALU.max, negate=True)\
                            .then_inc(unscaled.sem, 1)
                        dve.wait_ge(unscaled.sem, unscaled(i + 1))
                        nc.vector.tensor_scalar(nmax[:, i:i + 1], raw_max[:, i:i + 1], scale, None, ALU.mult)\
                            .then_inc(maxed.sem, 1)
                if bias_strips is None and 2 <= i < U + 2:
                    u = i - 2
                    g, j, nt = parts(u)
                    dve.wait_ge(p_turned.sem, p_turned(2 * u + 1))
                    if g >= 2 and u % 8 == 0:
                        dve.wait_ge(o_ready.sem, o_ready(g - 1))
                    nc.vector.tensor_copy(prob_t[:, g % 2, j, 0:4, nt * P:(nt + 1) * P],
                                          ps[:, T_BANK, :].rearrange("p (a b) -> p a b", a=4)).then_inc(pt_first.sem, 1)
                n = query_job(i, 1)
                if n is not None:
                    dve.wait_ge(nq_hi.sem, nq_hi(n + 1))
                    nc.vector.tensor_tensor(q_lo(n // 2 + PREPARED, n % 2), ps[:, O_BANK + n // 2 % 2, :],
                                            q_hi(n // 2 + PREPARED, n % 2).bitcast(F32), ALU.subtract)\
                        .then_inc(nq_lo.sem, 1)
                g = (i - 9) // 8
                if (i - 9) % 8 == 0 and 0 <= g < NG:
                    dve.wait_ge(p_ready.sem, p_ready(8 * (g + 1)))
                    nc.vector.reciprocal(inv[:, g], total[:, g]).then_inc(inv_ready.sem, 1)
                g = (i - 20) // 8
                if (i - 20) % 8 == 0 and 0 <= g < NG:
                    dve.wait_ge(y_ready.sem, y_ready(g + 1))
                    dve.wait_ge(inv_ready.sem, inv_ready(g + 1))
                    if g >= 2 and n_add:
                        dve.wait_ge(y_added.sem, y_added(n_add * (g - 1)))
                    rows = ps[:, O_BANK + g % 2, :].rearrange("p (n e) -> p n e", n=8)
                    if finish == "store":
                        for j in range(2):
                            ins = nc.vector.tensor_tensor(
                                out(g, j), ps[:, O_BANK + g % 2, :].rearrange("p (n j e) -> p n j e", n=4, j=2)[:, :, j],
                                wide(inv[:, g, :, j], D), ALU.mult)
                        ins.then_inc(y_scaled.sem, 1)
                    else:
                        nc.vector.tensor_tensor(y_sb[:, g % 2].rearrange("p n j e -> p (n j) e"), rows,
                                                wide(inv[:, g].rearrange("p n j -> p (n j)"), D), ALU.mult)\
                            .then_inc(y_scaled.sem, 1)

        if n_add:
            @block.gpsimd
            def _(pool):
                for g in range(NG):
                    pool.wait_ge(y_scaled.sem, y_scaled(g + 1))
                    for j in range(2):
                        if g or j:
                            pool.wait_ge(y_added.sem, y_added(2 * g + j))
                        pool.tensor_tensor(out(g, j), out(g, j), y_sb[:, g % 2, :, j, :], ALU.add)\
                            .then_inc(y_added.sem, 1)
    for s in (s_ready, maxed, p_ready, pt_first, pt_second):
        s.passed(U)
    if scale != 1.0:
        unscaled.passed(U)
    if bias_strips is not None:
        biased.passed(U)
    p_turned.passed(2 * U)
    for s in (o_ready, o_copied, y_ready, y_scaled, inv_ready):
        s.passed(NG)
    y_added.passed(n_add * NG)
    for s in (nq_made, nq_hi, nq_lo):
        s.passed(projected)


def project_stage(tw, jobs, values=None):
    nc, ps = tw.nc, tw.ps
    made, hi_made, lo_made = (tw.counter(x) for x in ("pj_made", "pj_hi", "pj_lo"))
    values_made, copied_act, copied_dve = (tw.counter(x) for x in ("vl_made", "vl_act", "vl_dve"))
    NV = NT if values else 0
    with ExitStack() as ctx:
        high = tw.sb("key_high", [P, 2, BANK], ctx=ctx)
        block = ctx.enter_context(nc.Block())

        def wait_bank_free(pe, n):
            m = n - 8
            if 0 <= m < NV:
                copied = copied_dve if m % 2 else copied_act
                pe.wait_ge(copied.sem, copied(m // 2 + 1))
            elif m >= NV:
                pe.wait_ge(hi_made.sem, hi_made(m - NV + 1))
                pe.wait_ge(lo_made.sem, lo_made(m - NV + 1))

        @block.tensor
        def _(pe):
            for t in range(NV):
                wait_bank_free(pe, t)
                wh, wl, cols = values[:3]
                nc.tensor.matmul(ps[:, t % 8, 0:cols], tw.xt[:, t * P:(t + 1) * P], wh, start=True, stop=False)
                nc.tensor.matmul(ps[:, t % 8, 0:cols], tw.xt[:, t * P:(t + 1) * P], wl, start=False, stop=True)\
                    .then_inc(values_made.sem, 1)
            for n, (wh, wl, col, bias, kind, dst) in enumerate(jobs):
                wait_bank_free(pe, NV + n)
                bank = (NV + n) % 8
                nc.tensor.matmul(ps[:, bank, :], wh, tw.xt[:, col:col + BANK], start=True, stop=False)
                nc.tensor.matmul(ps[:, bank, :], wl, tw.xt[:, col:col + BANK], start=False, stop=True)\
                    .then_inc(made.sem, 1)

        @block.scalar
        def _(act):
            for t in range(0, NV, 2):
                _, _, cols, dst, bias = values
                act.wait_ge(values_made.sem, values_made(t + 1))
                nc.scalar.copy(dst(t), ps[:, t % 8, 0:cols]).then_inc(copied_act.sem, 1)
            k = 0
            for n, (wh, wl, col, bias, kind, dst) in enumerate(jobs):
                bank = (NV + n) % 8
                act.wait_ge(made.sem, made(n + 1))
                b = bias if bias is not None else 0.0
                if kind == "queries":
                    nc.scalar.activation(dst[0], ps[:, bank, :], ACT.Identity, bias=b).then_inc(hi_made.sem, 1)
                else:
                    lower = b[D:P, :] if bias is not None else 0.0
                    upper = b[0:D, :] if bias is not None else 0.0
                    if k >= 2:
                        act.wait_ge(lo_made.sem, lo_made(n - 1))
                    nc.scalar.activation(dst[0][0:D, :], ps[0:D, bank, :], ACT.Identity, bias=upper)
                    nc.scalar.activation(high[D:P, k % 2, :].bitcast(F32R), ps[D:P, bank, :], ACT.Identity,
                                         bias=lower).then_inc(hi_made.sem, 1)
                    k += 1

        @block.vector
        def _(dve):
            for t in range(1, NV, 2):
                _, _, cols, dst, bias = values
                dve.wait_ge(values_made.sem, values_made(t + 1))
                nc.vector.tensor_copy(dst(t), ps[:, t % 8, 0:cols]).then_inc(copied_dve.sem, 1)
            k = 0
            for n, (wh, wl, col, bias, kind, dst) in enumerate(jobs):
                bank = (NV + n) % 8
                dve.wait_ge(hi_made.sem, hi_made(n + 1))
                b = bias if bias is not None else 0.0
                if kind == "queries":
                    nc.vector.scalar_tensor_tensor(out=dst[1], in0=ps[:, bank, :], scalar=b,
                                                   in1=dst[0].bitcast(F32), op0=ALU.add, op1=ALU.subtract)\
                        .then_inc(lo_made.sem, 1)
                else:
                    lower = b[D:P, :] if bias is not None else 0.0
                    nc.vector.scalar_tensor_tensor(out=dst[0][D:P, :], in0=ps[D:P, bank, :], scalar=lower,
                                                   in1=high[D:P, k % 2, :], op0=ALU.add, op1=ALU.subtract)\
                        .then_inc(lo_made.sem, 1)
                    k += 1

        if values and values[4] is not None:
            @block.gpsimd
            def _(pool):
                for t in range(NV):
                    dst, bias = values[3], values[4]
                    copied = copied_dve if t % 2 else copied_act
                    pool.wait_ge(copied.sem, copied(t // 2 + 1))
                    pool.tensor_tensor(dst(t), dst(t), bias, ALU.add)
    for s in (made, hi_made, lo_made):
        s.passed(len(jobs))
    values_made.passed(NV)
    copied_act.passed(NV // 2)
    copied_dve.passed(NV // 2)




def batch(b):
    return slice(NTB * b, NTB * (b + 1))


class Router:

    def __init__(self, tw, experts, gate, bias, second_softmax, selectors, next_func=None, hidden=None):
        self.tw, self.E, self.gate, self.bias, self.second = tw, experts, gate, bias, second_softmax
        self.selectors, self.next_func, self.hidden = selectors, next_func, hidden
        self.made, self.step, self.ex, self.turned, self.cleared = (
            tw.counter(x) for x in ("rt_made", "rt_step", "rt_exp", "rt_turned", "rt_cleared"))
        self.hidden_made, self.hidden_kept = tw.counter("rt_hidden_made"), tw.counter("rt_hidden_kept")
        self.split = isinstance(gate, tuple)
        self.centred_step = 3 + (1 if bias is not None else 0)
        self.last_step = self.centred_step + (16 if second_softmax else 15)

    def after(self, step, b):
        return self.step((1 if self.split else 0) + B * (step - 1) + b + 1)

    def place(self, ctx):
        tw, E = self.tw, self.E
        self.lg = tw.sb("rt_logits", [P, NT, E], ctx=ctx)
        self.mx = tw.sb("rt_max", [P, NT], ctx=ctx)
        self.pr = tw.sb("rt_probs", [P, NT, max(E, 8)], ctx=ctx)
        self.top = tw.sb("rt_top", [P, NT, 8], ctx=ctx)
        self.idx = tw.sb("rt_index", [P, NT, 8], U32, ctx=ctx)
        self.idf = tw.sb("rt_index_f", [P, NT, 2], ctx=ctx)
        self.wt = tw.sb("rt_weight", [P, NT, 2], ctx=ctx)
        self.sm = tw.sb("rt_sum", [P, NT], ctx=ctx)
        self.cw = tw.sb("rt_combine", [P, NT, E], ctx=ctx)
        self.c2 = tw.sb("rt_combine2", [P, NT, 2, E], ctx=ctx)
        self.gates = tw.sb("rt_gates", [P, 2, E], F32R, ctx=ctx)
        self.cp = tw.sb("rt_pair", [P, NT, P], ctx=ctx)
        self.table = tw.sb("rt_table", [P, 1], ctx=ctx)
        if self.hidden:
            self.rh = tw.sb("rt_hidden", [P, T], ctx=ctx)
        parts = 2 if self.split else 1
        self.logits = [tw.ps[:, bank, 0:NTB * parts * E].rearrange("p (t k e) -> p t k e", k=parts, e=E)
                       for bank in (4, 7)]

    def copy_gates(self):
        if self.split:
            self.tw.nc.vector.tensor_copy(self.gates[:, 0, :], self.gate[0])
            self.tw.nc.vector.tensor_copy(self.gates[:, 1, :], self.gate[1]).then_inc(self.step.sem, 1)

    def score(self, pe, g):
        nc, tw = self.tw.nc, self.tw
        if self.split and g == 0:
            pe.wait_ge(self.step.sem, self.step(1))
        if self.hidden:
            hi, lo, _ = self.hidden
            cols = slice(g * BANK, (g + 1) * BANK)
            bank = 5 + g % 2
            if g >= 2:
                pe.wait_ge(self.hidden_kept.sem, self.hidden_kept(g - 1))
            nc.tensor.matmul(tw.ps[:, bank, :], hi, tw.xt[:, cols], start=True, stop=False)
            nc.tensor.matmul(tw.ps[:, bank, :], lo, tw.xt[:, cols], start=False, stop=True)\
                .then_inc(self.hidden_made.sem, 1)
            groups = [g - 1] * (g > 0) + [g] * (g == G - 1)
        else:
            groups = [g]
        for q in groups:
            if self.hidden:
                pe.wait_ge(self.hidden_kept.sem, self.hidden_kept(q + 1))
            source = self.rh if self.hidden else tw.xt
            moving = self.gates[:, :, :].rearrange("p k e -> p (k e)") if self.split else self.gate
            for t in range(TPG * q, TPG * q + TPG):
                mm = nc.tensor.matmul(self.logits[t // NTB][:, t % NTB].rearrange("p k e -> p (k e)"), source[:, t * P:(t + 1) * P],
                                      moving, start=True, stop=True)
            mm.then_inc(self.made.sem, 1)

    def turn(self, pe):
        nc, tw = self.tw.nc, self.tw
        for g in range(G):
            pe.wait_ge(self.step.sem, self.after(self.last_step, g * B // G))
            for k in range(TPG):
                mm = nc.tensor.transpose(tw.ps[:, g, k * P:(k + 1) * P], self.cp[:, TPG * g + k, :], tw.w("ident"))
            mm.then_inc(self.turned.sem, 1)

    def exponentials(self, act):
        nc, tw = self.tw.nc, self.tw
        if self.hidden:
            for g in range(G):
                act.wait_ge(self.hidden_made.sem, self.hidden_made(g + 1))
                nc.scalar.activation(self.rh[:, g * BANK:(g + 1) * BANK], tw.ps[:, 5 + g % 2, :], ACT.Relu,
                                     bias=self.hidden[2]).then_inc(self.hidden_kept.sem, 1)
        nc.scalar.copy(self.selectors[:, :, :], wide(tw.w("expert_rows")[:, 0:self.E], self.selectors.shape[2]))
        act.wait_ge(self.cleared.sem, self.cleared(1))
        for b in range(B):
            act.wait_ge(self.step.sem, self.after(self.centred_step, b))
            nc.scalar.activation(self.pr[:, batch(b), 0:self.E], self.lg[:, batch(b), :], ACT.Exp)\
                .then_inc(self.ex.sem, 1)
        if self.second:
            for b in range(B):
                act.wait_ge(self.step.sem, self.after(self.centred_step + 7, b))
                nc.scalar.activation(self.wt[:, batch(b), 1], self.wt[:, batch(b), 1], ACT.Exp)\
                    .then_inc(self.ex.sem, 1)
        if self.next_func is not None:
            nc.scalar.activation(self.table[:, :], tw.minus_half[:, 0:1], self.next_func)
        for g in range(1, G, 2):
            act.wait_ge(self.turned.sem, self.turned(g + 1))
            nc.scalar.copy(tw.ct[:, BANK * g:BANK * g + BANK], tw.ps[:, g, :])

    def clear(self, pool):
        pool.memset(self.pr[:, :, :], -1.0).then_inc(self.cleared.sem, 1)
        pool.memset(self.cp[:, :, :], 0.0).then_inc(self.cleared.sem, 1)

    def choose(self, dve):
        nc, tw, E = self.tw.nc, self.tw, self.E
        lg, mx, pr, top, idx, idf = self.lg, self.mx, self.pr, self.top, self.idx, self.idf
        wt, sm, cw, c2, cp = self.wt, self.sm, self.cw, self.c2, self.cp
        taken = [0, 0]

        def wait_last(b):
            if taken[b]:
                dve.wait_ge(self.step.sem, self.after(taken[b], b))

        def done(b, ins):
            taken[b] += 1
            ins.then_inc(self.step.sem, 1)

        for b in range(B):
            t = batch(b)
            dve.wait_ge(self.made.sem, self.made(G // B * (b + 1)))
            done(b, nc.vector.reduce_sum(lg[:, t, :], self.logits[b].rearrange("p t k e -> p t e k"), AX.X))
        if self.bias is not None:
            for b in range(B):
                wait_last(b)
                done(b, nc.vector.tensor_tensor(lg[:, batch(b), :], lg[:, batch(b), :], rows_over(self.bias, NTB),
                                                ALU.add))
        for b in range(B):
            wait_last(b)
            done(b, nc.vector.reduce_max(mx[:, batch(b)], lg[:, batch(b), :], AX.X))
        for b in range(B):
            wait_last(b)
            done(b, nc.vector.tensor_tensor(lg[:, batch(b), :], lg[:, batch(b), :], wide(mx[:, batch(b)], E),
                                            ALU.subtract))
        assert taken[0] == self.centred_step
        for b in range(B):
            dve.wait_ge(self.ex.sem, self.ex(b + 1))
            done(b, nc.vector.reduce_sum(sm[:, batch(b)], pr[:, batch(b), 0:E], AX.X))
        for b in range(B):
            wait_last(b)
            done(b, nc.vector.reciprocal(sm[:, batch(b)], sm[:, batch(b)]))
        for b in range(B):
            wait_last(b)
            done(b, nc.vector.tensor_tensor(pr[:, batch(b), 0:E], pr[:, batch(b), 0:E], wide(sm[:, batch(b)], E),
                                            ALU.mult))
        for b in range(B):
            wait_last(b)
            for t in range(NTB * b, NTB * (b + 1)):
                ins = nc.vector.max(top[:, t, :], pr[:, t, :])
            done(b, ins)
        for b in range(B):
            wait_last(b)
            for t in range(NTB * b, NTB * (b + 1)):
                ins = nc.vector.max_index(idx[:, t, :], top[:, t, :], pr[:, t, :])
            done(b, ins)
        for b in range(B):
            wait_last(b)
            done(b, nc.vector.tensor_copy(idf[:, batch(b), :], idx[:, batch(b), 0:2]))
        if self.second:
            for b in range(B):
                wait_last(b)
                done(b, nc.vector.tensor_tensor(wt[:, batch(b), 1], top[:, batch(b), 1], top[:, batch(b), 0],
                                                ALU.subtract))
            for b in range(B):
                dve.wait_ge(self.ex.sem, self.ex(B + b + 1))
                done(b, nc.vector.tensor_scalar(sm[:, batch(b)], wt[:, batch(b), 1], 1.0, None, ALU.add))
            for b in range(B):
                wait_last(b)
                done(b, nc.vector.reciprocal(sm[:, batch(b)], sm[:, batch(b)]))
            for b in range(B):
                wait_last(b)
                done(b, nc.vector.tensor_copy(wt[:, batch(b), 0], sm[:, batch(b)]))
            for b in range(B):
                wait_last(b)
                done(b, nc.vector.tensor_tensor(wt[:, batch(b), 1], wt[:, batch(b), 1], sm[:, batch(b)], ALU.mult))
        else:
            for b in range(B):
                wait_last(b)
                done(b, nc.vector.tensor_tensor(sm[:, batch(b)], top[:, batch(b), 0], top[:, batch(b), 1], ALU.add))
            for b in range(B):
                wait_last(b)
                done(b, nc.vector.tensor_scalar(sm[:, batch(b)], sm[:, batch(b)], 1e-12, None, ALU.max))
            for b in range(B):
                wait_last(b)
                done(b, nc.vector.reciprocal(sm[:, batch(b)], sm[:, batch(b)]))
            for b in range(B):
                wait_last(b)
                done(b, nc.vector.tensor_tensor(wt[:, batch(b), :], top[:, batch(b), 0:2], wide(sm[:, batch(b)], 2),
                                                ALU.mult))
        for b in range(B):
            wait_last(b)
            done(b, nc.vector.tensor_tensor(c2[:, batch(b)].rearrange("p t k e -> p (t k) e"),
                                            rows_over(tw.w("iota")[:, 0:E], 2 * NTB),
                                            wide(idf[:, batch(b), :].rearrange("p t k -> p (t k)"), E), ALU.is_equal))
        for b in range(B):
            wait_last(b)
            chosen = c2[:, batch(b)].rearrange("p t k e -> p (t k) e")
            done(b, nc.vector.tensor_tensor(chosen, chosen, wide(wt[:, batch(b), :].rearrange("p t k -> p (t k)"), E),
                                            ALU.mult))
        for b in range(B):
            wait_last(b)
            done(b, nc.vector.tensor_tensor(cw[:, batch(b), :], c2[:, batch(b), 0], c2[:, batch(b), 1], ALU.add))
        dve.wait_ge(self.cleared.sem, self.cleared(2))
        for b in range(B):
            wait_last(b)
            done(b, nc.vector.tensor_copy(cp[:, batch(b), 0:E].bitcast(F32R), cw[:, batch(b), :]))
        for b in range(B):
            wait_last(b)
            done(b, nc.vector.tensor_tensor(cp[:, batch(b), D:D + E], cw[:, batch(b), :], cp[:, batch(b), 0:E],
                                            ALU.subtract))
        assert taken[0] == taken[1] == self.last_step
        for g in range(0, G, 2):
            dve.wait_ge(self.turned.sem, self.turned(g + 1))
            nc.vector.tensor_copy(tw.ct[:, BANK * g:BANK * g + BANK], tw.ps[:, g, :])

    def passed(self):
        self.made.passed(G)
        self.step.passed((1 if self.split else 0) + B * self.last_step)
        self.ex.passed(B * (2 if self.second else 1))
        self.cleared.passed(2)
        self.turned.passed(G)
        if self.hidden:
            self.hidden_made.passed(G)
            self.hidden_kept.passed(G)




def swiglu_experts_stage(tw, h, later):
    nc, ps = tw.nc, tw.ps
    U = G * E0
    up, silu, gated, hid_ready, down = (tw.counter(x) for x in ("x0_up", "x0_silu", "x0_gated", "x0_hidden", "x0_down"))
    up2, spread = tw.counter("x0_up2"), tw.counter("x0_spread")
    y_copied, y_ready, y_added = (tw.counter(x) for x in ("x_ycopied", "x_yready", "x_yadded"))
    Y = 6
    w1, w2 = tw.early["l0_w1"], tw.early["l0_w2"]
    with ExitStack() as ctx:
        sg = tw.sb("x0_sg", [P, 2, BANK], ctx=ctx)
        gt = tw.sb("x0_gt", [P, 2, BANK], ctx=ctx)
        hid = tw.sb("x0_hid", [P, 2, BANK], ctx=ctx)
        yt = tw.sb("x0_yt", [P, 2, BANK], ctx=ctx)
        raws = [tw.sb(f"later_raw{n}", [P, src.shape[1]], ctx=ctx) for n, (src, _, _) in enumerate(later)]
        block = ctx.enter_context(nc.Block())

        @block.sync
        def _(sp):
            for raw, (src, _, _) in zip(raws, later):
                for half in range(2):
                    sp.dma_start(raw[64 * half:64 * half + 64, :], src).then_inc(tw.later_landed, 16)

        @block.gpsimd
        def _(pool):
            pool.wait_ge(tw.later_landed, 32 * len(later))
            for n, (raw, (_, hi, lo)) in enumerate(zip(raws, later)):
                pool.tensor_scalar(hi[:, :], raw[:, :], 1.0, 1.0, ALU.mult, ALU.mult).then_inc(tw.later_hi, 1)
                pool.wait_ge(tw.later_hi, n + 1)
                pool.tensor_tensor(lo[:, :], raw[:, :], hi[:, :].bitcast(F32), ALU.subtract)

        @block.tensor
        def _(pe):
            for i in range(U + 4):
                if i < U:
                    t, e = i // E0, i % E0
                    cols = slice(t * BANK, (t + 1) * BANK)
                    for k, w, read, ready in ((0, w1, silu, up), (2, w2, gated, up2)):
                        if i >= 2:
                            pe.wait_ge(read.sem, read(i - 1))
                        for n, part in enumerate((tw.early_hi, tw.early_lo)):
                            mm = nc.tensor.matmul(ps[:, k + i % 2, :], part[:, w.start + e * H0:w.start + e * H0 + H0],
                                                  tw.xt[:, cols], start=(n == 0), stop=(n == 1))
                        mm.then_inc(ready.sem, 1)
                u = i - 2
                if 0 <= u < U:
                    t, e = u // E0, u % E0
                    pe.wait_ge(hid_ready.sem, hid_ready(u + 1))
                    if e == 0 and t >= 2:
                        pe.wait_ge(y_added.sem, y_added(t - 1))
                    half = 64 * (e % 2)
                    nc.tensor.matmul(ps[half:half + 64, Y + t % 2, :], tw.w("l0_w3")[:, e * D:(e + 1) * D],
                                     hid[:, u % 2, :], start=(e < 2), stop=(e >= E0 - 2)).then_inc(down.sem, 1)
                if i < U:
                    t, e = i // E0, i % E0
                    nc.tensor.matmul(ps[:, 4 + i % 2, :], tw.sel128[:, e, :], tw.ct[:, t * BANK:(t + 1) * BANK],
                                     start=True, stop=True).then_inc(spread.sem, 1)
                t = (i - 3) // E0 - 1
                if (i - 3) % E0 == 0 and 0 <= t < G:
                    pe.wait_ge(y_copied.sem, y_copied(t + 1))
                    for k in range(TPG):
                        mm = nc.tensor.matmul(ps[:, Y + t % 2, k * D:(k + 1) * D], yt[:, t % 2, k * P:(k + 1) * P],
                                              tw.w("fold"), start=True, stop=True)
                    mm.then_inc(y_ready.sem, 1)

        @block.scalar
        def _(act):
            for i in range(U + 4):
                if i < U:
                    act.wait_ge(up.sem, up(i + 1))
                    if i >= 2:
                        act.wait_ge(gated.sem, gated(i - 1))
                    nc.scalar.activation(sg[:, i % 2, :], ps[:, i % 2, :], ACT.Silu).then_inc(silu.sem, 1)
                t = (i - 2) // E0 - 1
                if (i - 2) % E0 == 0 and 0 <= t < G:
                    act.wait_ge(down.sem, down(E0 * (t + 1)))
                    nc.scalar.copy(yt[:, t % 2, :], ps[:, Y + t % 2, :]).then_inc(y_copied.sem, 1)

        @block.vector
        def _(dve):
            for i in range(U + 4):
                if i < U:
                    dve.wait_ge(silu.sem, silu(i + 1))
                    dve.wait_ge(up2.sem, up2(i + 1))
                    nc.vector.tensor_tensor(gt[:, i % 2, :], sg[:, i % 2, :], ps[:, 2 + i % 2, :], ALU.mult)\
                        .then_inc(gated.sem, 1)
                    dve.wait_ge(gated.sem, gated(i + 1))
                    dve.wait_ge(spread.sem, spread(i + 1))
                    if i >= 2:
                        dve.wait_ge(down.sem, down(i - 1))
                    nc.vector.tensor_tensor(hid[:, i % 2, :], gt[:, i % 2, :], ps[:, 4 + i % 2, :], ALU.mult)\
                        .then_inc(hid_ready.sem, 1)
                t = (i - 3) // E0 - 1
                if (i - 3) % E0 == 0 and 0 <= t < G:
                    dve.wait_ge(y_ready.sem, y_ready(t + 1))
                    rows = h[:, TPG * t:TPG * t + TPG, :]
                    nc.vector.tensor_tensor(rows, rows, ps[:, Y + t % 2, 0:TPG * D].rearrange("p (k d) -> p k d", d=D),
                                            ALU.add).then_inc(y_added.sem, 1)
    for s in (up, up2, spread, silu, gated, hid_ready, down):
        s.passed(U)
    for s in (y_copied, y_ready, y_added):
        s.passed(G)


def pair_experts_stage(tw, h, pairs, w1, b1, func, mid, w3, b3, extra, shared=None):
    nc, ps = tw.nc, tw.ps
    NS = pairs + (1 if shared else 0)
    U = G * NS
    up, act1, mid_ready, act2, hid_ready, down = (
        tw.counter(x) for x in ("xp_up", "xp_act1", "xp_mid", "xp_act2", "xp_hidden", "xp_down"))
    y_copied, y_ready, y_added, y_kept = (tw.counter(x) for x in ("x_ycopied", "x_yready", "x_yadded", "xp_kept"))
    Y = 6
    with ExitStack() as ctx:
        a1 = tw.sb("xp_a1", [P, 2, 2, BANK], ctx=ctx)
        a2 = tw.sb("xp_a2", [P, 2, BANK], ctx=ctx)
        hid = tw.sb("xp_hid", [P, 2, BANK], ctx=ctx)
        yt = tw.sb("xp_yt", [P, 2, BANK], ctx=ctx)
        block = ctx.enter_context(nc.Block())

        def is_shared(u):
            return u % NS == pairs

        routed_to = [sum(not is_shared(v) for v in range(u + 1)) for u in range(U)]
        MID, LAG = 5, (1 if mid is not None else 0)

        def spread_bank(u):
            return 4 if mid is not None else 4 + u % 2

        def ups(u):
            if is_shared(u):
                return [shared["w1"]]
            w = w1(u % NS)
            return w if isinstance(w, list) else [w]

        @block.tensor
        def _(pe):
            for i in range(U + 4):
                if i < U:
                    t = i // NS
                    cols = slice(t * BANK, (t + 1) * BANK)
                    if i >= 2:
                        pe.wait_ge(act1.sem, act1(i - 1))
                    for k, (hi, lo) in enumerate(ups(i)):
                        mm = nc.tensor.matmul(ps[:, 2 * (i % 2) + k, :], hi, tw.xt[:, cols], start=True, stop=False)
                        mm = nc.tensor.matmul(ps[:, 2 * (i % 2) + k, :], lo, tw.xt[:, cols], start=False, stop=True)
                    mm.then_inc(up.sem, 1)
                u = i - 1
                if mid is not None and 0 <= u < U:
                    pe.wait_ge(act1.sem, act1(u + 1))
                    if u >= 1:
                        if is_shared(u - 1):
                            pe.wait_ge(hid_ready.sem, hid_ready(u))
                        else:
                            pe.wait_ge(act2.sem, act2(routed_to[u - 1]))
                    if is_shared(u):
                        mm = nc.tensor.matmul(ps[:, MID, :], shared["w2"], a1[:, u % 2, 0, :], start=True, stop=True)
                    else:
                        ms = mid[0](u % NS)
                        if isinstance(ms, list):
                            for k, m in enumerate(ms):
                                mm = nc.tensor.matmul(ps[64 * k:64 * k + 64, MID, :], m, a1[:, u % 2, k, :],
                                                      start=True, stop=True)
                        else:
                            mm = nc.tensor.matmul(ps[:, MID, :], ms, a1[:, u % 2, 0, :], start=True, stop=True)
                    mm.then_inc(mid_ready.sem, 1)
                u = i - 2
                if 0 <= u < U:
                    t, q = u // NS, u % NS
                    pe.wait_ge(hid_ready.sem, hid_ready(u + 1))
                    if q == 0 and t >= 2:
                        pe.wait_ge(y_added.sem, y_added(t - 1))
                    half = 64 * (q % 2)
                    w = shared["w3"] if is_shared(u) else w3(q)
                    nc.tensor.matmul(ps[half:half + 64, Y + t % 2, :], w, hid[:, u % 2, :],
                                     start=(q < 2), stop=(q >= NS - 2)).then_inc(down.sem, 1)
                u = i - LAG
                if 0 <= u < U and not is_shared(u):
                    t, q = u // NS, u % NS
                    cols = slice(t * BANK, (t + 1) * BANK)
                    nc.tensor.matmul(ps[:, spread_bank(u), :],
                                     tw.sel64[:, 2 * q:2 * q + 2, :].rearrange("p a b -> p (a b)"),
                                     tw.ct[:, cols], start=True, stop=True).then_inc(tw.spread_ready.sem, 1)
                t = (i - 3) // NS - 1
                if (i - 3) % NS == 0 and 0 <= t < G:
                    pe.wait_ge(y_copied.sem, y_copied(t + 1))
                    for k in range(TPG):
                        dst = ps[:, Y + t % 2, k * D:(k + 1) * D]
                        nc.tensor.matmul(dst, yt[:, t % 2, k * P:(k + 1) * P], tw.w("fold"), start=True, stop=False)
                        c = t * BANK + k * P
                        mm = nc.tensor.matmul(dst, tw.ct[:, c:c + P].bitcast(F32), b3, start=False, stop=True)
                    mm.then_inc(y_ready.sem, 1)

        @block.scalar
        def _(act):
            for i in range(U + 4):
                if i < U:
                    act.wait_ge(up.sem, up(i + 1))
                    if i >= 2:
                        if mid is None:
                            act.wait_ge(hid_ready.sem, hid_ready(i - 1))
                        else:
                            act.wait_ge(mid_ready.sem, mid_ready(i - 1))
                    bs = [shared["b1"]] if is_shared(i) else b1(i % NS)
                    for k, b in enumerate(bs):
                        ins = nc.scalar.activation(a1[:, i % 2, k, :], ps[:, 2 * (i % 2) + k, :], func, bias=b)
                    ins.then_inc(act1.sem, 1)
                u = i - 1
                if mid is not None and 0 <= u < U and not is_shared(u):
                    act.wait_ge(mid_ready.sem, mid_ready(u + 1))
                    if u >= 2:
                        act.wait_ge(hid_ready.sem, hid_ready(u - 1))
                    nc.scalar.activation(a2[:, u % 2, :], ps[:, MID, :], ACT.Relu, bias=mid[1](u % NS))\
                        .then_inc(act2.sem, 1)
                t = (i - 2) // NS - 1
                if (i - 2) % NS == 0 and 0 <= t < G:
                    act.wait_ge(down.sem, down(NS * (t + 1)))
                    nc.scalar.copy(yt[:, t % 2, :], ps[:, Y + t % 2, :]).then_inc(y_copied.sem, 1)

        @block.vector
        def _(dve):
            for i in range(U + 5):
                u = i - 1
                if 0 <= u < U:
                    if u >= 2:
                        dve.wait_ge(down.sem, down(u - 1))
                    if is_shared(u):
                        dve.wait_ge(mid_ready.sem, mid_ready(u + 1))
                        nc.vector.tensor_scalar(hid[:, u % 2, :], ps[:, MID, :], shared["b2"], 0.0, ALU.add,
                                                ALU.max).then_inc(hid_ready.sem, 1)
                    else:
                        if mid is None:
                            dve.wait_ge(act1.sem, act1(u + 1))
                        else:
                            dve.wait_ge(act2.sem, act2(routed_to[u]))
                        dve.wait_ge(tw.spread_ready.sem, tw.spread_ready(routed_to[u]))
                        source = a1[:, u % 2, 0, :] if mid is None else a2[:, u % 2, :]
                        nc.vector.tensor_tensor(hid[:, u % 2, :], source, ps[:, spread_bank(u), :], ALU.mult)\
                            .then_inc(hid_ready.sem, 1)
                t = (i - 4) // NS - 1
                if (i - 4) % NS == 0 and 0 <= t < G:
                    rows = h[:, TPG * t:TPG * t + TPG, :]
                    if extra is not None:
                        nc.vector.tensor_tensor(rows, rows, extra(t), ALU.add).then_inc(y_kept.sem, 1)
                        dve.wait_ge(y_kept.sem, y_kept(t + 1))
                    dve.wait_ge(y_ready.sem, y_ready(t + 1))
                    nc.vector.tensor_tensor(rows, rows, ps[:, Y + t % 2, 0:TPG * D].rearrange("p (k d) -> p k d", d=D),
                                            ALU.add).then_inc(y_added.sem, 1)
    for s in (up, act1, hid_ready, down):
        s.passed(U)
    if mid is not None:
        mid_ready.passed(U)
        act2.passed(G * pairs)
    tw.spread_ready.passed(G * pairs)
    for s in (y_copied, y_ready, y_added):
        s.passed(G)
    if extra is not None:
        y_kept.passed(G)




def encoder_layers_stage(tw, x):
    nc, ps = tw.nc, tw.ps
    DH = D // HEADS2
    scale = float(DH) ** -0.25
    HB = NTB // 2
    GB = G // B
    sums, centred, squared, spread = (tw.counter(s) for s in ("ln_sums", "ln_centred", "ln_squared", "ln_spread"))
    eps_added, rooted, normed = (tw.counter(s) for s in ("ln_eps_added", "ln_rooted", "ln_normed"))
    hi_made, lo_made, turned = (tw.counter(s) for s in ("ln_hi_made", "ln_lo_made", "ln_turned"))
    xt_first, xt_second, x_added, bias_added = (
        tw.counter(s) for s in ("la_xt_first", "la_xt_second", "la_x_added", "la_bias_added"))
    scaled, rescaled = tw.counter("ln_scaled"), tw.counter("ln_rescaled")
    k_made, k_max, k_neg, k_exp, k_turned, k_copied = (
        tw.counter(s) for s in ("la_keys", "la_kmax", "la_kneg", "la_kexp", "la_kturned", "la_kcopied"))
    qv_made, v_copied, q_max, q_less, q_exp, q_sum, q_inv, q_normed, q_turned, q_copied = (
        tw.counter(s) for s in ("la_qv", "la_vcopied", "la_qmax", "la_qless", "la_qexp", "la_qsum", "la_qinv",
                                "la_qnormed", "la_qturned", "la_qcopied"))
    ctx_made, ctx_masked, k_inv, cw_made, cw_scaled, y_made = (
        tw.counter(s) for s in ("la_ctx", "la_masked", "la_kinv", "la_cw", "la_cwscaled", "la_y"))
    cleared = tw.counter("la_cleared")
    up_made, gelu_made, out_made = (tw.counter(s) for s in ("ml_up", "ml_gelu", "ml_out"))

    def tiles(b):
        return slice(NTB * b, NTB * (b + 1))

    def pack(which, name):
        return which[:, tw.mid[name]]

    def by_head(ap):
        return ap.rearrange("p t (h d) -> p t h d", d=DH)

    def over_head(ap):
        return ap.rearrange("p (t h) -> p t h", h=HEADS2).unsqueeze(3).to_broadcast([P, NTB, HEADS2, DH])

    def queries(b):
        return ps[:, 4 * b + 2:4 * b + 4, :].rearrange("p g (k c d) -> p (g k) c d", c=2, d=D)

    with ExitStack() as ctx:
        sb = lambda name, shape: tw.sb("la_" + name, shape, ctx=ctx)
        total, var, rstd = sb("total", [P, NT]), sb("var", [P, NT]), sb("rstd", [P, NT])
        xc, sq, pair = sb("xc", [P, NT, D]), sb("sq", [P, NT, D]), sb("pair", [P, NT, 2 * D])
        ek = sb("ek", [P, B, N])
        ekt = sb("ekt", [P, NT, D])
        vs = sb("v", [P, NTB, B, D])
        qc, qe, qn = (sb(s, [P, NT, D]) for s in ("qc", "qe", "qn"))
        qt = sb("qt", [P, B, BANK])
        qmx, qsm, qiv = (sb(s, [P, B, NTB * HEADS2]) for s in ("qmx", "qsm", "qiv"))
        km, kn, ks, ki = (sb(s, [P, B]) for s in ("km", "kn", "ks", "ki"))
        cms = sb("cm", [P, 2, D])
        hid = sb("hid", [P, B, 2 * GB, BANK])
        table = sb("table", [P, 1])
        block = ctx.enter_context(nc.Block())

        @block.vector
        def _(dve):
            def add_into_x(n):
                layer, which, b = (n - 2) // 4, (n - 2) % 4 // 2, n % 2
                r = 2 * layer + b
                if which == 0:
                    dve.wait_ge(y_made.sem, y_made(r + 1))
                    bank = 4 * b + 3
                else:
                    dve.wait_ge(out_made.sem, out_made(r + 1))
                    bank = 4 * b
                dve.wait_ge(bias_added.sem, bias_added(n - 1))
                nc.vector.tensor_tensor(x[:, tiles(b), :], x[:, tiles(b), :],
                                        ps[:, bank, :].rearrange("p (t d) -> p t d", d=D), ALU.add)\
                    .then_inc(x_added.sem, 1)

            for layer in range(LAYERS):
                for which in range(2):
                    n0 = 4 * layer + 2 * which
                    gamma, beta = (tw.r(f"l2_ln{which + 1}_{s}{layer}") for s in "gb")
                    for b in range(B):
                        n, t = n0 + b, tiles(b)
                        if n >= 2:
                            add_into_x(n)
                            dve.wait_ge(x_added.sem, x_added(n - 1))
                        nc.vector.reduce_sum(total[:, t], x[:, t, :], AX.X).then_inc(sums.sem, 1)
                        dve.wait_ge(sums.sem, sums(n + 1))
                        nc.vector.scalar_tensor_tensor(out=xc[:, t, :], in0=wide(total[:, t], D), scalar=-1.0 / D,
                                                       in1=x[:, t, :], op0=ALU.mult, op1=ALU.add)\
                            .then_inc(centred.sem, 1)
                    for b in range(B):
                        n, t = n0 + b, tiles(b)
                        dve.wait_ge(squared.sem, squared(n + 1))
                        nc.vector.reduce_sum(var[:, t], sq[:, t, :], AX.X).then_inc(spread.sem, 1)
                        dve.wait_ge(spread.sem, spread(n + 1))
                        nc.vector.tensor_scalar(var[:, t], var[:, t], EPS, None, ALU.add).then_inc(eps_added.sem, 1)
                    for b in range(B):
                        n, t = n0 + b, tiles(b)
                        y = tw.xn[:, t, :]
                        nc.vector.tensor_tensor(y, xc[:, t, :], rows_over(gamma, NTB), ALU.mult).then_inc(scaled.sem, 1)
                    for b in range(B):
                        n, t = n0 + b, tiles(b)
                        dve.wait_ge(scaled.sem, scaled(n + 1))
                        dve.wait_ge(rooted.sem, rooted(n + 1))
                        y = tw.xn[:, t, :]
                        nc.vector.tensor_tensor(y, y, wide(rstd[:, t], D), ALU.mult).then_inc(rescaled.sem, 1)
                        dve.wait_ge(rescaled.sem, rescaled(n + 1))
                        nc.vector.tensor_tensor(y, y, rows_over(beta, NTB), ALU.add).then_inc(normed.sem, 1)
                    for b in range(B):
                        n, t = n0 + b, tiles(b)
                        dve.wait_ge(hi_made.sem, hi_made(n + 1))
                        nc.vector.tensor_tensor(pair[:, t, D:2 * D], tw.xn[:, t, :], pair[:, t, 0:D], ALU.subtract)\
                            .then_inc(lo_made.sem, 1)
                    for b in range(B):
                        n = n0 + b
                        dve.wait_ge(turned.sem, turned(n + 1))
                        nc.vector.tensor_copy(tw.xt[:, N * b + BANK:N * (b + 1)], ps[:, 4 * b + 1, :])\
                            .then_inc(xt_second.sem, 1)
                    if which == 1:
                        continue
                    for b in range(B):
                        r = 2 * layer + b
                        dve.wait_ge(k_made.sem, k_made(r + 1))
                        nc.vector.tensor_reduce(km[:, b:b + 1], ps[:, 4 * b:4 * b + 2, :], AX.XY, ALU.max,
                                                negate=True).then_inc(k_max.sem, 1)
                        dve.wait_ge(k_max.sem, k_max(r + 1))
                        nc.vector.tensor_scalar(kn[:, b:b + 1], km[:, b:b + 1], scale, None, ALU.mult)\
                            .then_inc(k_neg.sem, 1)
                    for b in range(B):
                        r = 2 * layer + b
                        dve.wait_ge(qv_made.sem, qv_made(r + 1))
                        q = by_head(queries(b)[:, :, 0, :])
                        nc.vector.reduce_max(qmx[:, b, :].rearrange("p (t h) -> p t h", h=HEADS2), q, AX.X)\
                            .then_inc(q_max.sem, 1)
                        dve.wait_ge(q_max.sem, q_max(r + 1))
                        nc.vector.tensor_tensor(by_head(qc[:, tiles(b), :]), q, over_head(qmx[:, b, :]), ALU.subtract)\
                            .then_inc(q_less.sem, 1)
                    for b in range(B):
                        r = 2 * layer + b
                        dve.wait_ge(q_exp.sem, q_exp(r + 1))
                        nc.vector.reduce_sum(qsm[:, b, :], qe[:, tiles(b), :].rearrange("p t (h d) -> p (t h) d", d=DH),
                                             AX.X).then_inc(q_sum.sem, 1)
                        dve.wait_ge(q_sum.sem, q_sum(r + 1))
                        nc.vector.reciprocal(qiv[:, b, :], qsm[:, b, :]).then_inc(q_inv.sem, 1)
                        dve.wait_ge(q_inv.sem, q_inv(r + 1))
                        nc.vector.tensor_tensor(by_head(qn[:, tiles(b), :]), by_head(qe[:, tiles(b), :]),
                                                over_head(qiv[:, b, :]), ALU.mult).then_inc(q_normed.sem, 1)
                        dve.wait_ge(k_exp.sem, k_exp(r + 1))
                        nc.vector.reciprocal(ki[:, b:b + 1], ks[:, b:b + 1]).then_inc(k_inv.sem, 1)
                    for b in range(B):
                        rows = slice(D * b, D * b + D)
                        dve.wait_ge(ctx_made.sem, ctx_made(layer + 1))
                        nc.vector.tensor_tensor(cms[rows, :, :], rows_over(ps[rows, 1, rows], 2),
                                                rows_over(tw.w("head_mask")[rows, rows], 2), ALU.mult)\
                            .then_inc(ctx_masked.sem, 1)
                    for b in range(B):
                        r = 2 * layer + b
                        dve.wait_ge(cw_made.sem, cw_made(r + 1))
                        dve.wait_ge(k_inv.sem, k_inv(r + 1))
                        if r == 0:
                            dve.wait_ge(cleared.sem, cleared(1))
                        for half in range(2):
                            rows = slice(D * half, D * half + D)
                            nc.vector.tensor_scalar(tw.cw_block[rows, b, rows], ps[rows, 4 * b + 1, 2 * D:3 * D],
                                                    ki[rows, b:b + 1], None, ALU.mult).then_inc(cw_scaled.sem, 1)
            for b in range(B):
                add_into_x(4 * LAYERS + b)

        @block.scalar
        def _(act):
            def exp_keys(r, b):
                act.wait_ge(k_neg.sem, k_neg(r + 1))
                nc.scalar.activation(ek[:, b, :], ps[:, 4 * b:4 * b + 2, :].rearrange("p g c -> p (g c)"), ACT.Exp,
                                     bias=kn[:, b:b + 1], scale=scale, accum_out=ks[:, b:b + 1]).then_inc(k_exp.sem, 1)

            for layer in range(LAYERS):
                for which in range(2):
                    n0 = 4 * layer + 2 * which
                    for b in range(B):
                        n, t = n0 + b, tiles(b)
                        act.wait_ge(centred.sem, centred(n + 1))
                        nc.scalar.activation(sq[:, t, :], xc[:, t, :], ACT.Square, scale=float(D) ** -0.5)\
                            .then_inc(squared.sem, 1)
                    for b in range(B):
                        n, t = n0 + b, tiles(b)
                        act.wait_ge(normed.sem, normed(n + 1))
                        nc.scalar.copy(pair[:, t, 0:D].bitcast(F32R), tw.xn[:, t, :]).then_inc(hi_made.sem, 1)
                    nc.scalar.activation(table[:, :], tw.minus_half[:, 0:1], ACT.Gelu if which else ACT.Exp)
                    for b in range(B):
                        n = n0 + b
                        act.wait_ge(turned.sem, turned(n + 1))
                        nc.scalar.copy(tw.xt[:, N * b:N * b + BANK], ps[:, 4 * b, :]).then_inc(xt_first.sem, 1)
                    if which == 1:
                        for b in range(B):
                            r = 2 * layer + b
                            for i in range(2 * GB):
                                act.wait_ge(up_made.sem, up_made(2 * GB * r + i + 1))
                                nc.scalar.activation(hid[:, b, i, :], ps[:, 4 * b + i, :], ACT.Gelu,
                                                     bias=tw.w(f"l2_b1{layer}")[:, i % 2:i % 2 + 1])\
                                    .then_inc(gelu_made.sem, 1)
                        continue
                    for b in range(B):
                        exp_keys(2 * layer + b, b)
                    for b in range(B):
                        r = 2 * layer + b
                        act.wait_ge(q_less.sem, q_less(r + 1))
                        nc.scalar.activation(qe[:, tiles(b), :], qc[:, tiles(b), :], ACT.Exp, scale=scale)\
                            .then_inc(q_exp.sem, 1)
                        nc.scalar.copy(vs[:, :, b, :], queries(b)[:, :, 1, :]).then_inc(v_copied.sem, 1)
                    for b in range(B):
                        r = 2 * layer + b
                        act.wait_ge(k_turned.sem, k_turned(r + 1))
                        nc.scalar.copy(ekt[:, tiles(b), :].rearrange("p t d -> p (t d)"), ps[:, 4 * b, :])\
                            .then_inc(k_copied.sem, 1)
                    for b in range(B):
                        r = 2 * layer + b
                        act.wait_ge(q_turned.sem, q_turned(r + 1))
                        nc.scalar.copy(qt[:, b, :], ps[:, 4 * b + 2, :]).then_inc(q_copied.sem, 1)

        @block.gpsimd
        def _(pool):
            pool.memset(tw.cw_block[:, :, :], 0.0).then_inc(cleared.sem, 1)
            for layer in range(LAYERS):
                for which in range(2):
                    n0 = 4 * layer + 2 * which
                    for b in range(B):
                        n, t = n0 + b, tiles(b)
                        pool.wait_ge(eps_added.sem, eps_added(n + 1))
                        pool.tensor_tensor(rstd[:, t], var[:, t], tw.minus_half[:, t], ALU.pow).then_inc(rooted.sem, 1)
                    for b in range(B):
                        n, t = n0 + b, tiles(b)
                        pool.wait_ge(centred.sem, centred(n + 1))
                        bias = tw.r(f"l2_b2{layer}" if which else f"l2_bo{layer}")
                        pool.tensor_tensor(x[:, t, :], x[:, t, :], rows_over(bias, NTB), ALU.add)\
                            .then_inc(bias_added.sem, 1)

        @block.tensor
        def _(pe):
            def turn(n, b):
                pe.wait_ge(lo_made.sem, lo_made(n + 1))
                for t in range(NTB):
                    mm = nc.tensor.transpose(ps[:, 4 * b + t // TPG, t % TPG * P:(t % TPG + 1) * P],
                                             pair[:, NTB * b + t, :], tw.w("ident"))
                mm.then_inc(turned.sem, 1)

            def wait_turned(n, g):
                copied = (xt_first, xt_second)[g]
                pe.wait_ge(copied.sem, copied(n + 1))

            for layer in range(LAYERS):
                for b in range(B):
                    turn(4 * layer + b, b)
                for b in range(B):
                    for g in range(GB):
                        wait_turned(4 * layer + b, g)
                        for k, part in enumerate((tw.mid_hi, tw.mid_lo)):
                            mm = nc.tensor.matmul(ps[:, 4 * b + g, :], pack(part, f"l2_k{layer}"),
                                                  tw.xt[:, N * b + g * BANK:N * b + (g + 1) * BANK],
                                                  start=(k == 0), stop=(k == 1))
                    mm.then_inc(k_made.sem, 1)
                for b in range(B):
                    for t in range(NTB):
                        for k, part in enumerate((tw.mid_hi, tw.mid_lo)):
                            mm = nc.tensor.matmul(ps[:, 4 * b + 2 + t // TPG, t % TPG * P:(t % TPG + 1) * P],
                                                  tw.xt[:, N * b + t * P:N * b + (t + 1) * P],
                                                  pack(part, f"l2_qv{layer}"), start=(k == 0), stop=(k == 1))
                    mm.then_inc(qv_made.sem, 1)
                for b in range(B):
                    r = 2 * layer + b
                    pe.wait_ge(k_exp.sem, k_exp(r + 1))
                    for t in range(NTB):
                        mm = nc.tensor.transpose(ps[:, 4 * b, t * D:(t + 1) * D], ek[0:D, b, t * P:(t + 1) * P],
                                                 tw.w("ident")[0:D, 0:D])
                    mm.then_inc(k_turned.sem, 1)
                pe.wait_ge(k_copied.sem, k_copied(2 * layer + 2))
                pe.wait_ge(v_copied.sem, v_copied(2 * layer + 2))
                for t in range(NTB):
                    mm = nc.tensor.matmul(ps[:, 1, 0:P], vs[:, t].rearrange("p b d -> p (b d)"), ekt[:, t:NT:NTB, :],
                                          start=(t == 0), stop=(t == NTB - 1))
                mm.then_inc(ctx_made.sem, 1)
                for b in range(B):
                    r = 2 * layer + b
                    pe.wait_ge(q_normed.sem, q_normed(r + 1))
                    for k in range(HB):
                        mm = nc.tensor.transpose(ps[:, 4 * b + 2, k * P:(k + 1) * P],
                                                 qn[:, NTB * b + 2 * k:NTB * b + 2 * k + 2, :].rearrange("p t d -> p (t d)"),
                                                 tw.w("ident"))
                    mm.then_inc(q_turned.sem, 1)
                    if b == 0:
                        pe.wait_ge(ctx_masked.sem, ctx_masked(2 * layer + 2))
                        for c in range(B):
                            rows = slice(D * c, D * c + D)
                            nc.tensor.matmul(ps[:, 4 * c + 1, 2 * D:3 * D], cms[rows].rearrange("p k d -> p (k d)"),
                                             tw.w(f"l2_wo{layer}")[rows, :], start=True, stop=True)\
                                .then_inc(cw_made.sem, 1)
                for b in range(B):
                    r = 2 * layer + b
                    pe.wait_ge(cw_scaled.sem, cw_scaled(2 * r + 2))
                    pe.wait_ge(q_copied.sem, q_copied(r + 1))
                    for k in range(HB):
                        mm = nc.tensor.matmul(ps[:, 4 * b + 3, k * P:(k + 1) * P], qt[:, b, k * P:(k + 1) * P],
                                              tw.cw_block[:, b, :], start=True, stop=True)
                    mm.then_inc(y_made.sem, 1)
                w1, w2 = tw.mid[f"l2_w1{layer}"], tw.w(f"l2_w2{layer}")
                for b in range(B):
                    turn(4 * layer + 2 + b, b)
                for b in range(B):
                    for i in range(2 * GB):
                        g, c = i // 2, i % 2
                        if c == 0:
                            wait_turned(4 * layer + 2 + b, g)
                        if i == 1:
                            wait_turned(4 * layer + 2 + b, 1)
                        for k, part in enumerate((tw.mid_hi, tw.mid_lo)):
                            mm = nc.tensor.matmul(ps[:, 4 * b + i, :], part[:, w1.start + c * P:w1.start + (c + 1) * P],
                                                  tw.xt[:, N * b + g * BANK:N * b + (g + 1) * BANK],
                                                  start=(k == 0), stop=(k == 1))
                        mm.then_inc(up_made.sem, 1)
                for b in range(B):
                    r = 2 * layer + b
                    for t in range(NTB):
                        g = t // TPG
                        if t % TPG == 0:
                            pe.wait_ge(gelu_made.sem, gelu_made(2 * GB * r + 2 * g + 2))
                        for c in range(2):
                            mm = nc.tensor.matmul(ps[:, 4 * b, t * D:(t + 1) * D],
                                                  hid[:, b, 2 * g + c, t % TPG * P:(t % TPG + 1) * P],
                                                  w2[:, c * D:(c + 1) * D], start=(c == 0), stop=(c == 1))
                    mm.then_inc(out_made.sem, 1)
    for s in (sums, centred, squared, spread, eps_added, rooted, hi_made, lo_made, turned, xt_first, xt_second, x_added, bias_added,
              scaled, rescaled, normed):
        s.passed(2 * B * LAYERS)




def scale_shift_stage(tw, x, scale, shift):
    nc = tw.nc
    with nc.Block() as block:
        @block.vector
        def _(dve):
            nc.vector.scalar_tensor_tensor(out=x[:, :, :], in0=x[:, :, :], scalar=scale, in1=rows_over(shift, NT),
                                           op0=ALU.mult, op1=ALU.add)


def add_stage(tw, x, y):
    nc = tw.nc
    with nc.Block() as block:
        @block.vector
        def _(dve):
            nc.vector.tensor_tensor(x[:, :, :], x[:, :, :], y, ALU.add)


def score_matrices_stage(tw, w, a_hi, a_lo, h, bias):
    nc, ps = tw.nc, tw.ps
    made, hi_made = (tw.counter(x) for x in ("sm_made", "sm_hi"))
    with ExitStack() as ctx:
        block = ctx.enter_context(nc.Block())

        @block.tensor
        def _(pe):
            pe.wait_ge(tw.qk_landed, 16)
            for hd in range(HEADS):
                r = slice(64 * (hd % 2), 64 * (hd % 2) + 64)
                mm = nc.tensor.matmul(ps[:, hd, 0:P], w[r, 0, hd // 2, :], w[r, 1, hd // 2, :], start=True, stop=True)
                mm.then_inc(made.sem, 1)

        @block.scalar
        def _(act):
            act.wait_ge(made.sem, made(HEADS))
            nc.scalar.copy(a_hi[:, :, :], ps[:, :, 0:P]).then_inc(hi_made.sem, 1)

        @block.vector
        def _(dve):
            nc.vector.tensor_tensor(h[:, :, :], h[:, :, :], rows_over(bias, NT), ALU.add)
            dve.wait_ge(hi_made.sem, hi_made(1))
            nc.vector.tensor_tensor(a_lo[:, :, :], ps[:, :, 0:P], a_hi[:, :, :].bitcast(F32), ALU.subtract)
    made.passed(HEADS)
    hi_made.passed(1)


def vit_tower_kernel(nc, x, wk, early, mid, late, full, row, toeplitz, qk, out):
    with ExitStack() as ctx:
        tw = Tower(nc, ctx)
        tw.ps = ctx.enter_context(nc.psum_tensor("ps", [P, 8, BANK], F32))
        h = tw.h = tw.sb("h", [P, NT, D])
        tw.xt = tw.sb("xt", [P, T], F32R)
        tw.w_full = tw.sb("w_full", [P, tw.full.n])
        tw.w_row = tw.sb("w_row", [P, tw.row.n])
        tw.minus_half = tw.sb("minus_half", [P, NT])
        tw.late_hi = tw.sb("late_hi", [P, tw.late.n], F32R)
        tw.late_lo = tw.sb("late_lo", [P, tw.late.n], F32R)
        tw.early_landed, tw.full_landed, tw.row_landed, tw.later_landed, tw.later_hi, tw.strips_landed, tw.out_landed = (
            nc.alloc_semaphore(name) for name in ("early_landed", "full_landed", "row_landed", "later_landed",
                                                  "later_hi", "strips_landed", "out_landed"))
        tw.spread_ready = tw.counter("xp_spread")

        def parts(pack, lay, name):
            hi, lo = pack
            return hi[:, lay[name]], lo[:, lay[name]]

        tw.qk_landed = nc.alloc_semaphore("qk_landed")
        mids = ctx.enter_context(ExitStack())
        tw.xn = tw.sb("xn", [P, NT, D], ctx=mids)
        tw.mid_hi = tw.sb("mid_hi", [P, tw.mid.n], F32R, ctx=mids)
        tw.mid_lo = tw.sb("mid_lo", [P, tw.mid.n], F32R, ctx=mids)
        MID, LATE = (tw.mid_hi, tw.mid_lo), (tw.late_hi, tw.late_lo)

        with ExitStack() as l0:
            tw.early_hi = tw.sb("early_hi", [P, tw.early.n], F32R, ctx=l0)
            tw.early_lo = tw.sb("early_lo", [P, tw.early.n], F32R, ctx=l0)
            EARLY = (tw.early_hi, tw.early_lo)
            embed_stage(tw, x, wk, early, full, row)
            norm_stage(tw, h, keep=tw.xn)
            with ExitStack() as at:
                qh = tw.sb("a0_qh", [P, T], F32R, ctx=at)
                ql = tw.sb("a0_ql", [P, T], F32R, ctx=at)
                wh, wl = parts(EARLY, tw.early, "l0_attn")
                project_stage(tw, [(wh, wl, g * BANK, None, "queries",
                                    (qh[:, g * BANK:(g + 1) * BANK], ql[:, g * BANK:(g + 1) * BANK]))
                                   for g in range(G)])
                groups = [((0, 1), [b * N + nh * BANK for b in range(B)], [b * N for b in range(B)], 4 * nh)
                          for nh in range(2)]
                attention_stage(tw, "a0", groups, 1.0 / 8.0, lambda g, j: qh, lambda g, j: ql, tw.xt,
                                lambda m, w: tw.xn[:, NTB * m + w, :], lambda g: tw.w("ident"), None, "add",
                                lambda g, j: h[:, NTB * j + 4 * g:NTB * j + 4 * g + 4, :])
            tw.ct = tw.sb("ct0", [P, T], F32R, ctx=l0)
            tw.sel128 = tw.sb("sel128", [P, E0, H0], F32R, ctx=l0)
            norm_stage(tw, h, router=Router(tw, E0, parts(EARLY, tw.early, "l0_gate"), tw.r("l0_gate_b"), False,
                                            tw.sel128, ACT.Silu))
            swiglu_experts_stage(tw, h, [(mid, tw.mid_hi, tw.mid_lo), (late, tw.late_hi, tw.late_lo)])

        with ExitStack() as l1:
            strips = tw.sb("bias_strips", [P, 3, 7 * P], ctx=l1)
            norm_stage(tw, h, keep=tw.xn, turn=False, load=(strips[:, :, :], toeplitz, tw.strips_landed))
            norm_stage(tw, tw.xn, tw.r("l1_ln1_g"), tw.r("l1_ln1_b"), keep=tw.xn)
            qh = tw.sb("a1_qh", [P, T], F32R, ctx=l1)
            ql = tw.sb("a1_ql", [P, T], F32R, ctx=l1)
            kk = tw.sb("a1_k", [P, T], F32R, ctx=l1)
            vt = tw.sb("a1_v", [P, NT, D], ctx=l1)
            ob = tw.sb("a1_out", [P, NT, D], ctx=l1)
            jobs = []
            for g in range(G):
                cols = slice(g * BANK, (g + 1) * BANK)
                jobs.append((*parts(MID, tw.mid, "l1_q"), g * BANK, tw.w("l1_qb"), "queries",
                             (qh[:, cols], ql[:, cols])))
                jobs.append((*parts(MID, tw.mid, "l1_k"), g * BANK, tw.w("l1_kb"), "keys", (kk[:, cols],)))
            project_stage(tw, jobs, (*parts(MID, tw.mid, "l1_v"), D, lambda t: vt[:, t, :], tw.r("l1_vb")))
            groups = [((0, 1), [b * N + nh * BANK for b in range(B)], [b * N for b in range(B)], 4 * nh)
                      for nh in range(2)]
            attention_stage(tw, "a1", groups, 1.0, lambda g, j: qh, lambda g, j: ql, kk,
                            lambda m, w: vt[:, NTB * m + w, :], lambda g: tw.w("l1_post"), strips, "store",
                            lambda g, j: ob[:, NTB * j + 4 * g:NTB * j + 4 * g + 4, :])
            scale_shift_stage(tw, ob, tw.r("l1_scale"), tw.r("l1_proj_b"))
            norm_stage(tw, ob, tw.r("l1_ln2_g"), tw.r("l1_ln2_b"), keep=ob, turn=False)
            add_stage(tw, h, ob[:, :, :])
        with ExitStack() as f1:
            tw.ct = tw.sb("ct1", [P, T], F32R, ctx=f1)
            tw.sel64 = tw.sb("sel64_1", [P, E1, D], F32R, ctx=f1)
            norm_stage(tw, h, keep=tw.xn, router=Router(tw, E1, parts(MID, tw.mid, "l1_gate"), None, False,
                                                        tw.sel64, ACT.Gelu))
            w1 = tw.mid["l1_w1"].start
            pair_experts_stage(
                tw, h, E1 // 2,
                lambda q: tuple(p[:, w1 + q * P:w1 + (q + 1) * P] for p in MID),
                lambda q: [tw.w("l1_b1")[:, q:q + 1]], ACT.Gelu, None,
                lambda q: tw.w("l1_w2")[:, q * D:(q + 1) * D], tw.w("l1_b2"),
                lambda t: tw.xn[:, TPG * t:TPG * t + TPG, :])

        with ExitStack() as l2:
            x2 = tw.sb("x2", [P, NT, D], ctx=l2)
            tw.cw_block = tw.sb("cw_block", [P, B, P], ctx=l2)
            norm_stage(tw, h, keep=x2, turn=False)
            encoder_layers_stage(tw, x2)
            add_stage(tw, h, x2[:, :, :])
        with ExitStack() as f2:
            tw.ct = tw.sb("ct2", [P, T], F32R, ctx=f2)
            tw.sel64 = tw.sb("sel64_2", [P, E2, D], F32R, ctx=f2)
            norm_stage(tw, h, router=Router(tw, E2, tw.w("l2_rw2"), tw.r("l2_rb2"), True, tw.sel64,
                                            hidden=(*parts(MID, tw.mid, "l2_router"), tw.w("l2_rb1"))))
            w1 = tw.mid["l2_e1"].start
            pair_experts_stage(
                tw, h, E2 // 2,
                lambda q: tuple(p[:, w1 + q * P:w1 + (q + 1) * P] for p in MID),
                lambda q: [tw.w("l2_eb1")[:, q:q + 1]], ACT.Relu,
                (lambda q: tw.w("l2_e2")[:, q * P:(q + 1) * P], lambda q: tw.w("l2_eb2")[:, q:q + 1]),
                lambda q: tw.w("l2_e3")[:, q * D:(q + 1) * D], tw.w("l2_eb3"), None)
        mids.close()

        tw.xn = tw.sb("xn3", [P, NT, D])
        with ExitStack() as l3:
            vt = tw.sb("a3_v", [P, NT, HEADS * D], ctx=l3)
            qk_rows = vt[:, 0:2, :].rearrange("p a (k c) -> p a k c", k=HEADS // 2)
            norm_stage(tw, h, load=(vt[:, 0:2, :].rearrange("p a c -> p (a c)"), qk, tw.qk_landed))
            a_hi = tw.sb("a3_hi", [P, HEADS, P], F32R, ctx=l3)
            a_lo = tw.sb("a3_lo", [P, HEADS, P], F32R, ctx=l3)
            score_matrices_stage(tw, qk_rows, a_hi, a_lo, h, tw.r("l3_bout"))
            qh = tw.sb("a3_qh", [P, 2 * PREPARED, BANK], F32R, ctx=l3)
            ql = tw.sb("a3_ql", [P, 2 * PREPARED, BANK], F32R, ctx=l3)
            pairs = HEADS // 2
            groups = [((HEADS * b + 2 * k, HEADS * b + 2 * k + 1), [0, 0], [b * N, b * N], 4 * nh)
                      for b in range(B) for nh in range(2) for k in range(pairs)]

            def project(g, j):
                m = 2 * (g % pairs) + j
                return (a_hi[:, m, :], a_lo[:, m, :]), g // pairs * BANK

            def queries(which):
                return lambda g, j: which[:, 2 * (g % PREPARED) + j, :]

            q_hi, q_lo = queries(qh), queries(ql)
            jobs = [(project(g, j), "queries", (q_hi(g, j), q_lo(g, j))) for g in range(PREPARED) for j in range(2)]
            project_stage(tw, [(*w, c, None, kind, dst) for (w, c), kind, dst in jobs],
                          (*parts(LATE, tw.late, "l3_v"), HEADS * D, lambda t: vt[:, t, :], None))
            attention_stage(tw, "a3", groups, float(1.0 / np.sqrt(D / HEADS).astype(np.float32)),
                            q_hi, q_lo, tw.xt,
                            lambda m, w: vt[:, NTB * (m // HEADS) + w, (m % HEADS) * D:(m % HEADS + 1) * D],
                            lambda g: tw.w("l3_post")[:, g % pairs * P:(g % pairs + 1) * P], None, "add",
                            lambda g, j: h[:, TPG * (g // pairs):TPG * (g // pairs) + TPG, :], project)
        with ExitStack() as f3:
            tw.ct = tw.sb("ct3", [P, T], F32R, ctx=f3)
            tw.sel64 = tw.sb("sel64_3", [P, E3, D], F32R, ctx=f3)
            norm_stage(tw, h, router=Router(tw, E3, parts(LATE, tw.late, "l3_gate"), tw.r("l3_gate_b"), True,
                                            tw.sel64))
            w1 = tw.late["l3_e1"].start
            pair_experts_stage(
                tw, h, E3 // 2,
                lambda q: [tuple(p[:, w1 + e * P:w1 + (e + 1) * P] for p in LATE) for e in (2 * q, 2 * q + 1)],
                lambda q: [tw.w("l3_eb1")[:, e:e + 1] for e in (2 * q, 2 * q + 1)], ACT.Relu,
                (lambda q: [tw.w("l3_e2")[:, e * D:(e + 1) * D] for e in (2 * q, 2 * q + 1)],
                 lambda q: tw.w("l3_eb2")[:, q:q + 1]),
                lambda q: tw.w("l3_e3")[:, q * D:(q + 1) * D], tw.w("l3_eb3"),
                lambda t: rows_over(tw.r("l3_sb3"), TPG),
                shared=dict(w1=parts(LATE, tw.late, "l3_s1"), b1=tw.w("l3_sb1"), w2=tw.w("l3_s2"),
                            b2=tw.w("l3_sb2"), w3=tw.w("l3_s3")))
        store_stage(tw, h, out)


def store_stage(tw, h, out):
    with tw.nc.Block() as block:
        @block.sync
        def _(sp):
            for b in range(B):
                sp.dma_start(out[b].rearrange("(v p k) j -> p v (k j)", v=4, k=2),
                             h[:, NTB * b:NTB * (b + 1), :].rearrange("p (v k) j -> p v (k j)", k=2))\
                    .then_inc(tw.out_landed, 16)
            sp.wait_ge(tw.out_landed, 16 * B)




def twice(a):
    return np.concatenate([a, a], axis=-1)


def pad_to(a, rows, cols):
    out = np.zeros((rows, cols), a.dtype)
    out[:a.shape[0], :a.shape[1]] = a
    return out


def blocks_of(a, b):
    out = np.zeros((a.shape[0] + b.shape[0], a.shape[1] + b.shape[1]), a.dtype)
    out[:a.shape[0], :a.shape[1]] = a
    out[a.shape[0]:, a.shape[1]:] = b
    return out


def side_by_side(a):
    return np.concatenate(list(a), axis=1)


def stacked_pairs(a):
    return np.concatenate([np.concatenate([a[i], a[i + 1]], 0) for i in range(0, len(a), 2)], 1)


def pair_columns(a):
    return np.ascontiguousarray(a.reshape(len(a) // 2, 2 * D).T)


def by_expert(a):
    out = np.zeros((P, a.shape[1]), a.dtype)
    out[:len(a)] = a
    out[D:D + len(a)] = a
    return out


def pack(layout, parts, rows):
    f = np.zeros((rows, layout.n), np.float32)
    for name, a in parts.items():
        c = layout[name]
        assert a.shape == (rows, c.stop - c.start), (name, a.shape)
        f[:, c] = a
    assert set(parts) == set(layout.at)
    return f


def lay_out(i):
    k, t = np.arange(FREQ)[:, None], np.arange(PATCH)[None, :]
    nf = FREQ // 2
    dft = np.where(k < nf, np.cos(2 * np.pi * k * t / PATCH), -np.sin(2 * np.pi * (k - nf) * t / PATCH))
    dft = (dft / np.sqrt(PATCH)).astype(np.float32)
    w = pad_to(i["L0_tok_W"], TAP_SETS * TAP_FEATURES, FREQ * C).reshape(TAP_SETS, TAP_ROWS, C)
    spread = np.zeros((TAP_FEATURES, FREQ, 2, TAP_FEATURES, 2, 4), np.float32)
    for j in range(TAP_FEATURES):
        spread[j, :, :, j] = dft.reshape(FREQ, 2, 2, 4).transpose(0, 2, 1, 3)
    arrays = {"x": i["x"], "wk": np.concatenate([w.transpose(1, 0, 2).reshape(TAP_ROWS, TAP_SETS * C),
                                                 spread.reshape(TAP_ROWS, -1)], 1)}
    arrays["early"] = pack(split_layout_early(), {
        "l0_attn": twice(i["L0_attn_W"]), "l0_gate": i["L0_ffn_gate_w"],
        "l0_w1": side_by_side(i["L0_ffn_w1"]), "l0_w2": side_by_side(i["L0_ffn_w2"])}, D)
    qkv, qkvb = i["L1_attn_qkv_w"], i["L1_attn_qkv_b"]
    mid = {"l1_q": twice(qkv[:, 0:D]), "l1_k": twice(qkv[:, D:2 * D]), "l1_v": qkv[:, 2 * D:3 * D],
           "l1_gate": i["L1_ffn_router_w"].T, "l1_w1": side_by_side(i["L1_ffn_w1"]),
           "l2_router": pad_to(i["L2_ffn_router_w1"], D, P), "l2_e1": side_by_side(i["L2_ffn_expert_w1"])}
    for n in range(LAYERS):
        mid[f"l2_k{n}"] = twice(i["L2_attn_Wk"][n])
        mid[f"l2_qv{n}"] = np.concatenate([i["L2_attn_Wq"][n], i["L2_attn_Wv"][n]], 1)
        mid[f"l2_w1{n}"] = i["L2_attn_W1"][n]
    arrays["mid"] = pack(split_layout_mid(), mid, D)
    arrays["late"] = pack(split_layout_late(), {
        "l3_v": i["L3_attn_WV"], "l3_gate": i["L3_ffn_gW"], "l3_s1": pad_to(i["L3_ffn_sW1"], D, P),
        "l3_e1": side_by_side(i["L3_ffn_eW1"])}, D)
    eye = np.eye(P, dtype=np.float32)
    row, col = np.arange(P)[:, None], np.arange(P)[None, :]
    full = {"ident": eye, "fold": eye[:, :D] + eye[:, D:],
            "expert_rows": (row % D == np.arange(E0)[None, :]).astype(np.float32),
            "iota": np.broadcast_to(np.arange(16, dtype=np.float32), (P, 16)),
            "head_mask": (row // HEADS2 == col // HEADS2).astype(np.float32),
            "l0_w3": side_by_side(i["L0_ffn_w3"]),
            "l1_qb": twice(qkvb[0:D])[:, None], "l1_kb": twice(qkvb[D:2 * D])[:, None],
            "l1_post": blocks_of(i["L1_attn_proj_w"], i["L1_attn_proj_w"]),
            "l1_w2": stacked_pairs(i["L1_ffn_w2"]), "l1_b1": pair_columns(i["L1_ffn_b1"]),
            "l1_b2": by_expert(i["L1_ffn_b2"]),
            "l2_rb1": pad_to(i["L2_ffn_router_b1"][:, None], P, 1), "l2_rw2": pad_to(i["L2_ffn_router_w2"], P, E2),
            "l2_e2": side_by_side([blocks_of(i["L2_ffn_expert_w2"][e], i["L2_ffn_expert_w2"][e + 1])
                                   for e in range(0, E2, 2)]),
            "l2_e3": stacked_pairs(i["L2_ffn_expert_w3"]), "l2_eb1": pair_columns(i["L2_ffn_expert_b1"]),
            "l2_eb2": pair_columns(i["L2_ffn_expert_b2"]), "l2_eb3": by_expert(i["L2_ffn_expert_b3"]),
            "l3_post": side_by_side([blocks_of(i["L3_attn_Wout"][P * k:P * k + D], i["L3_attn_Wout"][P * k + D:P * k + P])
                                     for k in range(HEADS // 2)]),
            "l3_s2": pad_to(i["L3_ffn_sW2"], P, P), "l3_s3": i["L3_ffn_sW3"],
            "l3_sb1": pad_to(i["L3_ffn_sb1"][:, None], P, 1), "l3_sb2": i["L3_ffn_sb2"][:, None],
            "l3_e2": side_by_side(i["L3_ffn_eW2"]), "l3_e3": stacked_pairs(i["L3_ffn_eW3"]),
            "l3_eb1": i["L3_ffn_eb1"].T, "l3_eb2": pair_columns(i["L3_ffn_eb2"]), "l3_eb3": by_expert(i["L3_ffn_eb3"])}
    for n in range(LAYERS):
        full[f"l2_wo{n}"] = np.concatenate([i["L2_attn_Wo"][n]] * 2, 0)
        full[f"l2_w2{n}"] = np.concatenate([i["L2_attn_W2"][n][0:P], i["L2_attn_W2"][n][P:FF]], 1)
        full[f"l2_b1{n}"] = i["L2_attn_b1"][n].reshape(2, P).T
    arrays["full"] = pack(full_layout(), full, P)
    rows = {"l0_gate_b": i["L0_ffn_gate_b"], "l1_vb": qkvb[2 * D:], "l1_scale": i["L1_attn_scale"].reshape(1),
            "l1_proj_b": i["L1_attn_proj_b"], "l2_rb2": i["L2_ffn_router_b2"], "l3_bout": i["L3_attn_bout"],
            "l3_sb3": i["L3_ffn_sb3"], "l3_gate_b": i["L3_ffn_gb"]}
    for n in ("ln1_g", "ln1_b", "ln2_g", "ln2_b"):
        rows["l1_" + n] = i["L1_attn_" + n]
    for k in range(LAYERS):
        for n in ("ln1_g", "ln1_b", "bo", "ln2_g", "ln2_b", "b2"):
            rows[f"l2_{n}{k}"] = i["L2_attn_" + n][k]
    arrays["row"] = pack(row_layout(), {k: v[None, :] for k, v in rows.items()}, 1)[0]
    p, q, c = (np.arange(n) for n in (P, 3, 7 * P))
    distance = 2 * (c[None, None, :] - 3 * P - p[:, None, None]) + q[None, :, None] - 1
    arrays["toeplitz"] = i["L1_attn_bias_table"][np.minimum(distance + N - 1, len(i["L1_attn_bias_table"]) - 1)]

    def head_rows(w):
        t = w.T.reshape(HEADS // 2, P, D).transpose(1, 0, 2)
        return twice(t).reshape(P, HEADS // 2 * P)

    arrays["qk"] = np.concatenate([head_rows(i["L3_attn_WQ"]), head_rows(i["L3_attn_WK"])], 1)
    return {k: np.ascontiguousarray(v) for k, v in arrays.items()}


def kernel(**inputs):
    import concourse.bacc as _bacc
    from concourse.bass_utils import run_bass_kernel_spmd as _run

    arrays = lay_out({k: np.asarray(v) for k, v in inputs.items()})
    nc = _bacc.Bacc("TRN2", target_bir_lowering=False, num_devices=1)
    args = {k: nc.dram_tensor("in_" + k, a.shape, mybir.dt.from_np(a.dtype), kind="ExternalInput").ap()
            for k, a in arrays.items()}
    out = nc.dram_tensor("out_h", (B, N, D), F32, kind="ExternalOutput").ap()
    vit_tower_kernel(nc, out=out, **args)
    r = _run(nc, [{"in_" + k: a for k, a in arrays.items()}], core_ids=[0])
    return r.results[0]["out_h"]
```
